# Optimizing a Trainium2 kernel written in Bass

```python
import numpy as np
import jax
import jax.numpy as jnp

def _softmax(x, axis=-1):
    return jax.nn.softmax(x, axis=axis)

def _gelu(x):
    return jax.nn.gelu(x, approximate=True)

def _silu(x):
    return jax.nn.silu(x)

def _sigmoid(x):
    return jax.nn.sigmoid(x)

def _layernorm(x, axis=-1, eps=1e-05):
    m = jnp.mean(x, axis=axis, keepdims=True)
    v = jnp.var(x, axis=axis, keepdims=True)
    return (x - m) / jnp.sqrt(v + eps)

def _scatter_add(tgt, idx, src, axis=0):
    return tgt.at[idx].add(src)

def _segment_sum(src, seg, n):
    return jax.ops.segment_sum(src, seg, n)
kernel_name = 'mk_flamingo_gated_d1_seqx_r4_4e4fe0'

def setup_inputs(seed: int=0):
    np.random.seed(seed)
    _w = jnp.asarray

    def _rec_inputs():
        import jax
        import jax.numpy as jnp
        _rk = jax.random.key(seed)
        x = 7.22e-05 + 1 * jax.random.normal(jax.random.fold_in(_rk, 1), (2, 1024, 256), jnp.float32)
        _lenS = 1024 - jax.random.randint(jax.random.fold_in(_rk, 7), (2,), 0, max(1, 1024 // 4) + 1, jnp.int32)
        _lenS2 = 64 - jax.random.randint(jax.random.fold_in(_rk, 8), (2,), 0, max(1, 64 // 4) + 1, jnp.int32)
        _ctx_768P = jax.random.normal(jax.random.fold_in(_rk, 11), (2, 16, 192), jnp.float32)
        _ctx_768c = jax.random.dirichlet(jax.random.fold_in(_rk, 511), 0.3 * jnp.ones((16,), jnp.float32), (2, 64))
        _ctx_768t = jnp.einsum('bsk,bkd->bsd', _ctx_768c, _ctx_768P)
        _ctx_768t = _ctx_768t * jax.lax.rsqrt(jnp.mean(jnp.square(_ctx_768t)) + 1e-12) * 0.953939
        ctx_768 = -0.000191848 + 0.999787 * (_ctx_768t + 0.3 * jax.random.normal(jax.random.fold_in(_rk, 611), (2, 64, 192), jnp.float32))
        _g = jax.random.normal(jax.random.fold_in(_rk, 9001), (2, 1), jnp.float32)
        _g = jnp.sign(_g) * jnp.maximum(jnp.abs(_g), 1.0) + (_g == 0) * 1.0
        g_xattn = _g[0]
        g_ffn = _g[1]
        return (x, ctx_768, g_xattn, g_ffn)
    x, ctx_768, g_xattn, g_ffn = _rec_inputs()

    def _L0_xattn_setup():
        import jax, jax.numpy as jnp
        import numpy as np
        DIM = 256
        CTX_DIM = 192
        H = 16
        DH = 64
        INNER = H * DH
        EPS = 1e-05

        def layer_norm(x, gamma, beta):
            mu = jnp.mean(x, axis=-1, keepdims=True)
            var = jnp.mean(jnp.square(x - mu), axis=-1, keepdims=True)
            return (x - mu) * jax.lax.rsqrt(var + EPS) * gamma + beta
        key = jax.random.key(seed)
        ks = jax.random.split(key, 8)
        B, N, M = (4, 512, 512)
        x = jax.random.normal(ks[0], (B, N, DIM), dtype=jnp.float32)
        context = jax.random.normal(ks[1], (B, M, CTX_DIM), dtype=jnp.float32)
        g_x = jnp.ones((DIM,), jnp.float32)
        b_x = jnp.zeros((DIM,), jnp.float32)
        g_c = jnp.ones((CTX_DIM,), jnp.float32)
        b_c = jnp.zeros((CTX_DIM,), jnp.float32)
        Wq = jax.random.normal(ks[2], (DIM, INNER), dtype=jnp.float32) / np.sqrt(DIM)
        Wk = jax.random.normal(ks[3], (CTX_DIM, INNER), dtype=jnp.float32) / np.sqrt(CTX_DIM)
        Wv = jax.random.normal(ks[4], (CTX_DIM, INNER), dtype=jnp.float32) / np.sqrt(CTX_DIM)
        Wo = jax.random.normal(ks[5], (INNER, DIM), dtype=jnp.float32) / np.sqrt(INNER)
        return {'x': x, 'context': context, 'g_x': g_x, 'b_x': b_x, 'g_c': g_c, 'b_c': b_c, 'Wq': Wq, 'Wk': Wk, 'Wv': Wv, 'Wo': Wo}
    _L0_xattn_all = _L0_xattn_setup()
    _L0_xattn_in = {k: v for k, v in _L0_xattn_all.items() if k in ('g_x', 'b_x', 'g_c', 'b_c', 'Wq', 'Wk', 'Wv', 'Wo')}
    del _L0_xattn_all

    def _L0_ffn_setup():
        import jax, jax.numpy as jnp
        import numpy as np
        TOP_K = 2

        def gelu(x):
            return jax.nn.gelu(x, approximate=False)
        key = jax.random.key(seed)
        ks = jax.random.split(key, 6)
        B, L, D, H, E, S = (4, 512, 256, 512, 8, 2)
        sd = 0.02
        return {'x': jax.random.normal(ks[0], (B, L, D), dtype=jnp.float32), 'router_w': jax.random.normal(ks[1], (D, E), dtype=jnp.float32) * sd, 'router_b': jnp.zeros((E,), dtype=jnp.float32), 'w1': jax.random.normal(ks[2], (E, D, H), dtype=jnp.float32) * sd, 'b1': jnp.zeros((E, H), dtype=jnp.float32), 'w2': jax.random.normal(ks[3], (E, H, D), dtype=jnp.float32) * sd, 'b2': jnp.zeros((E, D), dtype=jnp.float32), 'sw1': jax.random.normal(ks[4], (S, D, H), dtype=jnp.float32) * sd, 'sb1': jnp.zeros((S, H), dtype=jnp.float32), 'sw2': jax.random.normal(ks[5], (S, H, D), dtype=jnp.float32) * sd, 'sb2': jnp.zeros((S, D), dtype=jnp.float32)}
    _L0_ffn_all = _L0_ffn_setup()
    _L0_ffn_in = {k: v for k, v in _L0_ffn_all.items() if k in ('router_w', 'router_b', 'w1', 'b1', 'w2', 'b2', 'sw1', 'sb1', 'sw2', 'sb2')}
    del _L0_ffn_all
    return {'x': x, 'ctx_768': ctx_768, 'g_xattn': g_xattn, 'g_ffn': g_ffn, 'L0_xattn_g_x': _L0_xattn_in['g_x'], 'L0_xattn_b_x': _L0_xattn_in['b_x'], 'L0_xattn_g_c': _L0_xattn_in['g_c'], 'L0_xattn_b_c': _L0_xattn_in['b_c'], 'L0_xattn_Wq': _L0_xattn_in['Wq'], 'L0_xattn_Wk': _L0_xattn_in['Wk'], 'L0_xattn_Wv': _L0_xattn_in['Wv'], 'L0_xattn_Wo': _L0_xattn_in['Wo'], 'L0_ffn_router_w': _L0_ffn_in['router_w'], 'L0_ffn_router_b': _L0_ffn_in['router_b'], 'L0_ffn_w1': _L0_ffn_in['w1'], 'L0_ffn_b1': _L0_ffn_in['b1'], 'L0_ffn_w2': _L0_ffn_in['w2'], 'L0_ffn_b2': _L0_ffn_in['b2'], 'L0_ffn_sw1': _L0_ffn_in['sw1'], 'L0_ffn_sb1': _L0_ffn_in['sb1'], 'L0_ffn_sw2': _L0_ffn_in['sw2'], 'L0_ffn_sb2': _L0_ffn_in['sb2']}

def reference(x, ctx_768, g_xattn, g_ffn, L0_xattn_g_x, L0_xattn_b_x, L0_xattn_g_c, L0_xattn_b_c, L0_xattn_Wq, L0_xattn_Wk, L0_xattn_Wv, L0_xattn_Wo, L0_ffn_router_w, L0_ffn_router_b, L0_ffn_w1, L0_ffn_b1, L0_ffn_w2, L0_ffn_b2, L0_ffn_sw1, L0_ffn_sb1, L0_ffn_sw2, L0_ffn_sb2):
    import jax
    import jax.numpy as jnp

    def _L0_xattn_ref(x, context, g_x, b_x, g_c, b_c, Wq, Wk, Wv, Wo):
        import jax, jax.numpy as jnp
        import numpy as np
        DIM = 256
        CTX_DIM = 192
        H = 16
        DH = 64
        INNER = H * DH
        EPS = 1e-05

        def layer_norm(x, gamma, beta):
            mu = jnp.mean(x, axis=-1, keepdims=True)
            var = jnp.mean(jnp.square(x - mu), axis=-1, keepdims=True)
            return (x - mu) * jax.lax.rsqrt(var + EPS) * gamma + beta
        B, N, _ = x.shape
        M = context.shape[1]
        xn = layer_norm(x, g_x, b_x)
        cn = layer_norm(context, g_c, b_c)
        q = (xn @ Wq).reshape(B, N, H, DH).transpose(0, 2, 1, 3)
        k = (cn @ Wk).reshape(B, M, H, DH).transpose(0, 2, 1, 3)
        v = (cn @ Wv).reshape(B, M, H, DH).transpose(0, 2, 1, 3)
        scale = jnp.float32(1.0 / np.sqrt(DH))
        sim = jnp.einsum('bhid,bhjd->bhij', q, k) * scale
        attn = jax.nn.softmax(sim, axis=-1)
        out = jnp.einsum('bhij,bhjd->bhid', attn, v)
        out = out.transpose(0, 2, 1, 3).reshape(B, N, INNER)
        return out @ Wo

    def _L0_ffn_ref(x, router_w, router_b, w1, b1, w2, b2, sw1, sb1, sw2, sb2):
        import jax, jax.numpy as jnp
        import numpy as np
        TOP_K = 2

        def gelu(x):
            return jax.nn.gelu(x, approximate=False)
        B, L, D = x.shape
        E = router_b.shape[0]
        S = sw1.shape[0]
        xf = x.reshape(-1, D)
        sh = gelu(jnp.einsum('nd,sdh->snh', xf, sw1) + sb1[:, None, :])
        shared_out = (jnp.einsum('snh,shd->nd', sh, sw2) + sb2.sum(0)) / S
        gates = xf @ router_w + router_b
        topv, topi = jax.lax.top_k(gates, TOP_K)
        probs = jax.nn.softmax(topv, axis=-1)
        comb = jnp.einsum('nke,nk->ne', jax.nn.one_hot(topi, E, dtype=xf.dtype), probs)
        h = gelu(jnp.einsum('nd,edh->enh', xf, w1) + b1[:, None, :])
        y = jnp.einsum('enh,ehd->end', h, w2) + b2[:, None, :]
        moe_out = jnp.einsum('ne,end->nd', comb, y)
        return (shared_out + moe_out).reshape(B, L, D)
    x = x + jnp.tanh(g_xattn[0]) * _L0_xattn_ref(_layernorm(x, axis=-1), ctx_768, L0_xattn_g_x, L0_xattn_b_x, L0_xattn_g_c, L0_xattn_b_c, L0_xattn_Wq, L0_xattn_Wk, L0_xattn_Wv, L0_xattn_Wo)
    x = x + jnp.tanh(g_ffn[0]) * _L0_ffn_ref(_layernorm(x, axis=-1), L0_ffn_router_w, L0_ffn_router_b, L0_ffn_w1, L0_ffn_b1, L0_ffn_w2, L0_ffn_b2, L0_ffn_sw1, L0_ffn_sb1, L0_ffn_sw2, L0_ffn_sb2)
    return x

_drawn_inputs = setup_inputs


def setup_inputs(seed=0):
    import zlib

    import numpy as np

    out = dict(_drawn_inputs(seed))
    spreads = {'L0_xattn_g_x': (1.0, 0.2),
     'L0_xattn_b_x': (0.0, 0.496),
     'L0_xattn_g_c': (1.0, 0.2),
     'L0_xattn_b_c': (0.0, 0.1),
     'L0_ffn_router_b': (0.0, 0.1),
     'L0_ffn_b1': (0.0, 0.529),
     'L0_ffn_b2': (0.0, 0.1),
     'L0_ffn_sb1': (0.0, 0.498),
     'L0_ffn_sb2': (0.0, 0.1)}
    factors = {}
    for name, (base, spread) in spreads.items():
        noise = np.random.default_rng([zlib.crc32(name.encode()), seed]).standard_normal(out[name].shape)
        drawn = base * np.exp(spread * noise) if base else spread * noise
        out[name] = jnp.asarray(drawn.astype(out[name].dtype))
    for name, factor in factors.items():
        out[name] = (out[name] * factor).astype(out[name].dtype)
    return out
```

```python
import numpy as np
import concourse.bass as bass
from concourse import mybir
from contextlib import ExitStack

F32 = mybir.dt.float32
I32 = mybir.dt.int32
U32 = mybir.dt.uint32
ALU = mybir.AluOpType
ACT = mybir.ActivationFunctionType
AX = mybir.AxisListType

P = 128
BATCH, SEQ, D = 2, 1024, 256
TOK = BATCH * SEQ
NT = TOK // P
TPB = SEQ // P
KD = D // P
H, DH, CTX, CDIM = 16, 64, 64, 192
NPAIR = H // 2
HJ = H * CTX
KC, CK = 2, CDIM // 2
E, S, HID = 8, 2, 512
HC = HID // P
SHC = S * HC
TOPK = 2
SLOT_TILES = TOK * TOPK // P + E - 1
SLOTS = SLOT_TILES * P
CHUNK = 512
TPC = CHUNK // P
NCHUNK = TOK // CHUNK
BANK = 512
INNER = H * DH
EPS = 1e-5
SCALE = 1.0 / np.sqrt(DH)
BIAS_ROWS = E + S
LEAD = 4
GBUF = 4


def build(nc, x, ctx, g_xattn, g_ffn, g_x, b_x, g_c, b_c, Wq, Wk, Wv, Wo,
          router_w, router_b, w1, b1, w2, b2, sw1, sb1, sw2, sb2, out):
    st = ExitStack()
    with st:
        def sb(name, shape, dt=F32):
            return st.enter_context(nc.sbuf_tensor(name, shape, dt))

        def sem(name):
            return st.enter_context(nc.semaphore(name))

        psum = st.enter_context(nc.psum_tensor("psum", [P, 8 * BANK], F32))
        bank = [psum[:, i * BANK:(i + 1) * BANK] for i in range(8)]

        x_slot = nc.dram_tensor("x_slot", [SLOTS, D], F32, kind="Internal").ap()
        y_slot = nc.dram_tensor("y_slot", [SLOTS, D], F32, kind="Internal").ap()

        xs_all = sb("xs_all", [P, NT, D])
        y_all = sb("y_all", [P, NT, D])
        yT = sb("yT", [P, KD, TOK])
        sw1_sb = sb("sw1_sb", [P, S, KD, HID])
        sw2_sb = sb("sw2_sb", [P, SHC, D])
        w1_sb = sb("w1_sb", [P, E, KD, HID])
        AVW = sb("AVW", [P, E * HC * D])
        A = AVW[:, 0:BATCH * KD * HJ].rearrange("p (b k n) -> p b k n", b=BATCH, k=KD)
        VW = AVW[:, BATCH * KD * HJ:].rearrange("p (b c n) -> p b c n", b=BATCH, c=NPAIR)
        w2_sb = AVW[:, :].rearrange("p (e m n) -> p e m n", e=E, m=HC)
        b1_bc = sb("b1_bc", [P, E * HID])
        ident = sb("ident", [P, P])
        ones = sb("ones", [P, P])
        before = sb("before", [P, P])
        NVEC = SHC + 2 * KD + 2 * KC
        vec_rows, vec_col = sb("vec_rows", [NVEC, P]), sb("vec_col", [P, NVEC])
        sb1_col = vec_col[:, 0:SHC]
        gx_col, bx_col = (vec_col[:, SHC + i * KD:SHC + (i + 1) * KD] for i in range(2))
        gc_col, bc_col = (vec_col[0:CK, SHC + 2 * KD + i * KC:SHC + 2 * KD + (i + 1) * KC] for i in range(2))
        rw_sb = sb("rw_sb", [P, KD, E])
        rb_bc = sb("rb_bc", [P, E])
        b2_rows = sb("b2_rows", [P, D])
        gate = sb("gate", [P, 2])
        tg = sb("tg", [P, 2])
        half_tg = sb("half_tg", [P, 1])
        minus_half = sb("minus_half", [P, NT])
        eps_col = sb("eps_col", [P, 1])
        zero_row = sb("zero_row", [P, D])

        st1 = sb("st1", [P, NT, 6])
        mv1 = sb("mv1", [P, NT, 2])
        ve1 = sb("ve1", [P, NT])
        ra, rq, rb, r1 = (sb(n, [P, NT]) for n in ("ra", "rq", "rb", "r1"))
        stc, mvc, vec, rc = sb("stc", [P, 6]), sb("mvc", [P, 2]), sb("vec", [P, 1]), sb("rc", [P, 1])
        st2, mv2, ve2, r2 = sb("st2", [P, 2, 6]), sb("mv2", [P, 2, 2]), sb("ve2", [P, 2]), sb("r2", [P, 2])

        ARENA = 10240
        arena = sb("arena", [P, ARENA])

        def carve(sizes):
            at, got = 0, []
            for n in sizes:
                got.append(arena[:, at:at + n])
                at += n
            assert at <= ARENA, at
            return got

        ctx_sb, cn, cnT_, kbd_, vbd_, wqT_ = carve([CDIM, CDIM, KC * P, NPAIR * BATCH * P, NPAIR * BATCH * P,
                                                    NPAIR * KD * P])
        cnT = cnT_.rearrange("p (k n) -> p k n", k=KC)
        kbd = kbd_.rearrange("p (c b n) -> p c b n", c=NPAIR, b=BATCH)
        vbd = vbd_.rearrange("p (c b n) -> p c b n", c=NPAIR, b=BATCH)
        wqT = wqT_.rearrange("p (c k n) -> p c k n", c=NPAIR, k=KD)
        y_flat = y_all[:, :, :].rearrange("p t d -> p (t d)")
        yT_flat = yT[:, :, :].rearrange("p k t -> p (k t)")
        wk_sb = y_flat[:, 0:KC * INNER].rearrange("p (k n) -> p k n", k=KC)
        wv_sb = y_flat[:, KC * INNER:2 * KC * INNER].rearrange("p (k n) -> p k n", k=KC)
        wq_sb = yT_flat[:, 0:KD * INNER].rearrange("p (k n) -> p k n", k=KD)
        wo_sb = yT_flat[:, KD * INNER:].rearrange("p (c n) -> p c n", c=NPAIR)
        Eb0, Eb1, PT_, zbuf_, xnT_, ybuf_, yTb_ = carve([HJ, HJ, HJ, 2 * D, 2 * D, 2 * D, 2 * D])
        zbuf, ybuf = (v.rearrange("p (a d) -> p a d", a=2) for v in (zbuf_, ybuf_))
        xnT, yTb = (v.rearrange("p (a k n) -> p a k n", a=2, k=KD) for v in (xnT_, yTb_))
        Eb = [e.rearrange("p (h j) -> p h j", h=H) for e in (Eb0, Eb1)]
        PT = PT_.rearrange("p (c n) -> p c n", c=NPAIR)
        mx, sm, rinv = sb("mx", [P, 2, H]), sb("sm", [P, 2, H]), sb("rinv", [P, 2, H])
        lg = sb("lg", [P, 2, E])
        v8, i8 = sb("v8", [P, 2, 8]), sb("i8", [P, 2, 8], U32)
        hT_, ct_cur, xsl_, xsT_, hs_, hTr_, ysl_, gb_ = carve(
            [SHC * CHUNK, CHUNK, 2 * D, 2 * D, 2 * HID, 2 * HID, 2 * D, GBUF * TOPK * D])
        hT = hT_.rearrange("p (m t) -> p m t", m=SHC)
        xsl = xsl_.rearrange("p (a d) -> p a d", a=2)
        xsT = xsT_.rearrange("p (a k n) -> p a k n", a=2, k=KD)
        hs = hs_.rearrange("p (a n) -> p a n", a=2)
        hTr = hTr_.rearrange("p (a m n) -> p a m n", a=2, m=HC)
        ysl = ysl_.rearrange("p (a d) -> p a d", a=2)
        gb = gb_.rearrange("p (a k d) -> p a k d", a=GBUF, k=TOPK)

        val = sb("val", [P, NT, TOPK])
        idx = sb("idx", [P, NT, TOPK])
        iota_e, iota_e_i = sb("iota_e", [P, E]), sb("iota_e_i", [P, E], I32)
        iota_tile, iota_tile_i = sb("iota_tile", [P, NT]), sb("iota_tile_i", [P, NT], I32)
        iota_slot, iota_slot_i = sb("iota_slot", [P, SLOT_TILES]), sb("iota_slot_i", [P, SLOT_TILES], I32)
        oh = sb("oh", [P, TOPK, NT, E])
        chosen = sb("chosen", [P, NT, E])
        PADT, PADE = NT // 2, E // 2
        run_t = [sb(f"run_t{i}", [P, PADT + NT, E]) for i in range(2)]
        run_e = [sb(f"run_e{i}", [P, PADE + E]) for i in range(2)]
        full_tile = sb("full_tile", [P, E, NT])
        tiles_e, start_e = sb("tiles_e", [P, E]), sb("start_e", [P, E])
        tot = sb("tot", [P, NT, E])
        place = sb("place", [P, NT, E])
        picked = sb("picked", [P, TOPK, NT, E])
        pos_f = sb("pos_f", [P, TOPK, NT])
        pos = sb("pos", [P, TOPK, NT], I32)
        passed = sb("passed", [P, SLOT_TILES, E - 1])
        emap_f, emap = sb("emap_f", [P, SLOT_TILES]), sb("emap", [P, SLOT_TILES], I32)
        dif, ex, den = sb("dif", [P, NT]), sb("ex", [P, NT]), sb("den", [P, NT])
        prob = sb("prob", [P, TOPK, NT])
        wgt = sb("wgt", [P, TOPK, NT])
        ohp = picked
        comb = sb("comb", [P, NT, BIAS_ROWS])
        combT = sb("combT", [P, TOK])

        ld_ctx, ld_k, ld_v, ld_q, ld_o, ld_small, ld_gate = (
            sem(n) for n in ("ld_ctx", "ld_k", "ld_v", "ld_q", "ld_o", "ld_small", "ld_gate"))
        NX = 4
        ld_x = [sem(f"ld_x{i}") for i in range(NX)]
        ld_sw, ld_w1, ld_w2, ld_b1, ld_b2 = (sem(n) for n in ("ld_sw", "ld_w1", "ld_w2", "ld_b1", "ld_b2"))
        consts, consts_a, zeros_ready, zero_filled = (
            sem(n) for n in ("consts", "consts_a", "zeros_ready", "zero_filled"))
        cst_ready, cmv_ready, cve_ready, crc_ready, cn_ready, cnt_psum, cnt_ready = (
            sem(n) for n in ("cst_ready", "cmv_ready", "cve_ready", "crc_ready", "cn_ready", "cnt_psum", "cnt_ready"))
        bd_zeroed, vec_psum, vec_ready, kv_psum, kv_ready, wqt_psum, wqt_ready, fold_psum, fold_ready = (
            sem(n) for n in ("bd_zeroed", "vec_psum", "vec_ready", "kv_psum", "kv_ready", "wqt_psum", "wqt_ready", "fold_psum", "fold_ready"))
        st1_ready, mv1_ready, r1_step, r1_ready, tg_ready, htg_ready = (
            sem(n) for n in ("st1_ready", "mv1_ready", "r1_step", "r1_ready", "tg_ready", "htg_ready"))
        z_ready, zt_psum, xn_ready, s_psum, max_ready, sub_ready, exp_ready, sum_ready, rcp_ready, p_ready = (
            sem(n) for n in ("z_ready", "zt_psum", "xn_ready", "s_psum", "max_ready", "sub_ready", "exp_ready",
                             "sum_ready", "rcp_ready", "p_ready"))
        pt_psum, pt_ready, o_psum, x1_ready, st2_ready, mv2_ready, ve2_ready, r2_ready, y_ready, y_kept = (
            sem(n) for n in ("pt_psum", "pt_ready", "o_psum", "x1_ready", "st2_ready", "mv2_ready", "ve2_ready",
                             "r2_ready", "y_ready", "y_kept"))
        yt_psum, yt_ready, l_psum, l_ready, val_ready, idx_ready, top_kept = (
            sem(n) for n in ("yt_psum", "yt_ready", "l_psum", "l_ready", "val_ready", "idx_ready", "top_kept"))
        route, chosen_ready, count_psum, dif_ready, ex_ready, pos_ready, comb_ready, ct_psum, ct_ready = (
            sem(n) for n in ("route", "chosen_ready", "count_psum", "dif_ready", "ex_ready", "pos_ready", "comb_ready",
                             "ct_psum", "ct_ready"))
        cur_ready, sh_psum, sh_ready, acc_psum, acc_free = (
            sem(n) for n in ("cur_ready", "sh_psum", "sh_ready", "acc_psum", "acc_free"))
        scattered = sem("scattered")
        xsl_loaded = [sem(f"xsl_loaded{i}") for i in range(2)]
        xt_psum, xt_ready, h_psum, h_ready, ht_psum, ht_ready, ye_psum, ye_ready = (
            sem(n) for n in ("xt_psum", "xt_ready", "h_psum", "h_ready", "ht_psum", "ht_ready", "ye_psum", "ye_ready"))
        y_stored = [sem(f"y_stored{i}") for i in range(2)]
        gathered = [sem(f"gathered{i}") for i in range(GBUF)]
        first_added, out_ready, out_stored = (sem(n) for n in ("first_added", "out_ready", "out_stored"))

        x_rows = x.rearrange("b (t p) d -> p (b t) d", p=P)
        out_rows = out.rearrange("b (t p) d -> p (b t) d", p=P)
        x_slot_tiles = x_slot.rearrange("(s p) d -> s p d", p=P)
        y_slot_tiles = y_slot.rearrange("(s p) d -> s p d", p=P)

        block = st.enter_context(nc.Block())

        def at(t):
            return bass.ds(t, 1)

        STEPS = range(-LEAD, NT + 2)
        LOOP0, LOOP1 = LEAD, NT - LEAD

        def attention(eng, step):
            for i in range(STEPS.start, LOOP0):
                step(i, i % 2, lambda t: 0 <= t < NT, i)
            with eng.Fori(0, (LOOP1 - LOOP0) // 2) as j:
                for par in range(2):
                    step(LOOP0 + par + j * 2, par, lambda t: True, None)
            for i in range(LOOP1, STEPS.stop):
                step(i, i % 2, lambda t: 0 <= t < NT, i)

        def routed(eng, step):
            step(0, 0, True, False)
            with eng.Fori(0, (SLOT_TILES - 3) // 2) as j:
                for u in range(2):
                    step(j * 2 + (u + 1), (u + 1) % 2, False, False)
            for s in (SLOT_TILES - 2, SLOT_TILES - 1):
                step(s, s % 2, False, s == SLOT_TILES - 1)

        @block.sync
        def _(sp):
            sp.dma_start(ctx_sb, ctx.rearrange("b j c -> (b j) c")).then_inc(ld_ctx, 16)
            sp.dma_start(wk_sb[0:CK], Wk.rearrange("(k p) n -> p k n", p=CK)).then_inc(ld_k, 16)
            sp.dma_start(wv_sb[0:CK], Wv.rearrange("(k p) n -> p k n", p=CK)).then_inc(ld_v, 16)
            sp.dma_start(wq_sb, Wq.rearrange("(k p) n -> p k n", p=P)).then_inc(ld_q, 16)
            for i in range(NX):
                n = NT // NX
                sp.dma_start(xs_all[:, i * n:(i + 1) * n, :], x_rows[:, i * n:(i + 1) * n, :]).then_inc(ld_x[i], 16)
            sp.dma_start(wo_sb, Wo.rearrange("(c p) n -> p c n", p=P)).then_inc(ld_o, 16)
            sp.dma_start(sw1_sb[:, :, :, :], sw1.rearrange("s (k p) n -> p s k n", p=P)).then_inc(ld_sw, 16)
            sp.dma_start(sw2_sb[:, :, :], sw2.rearrange("s (m p) n -> p (s m) n", p=P)).then_inc(ld_sw, 16)
            sp.dma_start(w1_sb[:, :, :, :], w1.rearrange("e (k p) n -> p e k n", p=P)).then_inc(ld_w1, 16)
            sp.dma_start(b1_bc[:, :], b1.rearrange("e n -> (e n)").partition_broadcast(P)).then_inc(ld_b1, 16)
            sp.wait_ge(zeros_ready, 1)
            sp.dma_start(x_slot_tiles.rearrange("s p d -> p s d"),
                         zero_row[:, :].unsqueeze(1).broadcast_to([P, SLOT_TILES, D])).then_inc(zero_filled, 16)
            sp.wait_ge(o_psum, NT)
            sp.dma_start(w2_sb, w2.rearrange("e (m p) n -> p e m n", p=P)).then_inc(ld_w2, 16)

            sp.wait_ge(scattered, 16 * TOPK * NT)
            for s in range(2):
                sp.dma_start(xsl[:, s, :], x_slot_tiles[s]).then_inc(xsl_loaded[s], 16)

            def step(s, par, first, last, load):
                if load:
                    sp.wait_ge(xt_psum, s + 1)
                    sp.dma_start(xsl[:, par, :], x_slot_tiles[at(s + 2)].rearrange("a p d -> p (a d)")
                                 ).then_inc(xsl_loaded[par], 16)
                sp.wait_ge(ye_ready, s + 1)
                sp.dma_start(y_slot_tiles[at(s)].rearrange("a p d -> p (a d)"), ysl[:, par, :]
                             ).then_inc(y_stored[par], 16)

            routed(sp, lambda s, par, first, last: step(s, par, first, last, not isinstance(s, int) or s + 2 < SLOT_TILES))

            with sp.Fori(0, NT) as t:
                sp.wait_ge(out_ready, t + 1)
                sp.dma_start(out_rows[:, at(t), :], xs_all[:, at(t), :]).then_inc(out_stored, 16)
            sp.wait_ge(out_stored, 16 * NT)

        @block.gpsimd
        def _(pool):
            nc.gpsimd.memset(zero_row[:, :], 0.0).then_inc(zeros_ready, 1)
            nc.gpsimd.memset(minus_half[:, :], -0.5).then_inc(consts_a, 1)
            nc.gpsimd.memset(eps_col[:, :], EPS).then_inc(consts_a, 1)
            nc.gpsimd.memset(ones[:, :], 1.0).then_inc(consts_a, 1)
            pool.wait_ge(consts_a, 3)
            nc.gpsimd.affine_select(out=ident[:, :], in_=ones[:, :], compare_op=ALU.is_equal, fill=0.0, base=0,
                                    pattern=[[-1, P]], channel_multiplier=1).then_inc(consts, 1)
            nc.gpsimd.affine_select(out=before[:, :], in_=ones[:, :], compare_op=ALU.is_gt, fill=0.0, base=0,
                                    pattern=[[1, P]], channel_multiplier=-1).then_inc(consts, 1)
            pool.wait_ge(cmv_ready, 1)
            nc.gpsimd.tensor_scalar(vec[:, :], mvc[:, 1:2], EPS, None, ALU.add).then_inc(cve_ready, 1)
            pool.wait_ge(cve_ready, 1)
            nc.gpsimd.tensor_tensor(rc[:, :], vec[:, :], minus_half[:, 0:1], ALU.pow).then_inc(crc_ready, 1)
            pool.wait_ge(mv1_ready, NT)
            nc.gpsimd.tensor_scalar(ve1[:, :], mv1[:, :, 1], EPS, None, ALU.add).then_inc(r1_step, 1)
            pool.wait_ge(r1_step, 1)
            nc.gpsimd.tensor_tensor(ra[:, :], ve1[:, :], minus_half[:, :], ALU.pow).then_inc(r1_step, 1)
            pool.wait_ge(r1_step, 2)
            nc.gpsimd.tensor_tensor(rq[:, :], ra[:, :], ra[:, :], ALU.mult).then_inc(r1_step, 1)
            pool.wait_ge(r1_step, 3)
            nc.gpsimd.tensor_tensor(rq[:, :], rq[:, :], mv1[:, :, 1], ALU.mult).then_inc(r1_step, 1)
            pool.wait_ge(r1_step, 4)
            nc.gpsimd.tensor_scalar(rq[:, :], rq[:, :], EPS, None, ALU.add).then_inc(r1_step, 1)
            pool.wait_ge(r1_step, 5)
            nc.gpsimd.tensor_tensor(rb[:, :], rq[:, :], minus_half[:, :], ALU.pow).then_inc(r1_step, 1)
            pool.wait_ge(r1_step, 6)
            nc.gpsimd.tensor_tensor(r1[:, :], ra[:, :], rb[:, :], ALU.mult).then_inc(r1_ready, 1)
            nc.gpsimd.iota(iota_e_i[:, :], [[1, E]], base=0, channel_multiplier=0).then_inc(consts, 1)
            nc.gpsimd.iota(iota_tile_i[:, :], [[P, NT]], base=0, channel_multiplier=0).then_inc(consts, 1)
            nc.gpsimd.iota(iota_slot_i[:, :], [[1, SLOT_TILES]], base=0, channel_multiplier=0).then_inc(consts, 1)

            def step(i, par, has, fixed):
                if has(i - 1):
                    q = 1 - par
                    pool.wait_ge(mv2_ready, i)
                    nc.gpsimd.tensor_tensor(ve2[:, q:q + 1], mv2[:, q, 1:2], eps_col[:, :], ALU.add).then_inc(ve2_ready, 1)
                    pool.wait_ge(ve2_ready, i)
                    nc.gpsimd.tensor_tensor(r2[:, q:q + 1], ve2[:, q:q + 1], minus_half[:, 0:1], ALU.pow
                                            ).then_inc(r2_ready, 1)
                if has(i + 1):
                    q = 1 - par
                    pool.wait_ge(rcp_ready, i + 2)
                    nc.gpsimd.tensor_tensor(Eb[q], Eb[q], rinv[:, q, :].unsqueeze(2).broadcast_to([P, H, CTX]), ALU.mult
                                            ).then_inc(p_ready, 1)

            attention(pool, step)

            pool.wait_ge(pos_ready, 1)
            pool.wait_ge(y_kept, NT)
            pool.wait_ge(zero_filled, 16)
            for k in range(TOPK):
                for t in range(NT):
                    nc.gpsimd.indirect_dma_start(x_slot, bass.IndirectOffsetOnAxis(ap=pos[:, k, t:t + 1], axis=0),
                                                 y_all[:, t, :], None).then_inc(scattered, 16)
            pool.wait_ge(y_stored[0], 16 * ((SLOT_TILES + 1) // 2))
            pool.wait_ge(y_stored[1], 16 * (SLOT_TILES // 2))
            for t in range(NT):
                if t >= GBUF:
                    pool.wait_ge(out_ready, t - GBUF + 1)
                for k in range(TOPK):
                    nc.gpsimd.indirect_dma_start(gb[:, t % GBUF, k, :], None, y_slot,
                                                 bass.IndirectOffsetOnAxis(ap=pos[:, k, t:t + 1], axis=0)
                                                 ).then_inc(gathered[t % GBUF], 16)

        @block.scalar
        def _(act):
            act.wait_ge(bd_zeroed, 1)
            act.dma_start(vec_rows[0:SHC, :], sb1.rearrange("s (m p) -> (s m) p", p=P)).then_inc(ld_small, 16)
            at_row = SHC
            for v, n, w in ((g_x, KD, P), (b_x, KD, P), (g_c, KC, CK), (b_c, KC, CK)):
                act.dma_start(vec_rows[at_row:at_row + n, 0:w], v.rearrange("(k p) -> k p", p=w)).then_inc(ld_small, 16)
                at_row += n
            act.dma_start(gate[:, 0:1], g_xattn.partition_broadcast(P)).then_inc(ld_gate, 16)
            act.dma_start(gate[:, 1:2], g_ffn.partition_broadcast(P)).then_inc(ld_gate, 16)
            act.dma_start(rw_sb[:, :, :], router_w.rearrange("(k p) e -> p k e", p=P)).then_inc(ld_b2, 16)
            act.dma_start(rb_bc[:, :], router_b.partition_broadcast(P)).then_inc(ld_b2, 16)
            act.wait_ge(bd_zeroed, 2)
            act.dma_start(b2_rows[0:E, :], b2).then_inc(ld_b2, 16)
            act.dma_start(b2_rows[E:BIAS_ROWS, :], sb2).then_inc(ld_b2, 16)
            act.wait_ge(ld_gate, 32)
            nc.scalar.activation(tg[:, :], gate[:, :], ACT.Tanh).then_inc(tg_ready, 1)
            act.wait_ge(vec_psum, 1)
            act.wait_ge(cnt_psum, 1)
            nc.scalar.activation(vec_col[:, :], bank[0][:, 2 * P:2 * P + NVEC], ACT.Copy).then_inc(vec_ready, 1)
            act.wait_ge(vec_ready, 1)
            act.wait_ge(cnt_psum, 1)
            for k in range(KC):
                nc.scalar.activation(cnT[0:CK, k, :], bank[0][0:CK, k * P:(k + 1) * P], ACT.Identity,
                                     bias=bc_col[:, k:k + 1], scale=gc_col[:, k:k + 1]).then_inc(cnt_ready, 1)
            act.wait_ge(bd_zeroed, 4)
            n = 0
            for dst, scale in ((kbd, SCALE), (vbd, 1.0)):
                for g in range(2):
                    act.wait_ge(kv_psum, n + 1)
                    src = bank[1 + n][:, :].rearrange("p (c b j) -> p c b j", c=NPAIR // 2, b=BATCH)
                    for a in range(2):
                        rows = slice(a * DH, (a + 1) * DH)
                        nc.scalar.activation(dst[rows, g * 4:(g + 1) * 4, :, a * CTX:(a + 1) * CTX], src[rows],
                                             ACT.Copy, scale=float(scale)).then_inc(kv_ready, 1)
                    n += 1
            for n in range(16):
                act.wait_ge(fold_psum, n + 1)
                src = bank[n % 4 + 1][:, :]
                if n < 8:
                    k, c = n // 4, (n % 4) * 2
                    dst = A[:, :, k, c * P:(c + 2) * P].rearrange("p b (c n) -> p c b n", c=2)
                    src = src.rearrange("p (c b n) -> p c b n", c=2, b=BATCH)
                else:
                    b, c = (n - 8) // 4, ((n - 8) % 4) * 2
                    dst, src = VW[:, b, c:c + 2, :], src.rearrange("p (c n) -> p c n", c=2)
                nc.scalar.activation(dst, src, ACT.Copy).then_inc(fold_ready, 1)

            def step(i, par, has, fixed):
                q = 1 - par
                if has(i):
                    act.wait_ge(pt_psum, i + 1)
                    for g in range(2):
                        last = nc.scalar.activation(PT[:, g * 4:(g + 1) * 4, :],
                                                    bank[6 + g][:, :].rearrange("p (c n) -> p c n", c=4), ACT.Copy)
                    last.then_inc(pt_ready, 1)
                if has(i - 1):
                    act.wait_ge(yt_psum, i)
                    if fixed is None or i >= 3:
                        act.wait_ge(l_psum, i - 2)
                    src = bank[7][:, 0:D].rearrange("p (k n) -> p k n", k=KD)
                    nc.scalar.activation(yTb[:, q, :, :], src, ACT.Copy)
                    nc.scalar.activation(yT[:, :, bass.ds((i - 1) * P, P)], src, ACT.Copy).then_inc(yt_ready, 1)
                if has(i + 3):
                    act.wait_ge(zt_psum, i + 4)
                    if fixed is None or i >= -1:
                        act.wait_ge(s_psum, i + 2)
                    for k in range(KD):
                        last = nc.scalar.activation(xnT[:, q, k, :], bank[0][:, k * P:(k + 1) * P], ACT.Identity,
                                                    bias=bx_col[:, k:k + 1], scale=gx_col[:, k:k + 1])
                    last.then_inc(xn_ready, 1)
                if has(i + 2):
                    act.wait_ge(sub_ready, i + 3)
                    nc.scalar.activation(Eb[par], Eb[par], ACT.Exp).then_inc(exp_ready, 1)

            attention(act, step)

            act.wait_ge(dif_ready, 1)
            nc.scalar.activation(ex[:, :], dif[:, :], ACT.Exp).then_inc(ex_ready, 1)
            act.wait_ge(ld_b2, 64)

            def shared(c):
                for m in range(SHC):
                    act.wait_ge(sh_psum, c * SHC + (m + 1))
                    nc.scalar.activation(hT[:, m, :], bank[2 + m % 4][:, :], ACT.Gelu, bias=sb1_col[:, m:m + 1]
                                         ).then_inc(sh_ready, 1)

            with act.Fori(0, NCHUNK // 2) as c:
                shared(c)

            def step(s, par, first, last):
                q = 1 - par
                if not first:
                    act.wait_ge(ye_psum, s)
                    if not isinstance(s, int) or s >= 3:
                        act.wait_ge(y_stored[q], ((s - 1) // 2) * 16 if isinstance(s, int) else stored(s, par))
                    nc.scalar.activation(ysl[:, q, :], bank[6 + q][:, 0:D], ACT.Copy).then_inc(ye_ready, 1)
                act.wait_ge(ht_psum, s + 1)
                nc.scalar.activation(hTr[:, par, :, :], bank[4 + par][:, :].rearrange("p (m n) -> p m n", m=HC),
                                     ACT.Gelu).then_inc(ht_ready, 1)
                if last:
                    act.wait_ge(ye_psum, s + 1)
                    act.wait_ge(y_stored[par], (s // 2) * 16)
                    nc.scalar.activation(ysl[:, par, :], bank[6 + par][:, 0:D], ACT.Copy).then_inc(ye_ready, 1)

            def stored(s, par):
                return (s - 1 - (1 - par)) * 8

            step(0, 0, True, False)
            step(1, 1, False, False)
            step(2, 0, False, False)
            with act.Fori(0, (SLOT_TILES - 5) // 2) as j:
                for u in range(2):
                    step(j * 2 + (u + 3), (u + 3) % 2, False, False)
            for s in (SLOT_TILES - 2, SLOT_TILES - 1):
                step(s, s % 2, False, s == SLOT_TILES - 1)

            with act.Fori(NCHUNK // 2, NCHUNK) as c:
                shared(c)

        @block.tensor
        def _(pe):
            pe.wait_ge(consts, 2)
            pe.wait_ge(ld_small, 80)
            nc.tensor.transpose(bank[0][:, 2 * P:2 * P + NVEC], vec_rows[:, :], ident[0:NVEC, 0:NVEC]).then_inc(vec_psum, 1)
            pe.wait_ge(cn_ready, 1)
            for k in range(KC):
                last = nc.tensor.transpose(bank[0][0:CK, k * P:(k + 1) * P], cn[:, k * CK:(k + 1) * CK], ident[:, :])
            last.then_inc(cnt_psum, 1)
            pe.wait_ge(ld_q, 16)
            for n in range(4):
                for u in range(4):
                    c, k = n * 2 + u // 2, u % 2
                    last = nc.tensor.transpose(bank[(5 + n) % 8][:, u * P:(u + 1) * P], wq_sb[:, k, c * P:(c + 1) * P],
                                               ident[:, :])
                last.then_inc(wqt_psum, 1)
                if n == 2:
                    pe.wait_ge(cnt_ready, KC)
            n = 0
            for w, loaded in ((wk_sb, ld_k), (wv_sb, ld_v)):
                pe.wait_ge(loaded, 16)
                for g in range(2):
                    for u in range(4):
                        c = g * 4 + u
                        for k in range(KC):
                            last = nc.tensor.matmul(bank[1 + n][:, u * P:(u + 1) * P], w[0:CK, k, c * P:(c + 1) * P],
                                                    cnT[0:CK, k, :], start=(k == 0), stop=(k == KC - 1))
                    last.then_inc(kv_psum, 1)
                    n += 1
            pe.wait_ge(wqt_ready, 4)
            for n in range(16):
                pe.wait_ge(kv_ready, 8)
                if n >= 4:
                    pe.wait_ge(fold_ready, n - 3)
                if n == 8:
                    pe.wait_ge(ld_o, 16)
                dst = bank[n % 4 + 1]
                for u in range(2):
                    o = dst[:, u * 2 * P:(u + 1) * 2 * P]
                    if n < 8:
                        k, c = n // 4, (n % 4) * 2 + u
                        last = nc.tensor.matmul(o, wqT[:, c, k, :], kbd[:, c, :, :], start=True, stop=True)
                    else:
                        b, c = (n - 8) // 4, ((n - 8) % 4) * 2 + u
                        last = nc.tensor.matmul(o, vbd[:, c, b, :], wo_sb[:, c, :], start=True, stop=True)
                last.then_inc(fold_psum, 1)
            pe.wait_ge(fold_ready, 16)
            pe.wait_ge(ld_b2, 64)

            def step(i, par, has, fixed):
                q = 1 - par
                if has(i):
                    pe.wait_ge(p_ready, i + 1)
                    for c in range(NPAIR):
                        last = nc.tensor.transpose(bank[6 + c // 4][:, (c % 4) * P:(c % 4 + 1) * P],
                                                   Eb[par].rearrange("p h j -> p (h j)")[:, c * P:(c + 1) * P], ident[:, :])
                    last.then_inc(pt_psum, 1)
                if has(i + 2):
                    pe.wait_ge(xn_ready, i + 3)
                    if fixed is None or i >= 0:
                        pe.wait_ge(sub_ready, i + 1)
                    b = (i + 2) // TPB
                    for g in range(2):
                        for k in range(KD):
                            last = nc.tensor.matmul(bank[2 + 2 * par + g][:, :], xnT[:, par, k, :],
                                                    A[:, at(b), k, g * 512:(g + 1) * 512].rearrange("p b n -> p (b n)"),
                                                    start=(k == 0), stop=(k == KD - 1))
                    last.then_inc(s_psum, 1)
                if has(i - 1):
                    pe.wait_ge(y_ready, i)
                    if has(i):
                        pe.wait_ge(pt_ready, i + 1)
                    for k in range(KD):
                        last = nc.tensor.transpose(bank[7][:, k * P:(k + 1) * P], ybuf[:, q, k * P:(k + 1) * P], ident[:, :])
                    last.then_inc(yt_psum, 1)
                if has(i + 3):
                    pe.wait_ge(z_ready, i + 4)
                    if fixed is None or i >= 2:
                        pe.wait_ge(l_ready, i - 1)
                    if fixed is None or i >= -2:
                        pe.wait_ge(xn_ready, i + 3)
                    for k in range(KD):
                        last = nc.tensor.transpose(bank[0][:, k * P:(k + 1) * P], zbuf[:, q, k * P:(k + 1) * P], ident[:, :])
                    last.then_inc(zt_psum, 1)
                if has(i):
                    pe.wait_ge(pt_ready, i + 1)
                    if fixed is None or i >= 1:
                        pe.wait_ge(x1_ready, i)
                    b = i // TPB
                    for c in range(NPAIR):
                        last = nc.tensor.matmul(bank[1][:, 0:D], PT[:, c, :],
                                                VW[:, at(b), c, :].rearrange("p b n -> p (b n)"),
                                                start=(c == 0), stop=(c == NPAIR - 1))
                    last.then_inc(o_psum, 1)
                if has(i - 1):
                    pe.wait_ge(yt_ready, i)
                    if has(i + 3):
                        pe.wait_ge(xn_ready, i + 4)
                    if fixed is not None and i >= 2:
                        pe.wait_ge(l_ready, i - 1)
                    for k in range(KD):
                        last = nc.tensor.matmul(bank[0][:, 0:E], yTb[:, q, k, :], rw_sb[:, k, :],
                                                start=(k == 0), stop=(k == KD - 1))
                    last.then_inc(l_psum, 1)

            attention(pe, step)

            def hidden(c, part=range(SHC)):
                for m in part:
                    if m >= 4:
                        pe.wait_ge(sh_ready, c * SHC + (m - 3))
                    s, hc = m // HC, m % HC
                    for k in range(KD):
                        last = nc.tensor.matmul(bank[2 + m % 4][:, :], sw1_sb[:, s, k, hc * P:(hc + 1) * P],
                                                yT[:, k, bass.ds(c * CHUNK, CHUNK)], start=(k == 0), stop=(k == KD - 1))
                    last.then_inc(sh_psum, 1)

            def project(c):
                pe.wait_ge(cur_ready, c + 1)
                pe.wait_ge(sh_ready, c * SHC + SHC)
                for t in range(TPC):
                    pe.wait_ge(acc_free, c * TPC + (t + 1))
                    o = bank[6 + t % 2][:, 0:D]
                    for m in range(SHC):
                        nc.tensor.matmul(o, hT[:, m, t * P:(t + 1) * P], sw2_sb[:, m, :], start=(m == 0), stop=False)
                    nc.tensor.matmul(o, ct_cur[:, t * P:(t + 1) * P], b2_rows[:, :], start=False, stop=True
                                     ).then_inc(acc_psum, 1)

            pe.wait_ge(ld_sw, 32)
            hidden(0, range(0, 2))
            pe.wait_ge(chosen_ready, 1)
            chosen_flat = chosen[:, :, :].rearrange("p t e -> p (t e)")
            nc.tensor.matmul(bank[0][:, 0:P], before[:, :], chosen_flat, start=True, stop=True)
            nc.tensor.matmul(bank[1][:, 0:P], ones[:, :], chosen_flat, start=True, stop=True).then_inc(count_psum, 1)

            hidden(0, range(2, SHC))
            pe.wait_ge(comb_ready, 1)
            for n in range(NCHUNK):
                if n >= 2:
                    pe.wait_ge(ct_ready, n - 1)
                for t in range(TPC):
                    last = nc.tensor.transpose(bank[n % 2][0:BIAS_ROWS, t * P:(t + 1) * P], comb[:, n * TPC + t, :],
                                               ident[:, :])
                last.then_inc(ct_psum, 1)
            project(0)
            hidden(1)
            project(1)

            pe.wait_ge(ld_w1, 16)
            pe.wait_ge(ld_w2, 16)
            pe.wait_ge(acc_free, NT // 2 + 2)

            def turn(s, par, fixed):
                pe.wait_ge(xsl_loaded[par], (s // 2 + 1) * 16 if isinstance(s, int) else (s - par) * 8 + 16)
                if not isinstance(s, int) or s >= 1:
                    pe.wait_ge(xt_ready, s)
                for k in range(KD):
                    last = nc.tensor.transpose(bank[0][:, k * P:(k + 1) * P], xsl[:, par, k * P:(k + 1) * P], ident[:, :])
                last.then_inc(xt_psum, 1)

            def give(s, par):
                expert = pe.value_load(emap[0:1, at(s)], min_val=0, max_val=E - 1)
                pe.wait_ge(ht_ready, s + 1)
                if not isinstance(s, int) or s >= 2:
                    pe.wait_ge(ye_ready, s - 1)
                for m in range(HC):
                    last = nc.tensor.matmul(bank[6 + par][:, 0:D], hTr[:, par, m, :],
                                            w2_sb[:, at(expert), m, :].rearrange("p e n -> p (e n)"),
                                            start=(m == 0), stop=(m == HC - 1))
                last.then_inc(ye_psum, 1)

            def step(s, par, first, last_step):
                expert = pe.value_load(emap[0:1, at(s)], min_val=0, max_val=E - 1)
                pe.wait_ge(xt_ready, s + 1)
                if not isinstance(s, int) or s >= 2:
                    pe.wait_ge(h_ready, s - 1)
                for k in range(KD):
                    last = nc.tensor.matmul(bank[2 + par][:, :], xsT[:, par, k, :],
                                            w1_sb[:, at(expert), k, :].rearrange("p e n -> p (e n)"),
                                            start=(k == 0), stop=(k == KD - 1))
                last.then_inc(h_psum, 1)
                if not last_step:
                    turn(s + 1, 1 - par, None)
                if not first:
                    give(s - 1, 1 - par)
                pe.wait_ge(h_ready, s + 1)
                if not isinstance(s, int) or s >= 2:
                    pe.wait_ge(ht_ready, s - 1)
                for m in range(HC):
                    last = nc.tensor.transpose(bank[4 + par][:, m * P:(m + 1) * P], hs[:, par, m * P:(m + 1) * P], ident[:, :])
                last.then_inc(ht_psum, 1)

            turn(0, 0, 0)
            step(0, 0, True, False)
            step(1, 1, False, False)
            step(2, 0, False, False)
            with pe.Fori(0, (SLOT_TILES - 5) // 2) as j:
                for u in range(2):
                    step(j * 2 + (u + 3), (u + 3) % 2, False, False)
            for s in (SLOT_TILES - 2, SLOT_TILES - 1):
                step(s, s % 2, False, s == SLOT_TILES - 1)
            give(SLOT_TILES - 1, (SLOT_TILES - 1) % 2)

            pe.wait_ge(ht_ready, SLOT_TILES)
            pe.wait_ge(ye_ready, SLOT_TILES)
            with pe.Fori(NCHUNK // 2, NCHUNK) as c:
                hidden(c)
                project(c)

        @block.vector
        def _(dve):
            dve.sem_inc(acc_free, 2)
            nc.vector.memset(vec_rows[:, :], 0.0).then_inc(bd_zeroed, 1)
            nc.vector.memset(b2_rows[:, :], 0.0).then_inc(bd_zeroed, 1)
            nc.vector.memset(kbd, 0.0).then_inc(bd_zeroed, 1)
            nc.vector.memset(vbd, 0.0).then_inc(bd_zeroed, 1)
            nc.vector.memset(combT[:, :], 0.0).then_inc(bd_zeroed, 1)
            dve.wait_ge(ld_ctx, 16)
            nc.vector.bn_stats(stc[:, :], ctx_sb).then_inc(cst_ready, 1)
            dve.wait_ge(cst_ready, 1)
            nc.vector.bn_aggr(mvc[:, :], stc[:, :]).then_inc(cmv_ready, 1)
            dve.wait_ge(crc_ready, 1)
            nc.vector.tensor_scalar(cn, ctx_sb, mvc[:, 0:1], rc[:, 0:1], ALU.subtract, ALU.mult).then_inc(cn_ready, 1)
            for n in range(4):
                dve.wait_ge(wqt_psum, n + 1)
                src = bank[(5 + n) % 8].rearrange("p (c k n) -> p c k n", c=2, k=KD)
                nc.vector.tensor_copy(wqT[:, n * 2:(n + 1) * 2, :, :], src).then_inc(wqt_ready, 1)
            for t in range(NT):
                if t % (NT // NX) == 0:
                    dve.wait_ge(ld_x[t // (NT // NX)], 16)
                nc.vector.bn_stats(st1[:, t, :], xs_all[:, t, :]).then_inc(st1_ready, 1)
            for t in range(NT):
                dve.wait_ge(st1_ready, t + 1)
                nc.vector.bn_aggr(mv1[:, t, :], st1[:, t, :]).then_inc(mv1_ready, 1)
            dve.wait_ge(tg_ready, 1)
            nc.vector.tensor_scalar(half_tg[:, :], tg[:, 1:2], 1.0 / S, None, ALU.mult).then_inc(htg_ready, 1)
            dve.wait_ge(consts, 5)
            nc.vector.tensor_copy(iota_e[:, :], iota_e_i[:, :]).then_inc(htg_ready, 1)
            nc.vector.tensor_copy(iota_tile[:, :], iota_tile_i[:, :]).then_inc(htg_ready, 1)
            nc.vector.tensor_copy(iota_slot[:, :], iota_slot_i[:, :]).then_inc(htg_ready, 1)
            dve.wait_ge(r1_ready, 1)
            dve.wait_ge(ld_b2, 64)
            dve.wait_ge(fold_ready, 16)

            def alone():
                dve.wait_ge(consts, 2)

            def step(i, par, has, fixed):
                q = 1 - par
                if has(i - 1):
                    dve.wait_ge(o_psum, i)
                    row = xs_all[:, at(i - 1), :].rearrange("p a d -> p (a d)")
                    nc.vector.scalar_tensor_tensor(row, bank[1][:, 0:D], tg[:, 0:1], row, ALU.mult, ALU.add
                                                   ).then_inc(x1_ready, 1)
                    alone()
                    dve.wait_ge(x1_ready, i)
                    nc.vector.bn_stats(st2[:, q, :], row).then_inc(st2_ready, 1)
                    alone()
                    dve.wait_ge(st2_ready, i)
                    nc.vector.bn_aggr(mv2[:, q, :], st2[:, q, :]).then_inc(mv2_ready, 1)
                if has(i + 1):
                    dve.wait_ge(exp_ready, i + 2)
                    nc.vector.tensor_reduce(sm[:, q, :], Eb[q], AX.X, ALU.add).then_inc(sum_ready, 1)
                    dve.wait_ge(sum_ready, i + 2)
                    nc.vector.reciprocal(rinv[:, q, :], sm[:, q, :]).then_inc(rcp_ready, 1)
                if has(i - 1):
                    dve.wait_ge(r2_ready, i)
                    if fixed is None or i >= 3:
                        dve.wait_ge(yt_psum, i - 2)
                    row = xs_all[:, at(i - 1), :].rearrange("p a d -> p (a d)")
                    nc.vector.tensor_scalar(ybuf[:, q, :], row, mv2[:, q, 0:1], r2[:, q:q + 1], ALU.subtract, ALU.mult
                                            ).then_inc(y_ready, 1)
                    dve.wait_ge(y_ready, i)
                    nc.vector.tensor_copy(y_all[:, at(i - 1), :].rearrange("p a d -> p (a d)"), ybuf[:, q, :]
                                          ).then_inc(y_kept, 1)
                if has(i - 2):
                    dve.wait_ge(l_psum, i - 1)
                    nc.vector.tensor_tensor(lg[:, par, :], bank[0][:, 0:E], rb_bc[:, :], ALU.add).then_inc(l_ready, 1)
                    alone()
                    dve.wait_ge(l_ready, i - 1)
                    nc.vector.max(v8[:, par, :], lg[:, par, :]).then_inc(val_ready, 1)
                    alone()
                    dve.wait_ge(val_ready, i - 1)
                    nc.vector.max_index(i8[:, par, :], v8[:, par, :], lg[:, par, :]).then_inc(idx_ready, 1)
                    dve.wait_ge(idx_ready, i - 1)
                    nc.vector.tensor_copy(val[:, at(i - 2), :].rearrange("p a k -> p (a k)"), v8[:, par, 0:TOPK]
                                          ).then_inc(top_kept, 1)
                    nc.vector.tensor_copy(idx[:, at(i - 2), :].rearrange("p a k -> p (a k)"), i8[:, par, 0:TOPK]
                                          ).then_inc(top_kept, 1)
                if has(i + 4):
                    if fixed is None or i >= -2:
                        dve.wait_ge(zt_psum, i + 3)
                    t = i + 4
                    nc.vector.tensor_scalar(zbuf[:, par, :], xs_all[:, at(t), :].rearrange("p a d -> p (a d)"),
                                            mv1[:, at(t), 0:1].rearrange("p a d -> p (a d)"), r1[:, at(t)],
                                            ALU.subtract, ALU.mult).then_inc(z_ready, 1)
                if has(i + 2):
                    dve.wait_ge(s_psum, i + 3)
                    scores = psum[:, (2 + 2 * par) * BANK:(4 + 2 * par) * BANK].rearrange("p (h j) -> p h j", h=H)
                    nc.vector.tensor_reduce(mx[:, par, :], scores, AX.X, ALU.max).then_inc(max_ready, 1)
                    dve.wait_ge(max_ready, i + 3)
                    if fixed is None or i >= 0:
                        dve.wait_ge(pt_psum, i + 1)
                    nc.vector.tensor_tensor(Eb[par], scores, mx[:, par, :].unsqueeze(2).broadcast_to([P, H, CTX]),
                                            ALU.subtract).then_inc(sub_ready, 1)

            attention(dve, step)

            count = [0]

            def link(ins):
                count[0] += 1
                ins.then_inc(route, 1)
                dve.wait_ge(route, count[0])

            dve.wait_ge(top_kept, 2 * NT)
            dve.wait_ge(htg_ready, 4)
            nc.vector.tensor_tensor(dif[:, :], val[:, :, 1], val[:, :, 0], ALU.subtract).then_inc(dif_ready, 1)
            for k in range(TOPK):
                link(nc.vector.tensor_tensor(oh[:, k, :, :], iota_e[:, :].unsqueeze(1).broadcast_to([P, NT, E]),
                                             idx[:, :, k].unsqueeze(2).broadcast_to([P, NT, E]), ALU.is_equal))
            nc.vector.tensor_tensor(chosen[:, :, :], oh[:, 0, :, :], oh[:, 1, :, :], ALU.add).then_inc(chosen_ready, 1)
            for r in (*run_t, *run_e):
                link(nc.vector.memset(r[:, :, :] if len(r.shape) == 3 else r[:, :], 0.0))
            dve.wait_ge(count_psum, 1)
            by_tile = bank[1][:, 0:P].rearrange("p (t e) -> p t e", t=NT)
            link(nc.vector.tensor_copy(tot[:, :, :], by_tile))
            link(nc.vector.tensor_copy(run_t[0][:, PADT:, :], tot[:, :, :]))
            a, d = 0, 1
            while d < NT:
                link(nc.vector.tensor_tensor(run_t[1 - a][:, PADT:, :], run_t[a][:, PADT:, :],
                                             run_t[a][:, PADT - d:PADT + NT - d, :], ALU.add))
                a, d = 1 - a, 2 * d
            upto = run_t[a][:, PADT:, :]
            link(nc.vector.tensor_tensor(full_tile[:, :, :], upto[:, NT - 1, :].unsqueeze(2).broadcast_to([P, E, NT]),
                                         iota_tile[:, :].unsqueeze(1).broadcast_to([P, E, NT]), ALU.is_gt))
            link(nc.vector.tensor_reduce(tiles_e[:, :], full_tile[:, :, :], AX.X, ALU.add))
            link(nc.vector.tensor_copy(run_e[0][:, PADE:], tiles_e[:, :]))
            f, d = 0, 1
            while d < E:
                link(nc.vector.tensor_tensor(run_e[1 - f][:, PADE:], run_e[f][:, PADE:], run_e[f][:, PADE - d:PADE + E - d],
                                             ALU.add))
                f, d = 1 - f, 2 * d
            ends = run_e[f][:, PADE:]
            link(nc.vector.tensor_tensor(start_e[:, :], ends, tiles_e[:, :], ALU.subtract))
            link(nc.vector.tensor_tensor(place[:, :, :], upto, tot[:, :, :], ALU.subtract))
            link(nc.vector.tensor_tensor(place[:, :, :], place[:, :, :],
                                         bank[0][:, 0:P].rearrange("p (t e) -> p t e", t=NT), ALU.add))
            link(nc.vector.scalar_tensor_tensor(place[:, :, :], start_e[:, :].unsqueeze(1).broadcast_to([P, NT, E]),
                                                float(P), place[:, :, :], ALU.mult, ALU.add))
            link(nc.vector.tensor_tensor(picked[:, 0, :, :], oh[:, 0, :, :], place[:, :, :], ALU.mult))
            link(nc.vector.tensor_tensor(picked[:, 1, :, :], oh[:, 1, :, :], place[:, :, :], ALU.mult))
            link(nc.vector.tensor_reduce(pos_f[:, :, :], picked[:, :, :, :], AX.X, ALU.add))
            nc.vector.tensor_copy(pos[:, :, :], pos_f[:, :, :]).then_inc(pos_ready, 1)
            link(nc.vector.tensor_tensor(passed[:, :, :], iota_slot[:, :].unsqueeze(2).broadcast_to([P, SLOT_TILES, E - 1]),
                                         ends[:, 0:E - 1].unsqueeze(1).broadcast_to([P, SLOT_TILES, E - 1]), ALU.is_ge))
            link(nc.vector.tensor_reduce(emap_f[:, :], passed[:, :, :], AX.X, ALU.add))
            link(nc.vector.tensor_copy(emap[:, :], emap_f[:, :]))
            dve.wait_ge(ex_ready, 1)
            link(nc.vector.tensor_scalar(den[:, :], ex[:, :], 1.0, None, ALU.add))
            link(nc.vector.reciprocal(prob[:, 0, :], den[:, :]))
            link(nc.vector.tensor_tensor(prob[:, 1, :], ex[:, :], prob[:, 0, :], ALU.mult))
            link(nc.vector.tensor_scalar(wgt[:, :, :], prob[:, :, :], tg[:, 1:2], None, ALU.mult))
            for k in range(TOPK):
                link(nc.vector.tensor_tensor(ohp[:, k, :, :], oh[:, k, :, :],
                                             prob[:, k, :].unsqueeze(2).broadcast_to([P, NT, E]), ALU.mult))
            link(nc.vector.memset(comb[:, :, :], 1.0))
            link(nc.vector.tensor_tensor(place[:, :, :], ohp[:, 0, :, :], ohp[:, 1, :, :], ALU.add))
            nc.vector.tensor_scalar(comb[:, :, 0:E], place[:, :, :], float(S), None, ALU.mult).then_inc(comb_ready, 1)
            for n in range(NCHUNK):
                dve.wait_ge(ct_psum, n + 1)
                nc.vector.tensor_copy(combT[0:BIAS_ROWS, n * CHUNK:(n + 1) * CHUNK], bank[0 + n % 2][0:BIAS_ROWS, :]
                                      ).then_inc(ct_ready, 1)

            def shared(c):
                dve.wait_ge(ct_ready, NCHUNK)
                nc.vector.tensor_copy(ct_cur, combT[:, bass.ds(c * CHUNK, CHUNK)]).then_inc(cur_ready, 1)
                for t in range(TPC):
                    dve.wait_ge(acc_psum, c * TPC + (t + 1))
                    row = xs_all[:, at(c * TPC + t), :].rearrange("p a d -> p (a d)")
                    nc.vector.scalar_tensor_tensor(row, bank[6 + t % 2][:, 0:D], half_tg[:, 0:1], row, ALU.mult, ALU.add
                                                   ).then_inc(acc_free, 1)

            with dve.Fori(0, NCHUNK // 2) as c:
                shared(c)

            dve.wait_ge(ld_b1, 16)

            def turn(s, par):
                dve.wait_ge(xt_psum, s + 1)
                nc.vector.tensor_copy(xsT[:, par, :, :], bank[0][:, 0:D].rearrange("p (k n) -> p k n", k=KD)
                                      ).then_inc(xt_ready, 1)

            def step(s, par, first, last):
                expert = dve.value_load(emap[0:1, at(s)], min_val=0, max_val=E - 1)
                dve.wait_ge(h_psum, s + 1)
                nc.vector.tensor_tensor(hs[:, par, :], bank[2 + par][:, :], b1_bc[:, bass.ds(expert * HID, HID)], ALU.add
                                        ).then_inc(h_ready, 1)
                if not last:
                    turn(s + 1, 1 - par)

            turn(0, 0)
            routed(dve, step)

            with dve.Fori(NCHUNK // 2, NCHUNK) as c:
                shared(c)

            dve.wait_ge(acc_free, NT + 2)
            with dve.Fori(0, NT // GBUF) as g:
                for u in range(GBUF):
                    dve.wait_ge(gathered[u], g * (16 * TOPK) + 16 * TOPK)
                    t = g * GBUF + u
                    row = xs_all[:, at(t), :].rearrange("p a d -> p (a d)")
                    for k in range(TOPK):
                        if k:
                            dve.wait_ge(first_added, t + 1)
                        nc.vector.scalar_tensor_tensor(row, gb[:, u, k, :], wgt[:, k, at(t)], row, ALU.mult, ALU.add
                                                       ).then_inc(out_ready if k else first_added, 1)


_INS = ['x', 'ctx_768', 'g_xattn', 'g_ffn', 'L0_xattn_g_x', 'L0_xattn_b_x', 'L0_xattn_g_c', 'L0_xattn_b_c', 'L0_xattn_Wq',
        'L0_xattn_Wk', 'L0_xattn_Wv', 'L0_xattn_Wo', 'L0_ffn_router_w', 'L0_ffn_router_b', 'L0_ffn_w1', 'L0_ffn_b1',
        'L0_ffn_w2', 'L0_ffn_b2', 'L0_ffn_sw1', 'L0_ffn_sb1', 'L0_ffn_sw2', 'L0_ffn_sb2']


def kernel(**inputs):
    import numpy as _np
    import concourse.bacc as _bacc
    from concourse import mybir as _mybir
    from concourse.bass_utils import run_bass_kernel_spmd as _run

    nc = _bacc.Bacc("TRN2", target_bir_lowering=False, num_devices=1)
    arrays, args = {}, []
    for name in _INS:
        a = _np.ascontiguousarray(inputs[name])
        arrays[f"in_{name}"] = a
        args.append(nc.dram_tensor(f"in_{name}", a.shape, _mybir.dt.from_np(a.dtype), kind="ExternalInput").ap())
    out = nc.dram_tensor("out_0", (BATCH, SEQ, D), F32, kind="ExternalOutput").ap()
    build(nc, *args, out)
    r = _run(nc, [arrays], core_ids=[0])
    return r.results[0]["out_0"]
```

```python
import numpy as np
import concourse.bass as bass
from concourse import mybir
from contextlib import ExitStack

F32 = mybir.dt.float32
I32 = mybir.dt.int32
U32 = mybir.dt.uint32
ALU = mybir.AluOpType
ACT = mybir.ActivationFunctionType
AX = mybir.AxisListType

P = 128
BATCH, SEQ, D = 2, 1024, 256
TOK = BATCH * SEQ
NT = TOK // P
TPB = SEQ // P
KD = D // P
H, DH, CTX, CDIM = 16, 64, 64, 192
NPAIR = H // 2
HJ = H * CTX
KC, CK = 2, CDIM // 2
E, S, HID = 8, 2, 512
HC = HID // P
SHC = S * HC
TOPK = 2
SLOT_TILES = TOK * TOPK // P + E - 1
SLOTS = SLOT_TILES * P
CHUNK = 512
TPC = CHUNK // P
NCHUNK = TOK // CHUNK
BANK = 512
INNER = H * DH
EPS = 1e-5
SCALE = 1.0 / np.sqrt(DH)
BIAS_ROWS = E + S
GROUPS = ((0, 4), (4, NT))
LEAD = 4
GBUF = 4


def build(nc, x, ctx, g_xattn, g_ffn, g_x, b_x, g_c, b_c, Wq, Wk, Wv, Wo,
          router_w, router_b, w1, b1, w2, b2, sw1, sb1, sw2, sb2, out):
    st = ExitStack()
    with st:
        def sb(name, shape, dt=F32):
            return st.enter_context(nc.sbuf_tensor(name, shape, dt))

        def sem(name):
            return st.enter_context(nc.semaphore(name))

        psum = st.enter_context(nc.psum_tensor("psum", [P, 8 * BANK], F32))
        bank = [psum[:, i * BANK:(i + 1) * BANK] for i in range(8)]

        x_slot = nc.dram_tensor("x_slot", [SLOTS, D], F32, kind="Internal").ap()
        y_slot = nc.dram_tensor("y_slot", [SLOTS, D], F32, kind="Internal").ap()

        xs_all = sb("xs_all", [P, NT, D])
        y_all = sb("y_all", [P, NT, D])
        yT = sb("yT", [P, KD, TOK])
        sw1_sb = sb("sw1_sb", [P, S, KD, HID])
        sw2_sb = sb("sw2_sb", [P, SHC, D])
        w1_sb = sb("w1_sb", [P, E, KD, HID])
        AVW = sb("AVW", [P, E * HC * D])
        A = AVW[:, 0:BATCH * KD * HJ].rearrange("p (b k n) -> p b k n", b=BATCH, k=KD)
        VW = AVW[:, BATCH * KD * HJ:].rearrange("p (b c n) -> p b c n", b=BATCH, c=NPAIR)
        w2_sb = AVW[:, :].rearrange("p (e m n) -> p e m n", e=E, m=HC)
        ident = sb("ident", [P, P])
        ones = sb("ones", [P, P])
        before = sb("before", [P, P])
        NVEC = SHC + 2 * KD + 2 * KC
        vec_rows, vec_col = sb("vec_rows", [NVEC, P]), sb("vec_col", [P, NVEC])
        sb1_col = vec_col[:, 0:SHC]
        gx_col, bx_col = (vec_col[:, SHC + i * KD:SHC + (i + 1) * KD] for i in range(2))
        gc_col, bc_col = (vec_col[0:CK, SHC + 2 * KD + i * KC:SHC + 2 * KD + (i + 1) * KC] for i in range(2))
        rw_sb = sb("rw_sb", [P, KD, E])
        rb_bc = sb("rb_bc", [P, E])
        b2_rows = sb("b2_rows", [P, D])
        gate = sb("gate", [P, 2])
        tg = sb("tg", [P, 2])
        half_tg = sb("half_tg", [P, 1])
        minus_half = sb("minus_half", [P, NT])
        eps_col = sb("eps_col", [P, 1])
        zero_row = sb("zero_row", [P, D])

        st1 = sb("st1", [P, NT, 6])
        mv1 = sb("mv1", [P, NT, 2])
        ve1 = sb("ve1", [P, NT])
        ra, rq, rb, r1 = (sb(n, [P, NT]) for n in ("ra", "rq", "rb", "r1"))
        stc, mvc, vec, rc = sb("stc", [P, 6]), sb("mvc", [P, 2]), sb("vec", [P, 1]), sb("rc", [P, 1])
        st2, mv2, ve2, r2 = sb("st2", [P, 2, 6]), sb("mv2", [P, 2, 2]), sb("ve2", [P, 2]), sb("r2", [P, 2])

        ARENA = 10240
        arena = sb("arena", [P, ARENA])

        def carve(sizes):
            at, got = 0, []
            for n in sizes:
                got.append(arena[:, at:at + n])
                at += n
            assert at <= ARENA, at
            return got

        ctx_sb, cn, cnT_, kbd_, wqT_, _, vbd_ = carve([CDIM, CDIM, KC * P, NPAIR * BATCH * P, NPAIR * KD * P, P * 3,
                                                       NPAIR * BATCH * P])
        cnT = cnT_.rearrange("p (k n) -> p k n", k=KC)
        kbd = kbd_.rearrange("p (c b n) -> p c b n", c=NPAIR, b=BATCH)
        vbd = vbd_.rearrange("p (c b n) -> p c b n", c=NPAIR, b=BATCH)
        wqT = wqT_.rearrange("p (c k n) -> p c k n", c=NPAIR, k=KD)
        y_flat = y_all[:, :, :].rearrange("p t d -> p (t d)")
        b1_bc = y_flat[:, 0:E * HID]
        yT_flat = yT[:, :, :].rearrange("p k t -> p (k t)")
        wk_sb = y_flat[:, 0:KC * INNER].rearrange("p (k n) -> p k n", k=KC)
        wv_sb = y_flat[:, KC * INNER:2 * KC * INNER].rearrange("p (k n) -> p k n", k=KC)
        wq_sb = yT_flat[:, 0:KD * INNER].rearrange("p (k n) -> p k n", k=KD)
        wo_sb = yT_flat[:, KD * INNER:].rearrange("p (c n) -> p c n", c=NPAIR)
        Eb0, Eb1, PT_, zbuf_, xnT_, ybuf_, yTb_ = carve([HJ, HJ, HJ, 2 * D, 2 * D, 2 * D, 2 * D])
        zbuf, ybuf = (v.rearrange("p (a d) -> p a d", a=2) for v in (zbuf_, ybuf_))
        xnT, yTb = (v.rearrange("p (a k n) -> p a k n", a=2, k=KD) for v in (xnT_, yTb_))
        Eb = [e.rearrange("p (h j) -> p h j", h=H) for e in (Eb0, Eb1)]
        PT = PT_.rearrange("p (c n) -> p c n", c=NPAIR)
        mx, sm, rinv = sb("mx", [P, 2, H]), sb("sm", [P, 2, H]), sb("rinv", [P, 2, H])
        lg = sb("lg", [P, 2, E])
        v8, i8 = sb("v8", [P, 2, 8]), sb("i8", [P, 2, 8], U32)
        hT_, ct_cur, xsl_, xsT_, hs_, hTr_, ysl_, gb_ = carve(
            [SHC * CHUNK, CHUNK, 2 * D, 2 * D, 2 * HID, 2 * HID, 2 * D, GBUF * TOPK * D])
        hT = hT_.rearrange("p (m t) -> p m t", m=SHC)
        xsl = xsl_.rearrange("p (a d) -> p a d", a=2)
        xsT = xsT_.rearrange("p (a k n) -> p a k n", a=2, k=KD)
        hs = hs_.rearrange("p (a n) -> p a n", a=2)
        hTr = hTr_.rearrange("p (a m n) -> p a m n", a=2, m=HC)
        ysl = ysl_.rearrange("p (a d) -> p a d", a=2)
        gb = gb_.rearrange("p (a k d) -> p a k d", a=GBUF, k=TOPK)

        val = sb("val", [P, NT, TOPK])
        idx = sb("idx", [P, NT, TOPK])
        iota_e, iota_e_i = sb("iota_e", [P, E]), sb("iota_e_i", [P, E], I32)
        iota_tile, iota_tile_i = sb("iota_tile", [P, NT]), sb("iota_tile_i", [P, NT], I32)
        iota_slot, iota_slot_i = sb("iota_slot", [P, SLOT_TILES]), sb("iota_slot_i", [P, SLOT_TILES], I32)
        oh = sb("oh", [P, TOPK, NT, E])
        chosen = sb("chosen", [P, NT, E])
        PADT, PADE = NT // 2, E // 2
        run_t = [sb(f"run_t{i}", [P, PADT + NT, E]) for i in range(2)]
        run_e = [sb(f"run_e{i}", [P, PADE + E]) for i in range(2)]
        full_tile = sb("full_tile", [P, E, NT])
        tiles_e, start_e = sb("tiles_e", [P, E]), sb("start_e", [P, E])
        tot = sb("tot", [P, NT, E])
        place = sb("place", [P, NT, E])
        picked = sb("picked", [P, TOPK, NT, E])
        pos_f = sb("pos_f", [P, TOPK, NT])
        pos = sb("pos", [P, TOPK, NT], I32)
        passed = sb("passed", [P, SLOT_TILES, E - 1])
        emap_f, emap = sb("emap_f", [P, SLOT_TILES]), sb("emap", [P, SLOT_TILES], I32)
        dif, ex, den = sb("dif", [P, NT]), sb("ex", [P, NT]), sb("den", [P, NT])
        prob = sb("prob", [P, TOPK, NT])
        wgt = sb("wgt", [P, TOPK, NT])
        ohp = picked
        comb = sb("comb", [P, NT, BIAS_ROWS])
        comb_cur = sb("comb_cur", [P, TPC, BIAS_ROWS])

        ld_ctx, ld_k, ld_v, ld_q, ld_o, ld_small, ld_gate = (
            sem(n) for n in ("ld_ctx", "ld_k", "ld_v", "ld_q", "ld_o", "ld_small", "ld_gate"))
        NX = 4
        ld_x = [sem(f"ld_x{i}") for i in range(NX)]
        ld_sw, ld_w1, ld_w2, ld_b1, ld_b2 = (sem(n) for n in ("ld_sw", "ld_w1", "ld_w2", "ld_b1", "ld_b2"))
        consts, consts_a, zeros_ready, zero_filled = (
            sem(n) for n in ("consts", "consts_a", "zeros_ready", "zero_filled"))
        cst_ready, cmv_ready, cve_ready, crc_ready, cn_ready, cnt_psum, cnt_ready = (
            sem(n) for n in ("cst_ready", "cmv_ready", "cve_ready", "crc_ready", "cn_ready", "cnt_psum", "cnt_ready"))
        bd_zeroed, kv_zeroed, vec_psum, vec_ready, kv_psum, kv_ready, wqt_psum, wqt_ready, fold_psum, fold_ready, vw_psum, vw_ready = (
            sem(n) for n in ("bd_zeroed", "kv_zeroed", "vec_psum", "vec_ready", "kv_psum", "kv_ready", "wqt_psum", "wqt_ready", "fold_psum", "fold_ready", "vw_psum", "vw_ready"))
        st1_ready, mv1_ready, r1_step, r1_ready, tg_ready, htg_ready = (
            sem(n) for n in ("st1_ready", "mv1_ready", "r1_step", "r1_ready", "tg_ready", "htg_ready"))
        z_ready, zt_psum, xn_ready, s_psum, max_ready, sub_ready, exp_ready, sum_ready, rcp_ready, p_ready = (
            sem(n) for n in ("z_ready", "zt_psum", "xn_ready", "s_psum", "max_ready", "sub_ready", "exp_ready",
                             "sum_ready", "rcp_ready", "p_ready"))
        pt_psum, pt_ready, o_psum, x1_ready, st2_ready, mv2_ready, ve2_ready, r2_ready, y_ready, y_kept = (
            sem(n) for n in ("pt_psum", "pt_ready", "o_psum", "x1_ready", "st2_ready", "mv2_ready", "ve2_ready",
                             "r2_ready", "y_ready", "y_kept"))
        yt_psum, yt_ready, l_psum, l_ready, val_ready, idx_ready, top_kept = (
            sem(n) for n in ("yt_psum", "yt_ready", "l_psum", "l_ready", "val_ready", "idx_ready", "top_kept"))
        route, chosen_ready, count_psum, dif_ready, ex_ready, pos_ready, comb_ready, ct_psum = (
            sem(n) for n in ("route", "chosen_ready", "count_psum", "dif_ready", "ex_ready", "pos_ready", "comb_ready",
                             "ct_psum"))
        cur_ready, sh_psum, sh_ready, acc_psum, acc_free = (
            sem(n) for n in ("cur_ready", "sh_psum", "sh_ready", "acc_psum", "acc_free"))
        scattered = sem("scattered")
        xsl_loaded = [sem(f"xsl_loaded{i}") for i in range(2)]
        xt_psum, xt_ready, h_psum, h_ready, ht_psum, ht_ready, ye_psum, ye_ready = (
            sem(n) for n in ("xt_psum", "xt_ready", "h_psum", "h_ready", "ht_psum", "ht_ready", "ye_psum", "ye_ready"))
        y_stored = [sem(f"y_stored{i}") for i in range(2)]
        gathered = [sem(f"gathered{i}") for i in range(GBUF)]
        first_added, out_ready, out_stored = (sem(n) for n in ("first_added", "out_ready", "out_stored"))

        x_rows = x.rearrange("b (t p) d -> p (b t) d", p=P)
        out_rows = out.rearrange("b (t p) d -> p (b t) d", p=P)
        x_slot_tiles = x_slot.rearrange("(s p) d -> s p d", p=P)
        y_slot_tiles = y_slot.rearrange("(s p) d -> s p d", p=P)

        block = st.enter_context(nc.Block())

        def at(t):
            return bass.ds(t, 1)

        STEPS = range(-LEAD, NT + 2)
        LOOP0, LOOP1 = LEAD, NT - LEAD

        VW_BANKS = (1, 6, 7)

        def attention(eng, step, before_first=None):
            for i in range(STEPS.start, LOOP0):
                if i == 0 and before_first:
                    before_first()
                step(i, i % 2, lambda t: 0 <= t < NT, i)
            with eng.Fori(0, (LOOP1 - LOOP0) // 2) as j:
                for par in range(2):
                    step(LOOP0 + par + j * 2, par, lambda t: True, None)
            for i in range(LOOP1, STEPS.stop):
                step(i, i % 2, lambda t: 0 <= t < NT, i)

        def routed(eng, step):
            step(0, 0, True, False)
            with eng.Fori(0, (SLOT_TILES - 3) // 2) as j:
                for u in range(2):
                    step(j * 2 + (u + 1), (u + 1) % 2, False, False)
            for s in (SLOT_TILES - 2, SLOT_TILES - 1):
                step(s, s % 2, False, s == SLOT_TILES - 1)

        @block.sync
        def _(sp):
            sp.dma_start(ctx_sb, ctx.rearrange("b j c -> (b j) c")).then_inc(ld_ctx, 16)
            sp.dma_start(wq_sb, Wq.rearrange("(k p) n -> p k n", p=P)).then_inc(ld_q, 16)
            sp.dma_start(wk_sb[0:CK], Wk.rearrange("(k p) n -> p k n", p=CK)).then_inc(ld_k, 16)
            n = NT // NX
            sp.dma_start(xs_all[:, 0:n, :], x_rows[:, 0:n, :]).then_inc(ld_x[0], 16)
            sp.dma_start(wv_sb[0:CK], Wv.rearrange("(k p) n -> p k n", p=CK)).then_inc(ld_v, 16)
            for i in range(1, NX):
                sp.dma_start(xs_all[:, i * n:(i + 1) * n, :], x_rows[:, i * n:(i + 1) * n, :]).then_inc(ld_x[i], 16)
            sp.dma_start(wo_sb, Wo.rearrange("(c p) n -> p c n", p=P)).then_inc(ld_o, 16)
            sp.dma_start(sw1_sb[:, :, :, :], sw1.rearrange("s (k p) n -> p s k n", p=P)).then_inc(ld_sw, 16)
            sp.dma_start(sw2_sb[:, :, :], sw2.rearrange("s (m p) n -> p (s m) n", p=P)).then_inc(ld_sw, 16)
            sp.dma_start(w1_sb[:, :, :, :], w1.rearrange("e (k p) n -> p e k n", p=P)).then_inc(ld_w1, 16)
            sp.wait_ge(zeros_ready, 1)
            sp.dma_start(x_slot_tiles.rearrange("s p d -> p s d"),
                         zero_row[:, :].unsqueeze(1).broadcast_to([P, SLOT_TILES, D])).then_inc(zero_filled, 16)
            sp.wait_ge(o_psum, NT)
            sp.dma_start(w2_sb, w2.rearrange("e (m p) n -> p e m n", p=P)).then_inc(ld_w2, 16)

            sp.wait_ge(scattered, 16 * TOPK * NT)
            for s in range(2):
                sp.dma_start(xsl[:, s, :], x_slot_tiles[s]).then_inc(xsl_loaded[s], 16)
            sp.dma_start(b1_bc, b1.rearrange("e n -> (e n)").partition_broadcast(P)).then_inc(ld_b1, 16)

            def load(s, par):
                sp.wait_ge(xt_psum, s - 1)
                sp.dma_start(xsl[:, par, :], x_slot_tiles[at(s)].rearrange("a p d -> p (a d)")
                             ).then_inc(xsl_loaded[par], 16)

            with sp.Fori(0, (SLOT_TILES - 3) // 2) as j:
                for u in range(2):
                    load(j * 2 + (u + 2), u)
            load(SLOT_TILES - 1, (SLOT_TILES - 1) % 2)

            with sp.Fori(0, NT) as t:
                sp.wait_ge(out_ready, t + 1)
                sp.dma_start(out_rows[:, at(t), :], xs_all[:, at(t), :]).then_inc(out_stored, 16)
            sp.wait_ge(out_stored, 16 * NT)

        @block.gpsimd
        def _(pool):
            nc.gpsimd.memset(zero_row[:, :], 0.0).then_inc(zeros_ready, 1)
            nc.gpsimd.memset(minus_half[:, :], -0.5).then_inc(consts_a, 1)
            nc.gpsimd.memset(eps_col[:, :], EPS).then_inc(consts_a, 1)
            nc.gpsimd.memset(ones[:, :], 1.0).then_inc(consts_a, 1)
            pool.wait_ge(consts_a, 3)
            nc.gpsimd.affine_select(out=ident[:, :], in_=ones[:, :], compare_op=ALU.is_equal, fill=0.0, base=0,
                                    pattern=[[-1, P]], channel_multiplier=1).then_inc(consts, 1)
            nc.gpsimd.affine_select(out=before[:, :], in_=ones[:, :], compare_op=ALU.is_gt, fill=0.0, base=0,
                                    pattern=[[1, P]], channel_multiplier=-1).then_inc(consts, 1)
            nc.gpsimd.memset(kbd, 0.0).then_inc(kv_zeroed, 1)
            nc.gpsimd.memset(vbd, 0.0).then_inc(kv_zeroed, 1)
            pool.wait_ge(cmv_ready, 1)
            nc.gpsimd.tensor_scalar(vec[:, :], mvc[:, 1:2], EPS, None, ALU.add).then_inc(cve_ready, 1)
            pool.wait_ge(cve_ready, 1)
            nc.gpsimd.tensor_tensor(rc[:, :], vec[:, :], minus_half[:, 0:1], ALU.pow).then_inc(crc_ready, 1)
            n = 0
            for first, end in GROUPS:
                g = slice(first, end)
                pool.wait_ge(mv1_ready, end)
                nc.gpsimd.tensor_scalar(ve1[:, g], mv1[:, g, 1], EPS, None, ALU.add).then_inc(r1_step, 1)
                pool.wait_ge(r1_step, n + 1)
                nc.gpsimd.tensor_tensor(ra[:, g], ve1[:, g], minus_half[:, g], ALU.pow).then_inc(r1_step, 1)
                pool.wait_ge(r1_step, n + 2)
                nc.gpsimd.tensor_tensor(rq[:, g], ra[:, g], ra[:, g], ALU.mult).then_inc(r1_step, 1)
                pool.wait_ge(r1_step, n + 3)
                nc.gpsimd.tensor_tensor(rq[:, g], rq[:, g], mv1[:, g, 1], ALU.mult).then_inc(r1_step, 1)
                pool.wait_ge(r1_step, n + 4)
                nc.gpsimd.tensor_scalar(rq[:, g], rq[:, g], EPS, None, ALU.add).then_inc(r1_step, 1)
                pool.wait_ge(r1_step, n + 5)
                nc.gpsimd.tensor_tensor(rb[:, g], rq[:, g], minus_half[:, g], ALU.pow).then_inc(r1_step, 1)
                pool.wait_ge(r1_step, n + 6)
                nc.gpsimd.tensor_tensor(r1[:, g], ra[:, g], rb[:, g], ALU.mult).then_inc(r1_ready, 1)
                n += 6
            nc.gpsimd.iota(iota_e_i[:, :], [[1, E]], base=0, channel_multiplier=0).then_inc(consts, 1)
            nc.gpsimd.iota(iota_tile_i[:, :], [[P, NT]], base=0, channel_multiplier=0).then_inc(consts, 1)
            nc.gpsimd.iota(iota_slot_i[:, :], [[1, SLOT_TILES]], base=0, channel_multiplier=0).then_inc(consts, 1)

            def step(i, par, has, fixed):
                if has(i - 1):
                    q = 1 - par
                    pool.wait_ge(mv2_ready, i)
                    nc.gpsimd.tensor_tensor(ve2[:, q:q + 1], mv2[:, q, 1:2], eps_col[:, :], ALU.add).then_inc(ve2_ready, 1)
                    pool.wait_ge(ve2_ready, i)
                    nc.gpsimd.tensor_tensor(r2[:, q:q + 1], ve2[:, q:q + 1], minus_half[:, 0:1], ALU.pow
                                            ).then_inc(r2_ready, 1)
                if has(i + 1):
                    q = 1 - par
                    pool.wait_ge(rcp_ready, i + 2)
                    nc.gpsimd.tensor_tensor(Eb[q], Eb[q], rinv[:, q, :].unsqueeze(2).broadcast_to([P, H, CTX]), ALU.mult
                                            ).then_inc(p_ready, 1)

            attention(pool, step)

            pool.wait_ge(pos_ready, 1)
            pool.wait_ge(y_kept, NT)
            pool.wait_ge(zero_filled, 16)
            for k in range(TOPK):
                for t in range(NT):
                    nc.gpsimd.indirect_dma_start(x_slot, bass.IndirectOffsetOnAxis(ap=pos[:, k, t:t + 1], axis=0),
                                                 y_all[:, t, :], None).then_inc(scattered, 16)
            pool.wait_ge(y_stored[0], 16 * ((SLOT_TILES + 1) // 2))
            pool.wait_ge(y_stored[1], 16 * (SLOT_TILES // 2))
            for t in range(NT):
                if t >= GBUF:
                    pool.wait_ge(out_ready, t - GBUF + 1)
                for k in range(TOPK):
                    nc.gpsimd.indirect_dma_start(gb[:, t % GBUF, k, :], None, y_slot,
                                                 bass.IndirectOffsetOnAxis(ap=pos[:, k, t:t + 1], axis=0)
                                                 ).then_inc(gathered[t % GBUF], 16)

        @block.scalar
        def _(act):
            act.wait_ge(bd_zeroed, 1)
            act.dma_start(vec_rows[0:SHC, :], sb1.rearrange("s (m p) -> (s m) p", p=P)).then_inc(ld_small, 16)
            at_row = SHC
            for v, n, w in ((g_x, KD, P), (b_x, KD, P), (g_c, KC, CK), (b_c, KC, CK)):
                act.dma_start(vec_rows[at_row:at_row + n, 0:w], v.rearrange("(k p) -> k p", p=w)).then_inc(ld_small, 16)
                at_row += n
            act.dma_start(gate[:, 0:1], g_xattn.partition_broadcast(P)).then_inc(ld_gate, 16)
            act.dma_start(gate[:, 1:2], g_ffn.partition_broadcast(P)).then_inc(ld_gate, 16)
            act.dma_start(rw_sb[:, :, :], router_w.rearrange("(k p) e -> p k e", p=P)).then_inc(ld_b2, 16)
            act.dma_start(rb_bc[:, :], router_b.partition_broadcast(P)).then_inc(ld_b2, 16)
            act.wait_ge(bd_zeroed, 2)
            act.dma_start(b2_rows[0:E, :], b2).then_inc(ld_b2, 16)
            act.dma_start(b2_rows[E:BIAS_ROWS, :], sb2).then_inc(ld_b2, 16)
            act.wait_ge(ld_gate, 32)
            nc.scalar.activation(tg[:, :], gate[:, :], ACT.Tanh).then_inc(tg_ready, 1)
            act.wait_ge(vec_psum, 1)
            act.wait_ge(cnt_psum, 1)
            nc.scalar.activation(vec_col[:, :], bank[0][:, 2 * P:2 * P + NVEC], ACT.Copy).then_inc(vec_ready, 1)
            act.wait_ge(vec_ready, 1)
            act.wait_ge(cnt_psum, 1)
            for k in range(KC):
                nc.scalar.activation(cnT[0:CK, k, :], bank[0][0:CK, k * P:(k + 1) * P], ACT.Identity,
                                     bias=bc_col[:, k:k + 1], scale=gc_col[:, k:k + 1]).then_inc(cnt_ready, 1)
            act.wait_ge(kv_zeroed, 2)
            n = 0
            for dst, scale in ((kbd, SCALE), (vbd, 1.0)):
                for g in range(2):
                    act.wait_ge(kv_psum, n + 1)
                    src = bank[1 + n][:, :].rearrange("p (c b j) -> p c b j", c=NPAIR // 2, b=BATCH)
                    for a in range(2):
                        rows = slice(a * DH, (a + 1) * DH)
                        nc.scalar.activation(dst[rows, g * 4:(g + 1) * 4, :, a * CTX:(a + 1) * CTX], src[rows],
                                             ACT.Copy, scale=float(scale)).then_inc(kv_ready, 1)
                    n += 1
            for n in range(8):
                act.wait_ge(fold_psum, n + 1)
                k, c = n // 4, (n % 4) * 2
                nc.scalar.activation(A[:, :, k, c * P:(c + 2) * P].rearrange("p b (c n) -> p c b n", c=2),
                                     bank[n % 4 + 1].rearrange("p (c b n) -> p c b n", c=2, b=BATCH), ACT.Copy
                                     ).then_inc(fold_ready, 1)

            def values_out():
                for n in range(8):
                    act.wait_ge(vw_psum, n + 1)
                    b, c = n // 4, (n % 4) * 2
                    nc.scalar.activation(VW[:, b, c:c + 2, :], bank[VW_BANKS[n % 3]].rearrange("p (c n) -> p c n", c=2),
                                         ACT.Copy).then_inc(vw_ready, 1)

            def step(i, par, has, fixed):
                q = 1 - par
                if has(i):
                    act.wait_ge(pt_psum, i + 1)
                    for g in range(2):
                        last = nc.scalar.activation(PT[:, g * 4:(g + 1) * 4, :],
                                                    bank[6 + g][:, :].rearrange("p (c n) -> p c n", c=4), ACT.Copy)
                    last.then_inc(pt_ready, 1)
                if has(i - 1):
                    act.wait_ge(yt_psum, i)
                    if fixed is None or i >= 3:
                        act.wait_ge(l_psum, i - 2)
                    src = bank[7][:, 0:D].rearrange("p (k n) -> p k n", k=KD)
                    nc.scalar.activation(yTb[:, q, :, :], src, ACT.Copy)
                    nc.scalar.activation(yT[:, :, bass.ds((i - 1) * P, P)], src, ACT.Copy).then_inc(yt_ready, 1)
                if has(i + 3):
                    act.wait_ge(zt_psum, i + 4)
                    if fixed is None or i >= -1:
                        act.wait_ge(s_psum, i + 2)
                    for k in range(KD):
                        last = nc.scalar.activation(xnT[:, q, k, :], bank[0][:, k * P:(k + 1) * P], ACT.Identity,
                                                    bias=bx_col[:, k:k + 1], scale=gx_col[:, k:k + 1])
                    last.then_inc(xn_ready, 1)
                if has(i + 2):
                    act.wait_ge(sub_ready, i + 3)
                    nc.scalar.activation(Eb[par], Eb[par], ACT.Exp).then_inc(exp_ready, 1)

            attention(act, step, values_out)

            act.wait_ge(dif_ready, 1)
            nc.scalar.activation(ex[:, :], dif[:, :], ACT.Exp).then_inc(ex_ready, 1)
            act.wait_ge(ld_b2, 64)

            def shared(c):
                for m in range(SHC):
                    act.wait_ge(sh_psum, c * SHC + (m + 1))
                    nc.scalar.activation(hT[:, m, :], bank[2 + m % 4][:, :], ACT.Gelu, bias=sb1_col[:, m:m + 1]
                                         ).then_inc(sh_ready, 1)

            with act.Fori(0, NCHUNK // 2) as c:
                shared(c)

            def step(s, par, first, last):
                q = 1 - par
                if not first:
                    act.wait_ge(ye_psum, s)
                    if not isinstance(s, int) or s >= 3:
                        act.wait_ge(y_stored[q], ((s - 1) // 2) * 16 if isinstance(s, int) else stored(s, par))
                    nc.scalar.activation(ysl[:, q, :], bank[6 + q][:, 0:D], ACT.Copy).then_inc(ye_ready, 1)
                act.wait_ge(ht_psum, s + 1)
                nc.scalar.activation(hTr[:, par, :, :], bank[4 + par].rearrange("p (m n) -> p m n", m=HC),
                                     ACT.Gelu).then_inc(ht_ready, 1)
                if not first:
                    store(s - 1, q, s)
                if last:
                    act.wait_ge(ye_psum, s + 1)
                    act.wait_ge(y_stored[par], (s // 2) * 16)
                    nc.scalar.activation(ysl[:, par, :], bank[6 + par][:, 0:D], ACT.Copy).then_inc(ye_ready, 1)
                    store(s, par, s + 1)

            def store(s, par, copied):
                act.wait_ge(ye_ready, copied)
                act.dma_start(y_slot_tiles[at(s)].rearrange("a p d -> p (a d)"), ysl[:, par, :]).then_inc(y_stored[par], 16)

            def stored(s, par):
                return (s - 1 - (1 - par)) * 8

            step(0, 0, True, False)
            step(1, 1, False, False)
            step(2, 0, False, False)
            with act.Fori(0, (SLOT_TILES - 5) // 2) as j:
                for u in range(2):
                    step(j * 2 + (u + 3), (u + 3) % 2, False, False)
            for s in (SLOT_TILES - 2, SLOT_TILES - 1):
                step(s, s % 2, False, s == SLOT_TILES - 1)

            with act.Fori(NCHUNK // 2, NCHUNK) as c:
                shared(c)

        @block.tensor
        def _(pe):
            pe.wait_ge(consts, 2)
            pe.wait_ge(ld_q, 16)
            for n in range(4):
                for u in range(4):
                    c, k = n * 2 + u // 2, u % 2
                    last = nc.tensor.transpose(bank[(5 + n) % 8][:, u * P:(u + 1) * P], wq_sb[:, k, c * P:(c + 1) * P],
                                               ident[:, :])
                last.then_inc(wqt_psum, 1)
            pe.wait_ge(wqt_ready, 4)
            pe.wait_ge(ld_small, 80)
            nc.tensor.transpose(bank[0][:, 2 * P:2 * P + NVEC], vec_rows[:, :], ident[0:NVEC, 0:NVEC]).then_inc(vec_psum, 1)
            pe.wait_ge(cn_ready, 1)
            for k in range(KC):
                last = nc.tensor.transpose(bank[0][0:CK, k * P:(k + 1) * P], cn[:, k * CK:(k + 1) * CK], ident[:, :])
            last.then_inc(cnt_psum, 1)
            pe.wait_ge(cnt_ready, KC)
            n = 0
            for w, loaded in ((wk_sb, ld_k), (wv_sb, ld_v)):
                pe.wait_ge(loaded, 16)
                for g in range(2):
                    for u in range(4):
                        c = g * 4 + u
                        for k in range(KC):
                            last = nc.tensor.matmul(bank[1 + n][:, u * P:(u + 1) * P], w[0:CK, k, c * P:(c + 1) * P],
                                                    cnT[0:CK, k, :], start=(k == 0), stop=(k == KC - 1))
                    last.then_inc(kv_psum, 1)
                    n += 1
            pe.wait_ge(kv_ready, 8)
            for n in range(8):
                if n >= 4:
                    pe.wait_ge(fold_ready, n - 3)
                for u in range(2):
                    k, c = n // 4, (n % 4) * 2 + u
                    last = nc.tensor.matmul(bank[n % 4 + 1][:, u * 2 * P:(u + 1) * 2 * P], wqT[:, c, k, :], kbd[:, c, :, :],
                                            start=True, stop=True)
                last.then_inc(fold_psum, 1)
            pe.wait_ge(fold_ready, 8)
            pe.wait_ge(ld_b2, 64)

            def values():
                pe.wait_ge(ld_o, 16)
                for n in range(8):
                    if n >= 3:
                        pe.wait_ge(vw_ready, n - 2)
                    for u in range(2):
                        b, c = n // 4, (n % 4) * 2 + u
                        last = nc.tensor.matmul(bank[VW_BANKS[n % 3]][:, u * D:(u + 1) * D], vbd[:, c, b, :], wo_sb[:, c, :],
                                                start=True, stop=True)
                    last.then_inc(vw_psum, 1)
                pe.wait_ge(vw_ready, 8)

            def step(i, par, has, fixed):
                q = 1 - par
                if has(i):
                    pe.wait_ge(p_ready, i + 1)
                    for c in range(NPAIR):
                        last = nc.tensor.transpose(bank[6 + c // 4][:, (c % 4) * P:(c % 4 + 1) * P],
                                                   Eb[par].rearrange("p h j -> p (h j)")[:, c * P:(c + 1) * P], ident[:, :])
                    last.then_inc(pt_psum, 1)
                if has(i + 2):
                    pe.wait_ge(xn_ready, i + 3)
                    if fixed is None or i >= 0:
                        pe.wait_ge(sub_ready, i + 1)
                    b = (i + 2) // TPB
                    for g in range(2):
                        for k in range(KD):
                            last = nc.tensor.matmul(bank[2 + 2 * par + g][:, :], xnT[:, par, k, :],
                                                    A[:, at(b), k, g * 512:(g + 1) * 512].rearrange("p b n -> p (b n)"),
                                                    start=(k == 0), stop=(k == KD - 1))
                    last.then_inc(s_psum, 1)
                if has(i - 1):
                    pe.wait_ge(y_ready, i)
                    if has(i):
                        pe.wait_ge(pt_ready, i + 1)
                    for k in range(KD):
                        last = nc.tensor.transpose(bank[7][:, k * P:(k + 1) * P], ybuf[:, q, k * P:(k + 1) * P], ident[:, :])
                    last.then_inc(yt_psum, 1)
                if has(i + 3):
                    pe.wait_ge(z_ready, i + 4)
                    if fixed is None or i >= 2:
                        pe.wait_ge(l_ready, i - 1)
                    if fixed is None or i >= -2:
                        pe.wait_ge(xn_ready, i + 3)
                    for k in range(KD):
                        last = nc.tensor.transpose(bank[0][:, k * P:(k + 1) * P], zbuf[:, q, k * P:(k + 1) * P], ident[:, :])
                    last.then_inc(zt_psum, 1)
                if has(i):
                    pe.wait_ge(pt_ready, i + 1)
                    if fixed is None or i >= 1:
                        pe.wait_ge(x1_ready, i)
                    b = i // TPB
                    for c in range(NPAIR):
                        last = nc.tensor.matmul(bank[1][:, 0:D], PT[:, c, :],
                                                VW[:, at(b), c, :].rearrange("p b n -> p (b n)"),
                                                start=(c == 0), stop=(c == NPAIR - 1))
                    last.then_inc(o_psum, 1)
                if has(i - 1):
                    pe.wait_ge(yt_ready, i)
                    if has(i + 3):
                        pe.wait_ge(xn_ready, i + 4)
                    if fixed is not None and i >= 2:
                        pe.wait_ge(l_ready, i - 1)
                    for k in range(KD):
                        last = nc.tensor.matmul(bank[0][:, 0:E], yTb[:, q, k, :], rw_sb[:, k, :],
                                                start=(k == 0), stop=(k == KD - 1))
                    last.then_inc(l_psum, 1)

            attention(pe, step, values)

            def hidden(c, part=range(SHC)):
                for m in part:
                    if m >= 4:
                        pe.wait_ge(sh_ready, c * SHC + (m - 3))
                    s, hc = m // HC, m % HC
                    for k in range(KD):
                        last = nc.tensor.matmul(bank[2 + m % 4][:, :], sw1_sb[:, s, k, hc * P:(hc + 1) * P],
                                                yT[:, k, bass.ds(c * CHUNK, CHUNK)], start=(k == 0), stop=(k == KD - 1))
                    last.then_inc(sh_psum, 1)

            def project(c):
                pe.wait_ge(comb_ready, c + 1)
                for t in range(TPC):
                    last = nc.tensor.transpose(bank[0][0:BIAS_ROWS, t * P:(t + 1) * P], comb_cur[:, t, :], ident[:, :])
                last.then_inc(ct_psum, 1)
                pe.wait_ge(cur_ready, c + 1)
                pe.wait_ge(sh_ready, c * SHC + SHC)
                for t in range(TPC):
                    pe.wait_ge(acc_free, c * TPC + (t + 1))
                    o = bank[6 + t % 2][:, 0:D]
                    for m in range(SHC):
                        nc.tensor.matmul(o, hT[:, m, t * P:(t + 1) * P], sw2_sb[:, m, :], start=(m == 0), stop=False)
                    nc.tensor.matmul(o, ct_cur[:, t * P:(t + 1) * P], b2_rows[:, :], start=False, stop=True
                                     ).then_inc(acc_psum, 1)

            pe.wait_ge(ld_sw, 32)
            hidden(0, range(0, 2))
            pe.wait_ge(chosen_ready, 1)
            chosen_flat = chosen[:, :, :].rearrange("p t e -> p (t e)")
            nc.tensor.matmul(bank[0][:, 0:P], before[:, :], chosen_flat, start=True, stop=True)
            nc.tensor.matmul(bank[1][:, 0:P], ones[:, :], chosen_flat, start=True, stop=True).then_inc(count_psum, 1)

            hidden(0, range(2, SHC))
            project(0)
            hidden(1)
            project(1)

            pe.wait_ge(ld_w1, 16)
            pe.wait_ge(ld_w2, 16)
            pe.wait_ge(acc_free, NT // 2 + 2)

            def turn(s, par, fixed):
                pe.wait_ge(xsl_loaded[par], (s // 2 + 1) * 16 if isinstance(s, int) else (s - par) * 8 + 16)
                if not isinstance(s, int) or s >= 1:
                    pe.wait_ge(xt_ready, s)
                for k in range(KD):
                    last = nc.tensor.transpose(bank[0][:, k * P:(k + 1) * P], xsl[:, par, k * P:(k + 1) * P], ident[:, :])
                last.then_inc(xt_psum, 1)

            def give(s, par):
                expert = pe.value_load(emap[0:1, at(s)], min_val=0, max_val=E - 1)
                pe.wait_ge(ht_ready, s + 1)
                if not isinstance(s, int) or s >= 2:
                    pe.wait_ge(ye_ready, s - 1)
                for m in range(HC):
                    last = nc.tensor.matmul(bank[6 + par][:, 0:D], hTr[:, par, m, :],
                                            w2_sb[:, at(expert), m, :].rearrange("p e n -> p (e n)"),
                                            start=(m == 0), stop=(m == HC - 1))
                last.then_inc(ye_psum, 1)

            def step(s, par, first, last_step):
                expert = pe.value_load(emap[0:1, at(s)], min_val=0, max_val=E - 1)
                pe.wait_ge(xt_ready, s + 1)
                if not isinstance(s, int) or s >= 2:
                    pe.wait_ge(h_ready, s - 1)
                for k in range(KD):
                    last = nc.tensor.matmul(bank[2 + par][:, :], xsT[:, par, k, :],
                                            w1_sb[:, at(expert), k, :].rearrange("p e n -> p (e n)"),
                                            start=(k == 0), stop=(k == KD - 1))
                last.then_inc(h_psum, 1)
                if not last_step:
                    turn(s + 1, 1 - par, None)
                if not first:
                    give(s - 1, 1 - par)
                pe.wait_ge(h_ready, s + 1)
                if not isinstance(s, int) or s >= 2:
                    pe.wait_ge(ht_ready, s - 1)
                for m in range(HC):
                    last = nc.tensor.transpose(bank[4 + par][:, m * P:(m + 1) * P], hs[:, par, m * P:(m + 1) * P], ident[:, :])
                last.then_inc(ht_psum, 1)

            turn(0, 0, 0)
            step(0, 0, True, False)
            step(1, 1, False, False)
            step(2, 0, False, False)
            with pe.Fori(0, (SLOT_TILES - 5) // 2) as j:
                for u in range(2):
                    step(j * 2 + (u + 3), (u + 3) % 2, False, False)
            for s in (SLOT_TILES - 2, SLOT_TILES - 1):
                step(s, s % 2, False, s == SLOT_TILES - 1)
            give(SLOT_TILES - 1, (SLOT_TILES - 1) % 2)

            pe.wait_ge(ht_ready, SLOT_TILES)
            pe.wait_ge(ye_ready, SLOT_TILES)
            with pe.Fori(NCHUNK // 2, NCHUNK) as c:
                hidden(c)
                project(c)

        @block.vector
        def _(dve):
            dve.sem_inc(acc_free, 2)
            nc.vector.memset(vec_rows[:, :], 0.0).then_inc(bd_zeroed, 1)
            nc.vector.memset(b2_rows[:, :], 0.0).then_inc(bd_zeroed, 1)
            dve.wait_ge(ld_ctx, 16)
            nc.vector.bn_stats(stc[:, :], ctx_sb).then_inc(cst_ready, 1)
            dve.wait_ge(cst_ready, 1)
            nc.vector.bn_aggr(mvc[:, :], stc[:, :]).then_inc(cmv_ready, 1)
            dve.wait_ge(crc_ready, 1)
            nc.vector.tensor_scalar(cn, ctx_sb, mvc[:, 0:1], rc[:, 0:1], ALU.subtract, ALU.mult).then_inc(cn_ready, 1)
            for n in range(4):
                dve.wait_ge(wqt_psum, n + 1)
                src = bank[(5 + n) % 8].rearrange("p (c k n) -> p c k n", c=2, k=KD)
                nc.vector.tensor_copy(wqT[:, n * 2:(n + 1) * 2, :, :], src).then_inc(wqt_ready, 1)
            for first, end in GROUPS:
                for t in range(first, end):
                    if t % (NT // NX) == 0:
                        dve.wait_ge(ld_x[t // (NT // NX)], 16)
                    nc.vector.bn_stats(st1[:, t, :], xs_all[:, t, :]).then_inc(st1_ready, 1)
                for t in range(first, end):
                    dve.wait_ge(st1_ready, t + 1)
                    nc.vector.bn_aggr(mv1[:, t, :], st1[:, t, :]).then_inc(mv1_ready, 1)
            dve.wait_ge(tg_ready, 1)
            nc.vector.tensor_scalar(half_tg[:, :], tg[:, 1:2], 1.0 / S, None, ALU.mult).then_inc(htg_ready, 1)
            dve.wait_ge(consts, 5)
            nc.vector.tensor_copy(iota_e[:, :], iota_e_i[:, :]).then_inc(htg_ready, 1)
            nc.vector.tensor_copy(iota_tile[:, :], iota_tile_i[:, :]).then_inc(htg_ready, 1)
            nc.vector.tensor_copy(iota_slot[:, :], iota_slot_i[:, :]).then_inc(htg_ready, 1)
            dve.wait_ge(r1_ready, 1)
            dve.wait_ge(ld_b2, 64)
            dve.wait_ge(fold_ready, 8)

            def alone():
                dve.wait_ge(consts, 2)

            def step(i, par, has, fixed):
                q = 1 - par
                if has(i - 1):
                    dve.wait_ge(o_psum, i)
                    row = xs_all[:, at(i - 1), :].rearrange("p a d -> p (a d)")
                    nc.vector.scalar_tensor_tensor(row, bank[1][:, 0:D], tg[:, 0:1], row, ALU.mult, ALU.add
                                                   ).then_inc(x1_ready, 1)
                    alone()
                    dve.wait_ge(x1_ready, i)
                    nc.vector.bn_stats(st2[:, q, :], row).then_inc(st2_ready, 1)
                    alone()
                    dve.wait_ge(st2_ready, i)
                    nc.vector.bn_aggr(mv2[:, q, :], st2[:, q, :]).then_inc(mv2_ready, 1)
                if has(i + 1):
                    dve.wait_ge(exp_ready, i + 2)
                    nc.vector.tensor_reduce(sm[:, q, :], Eb[q], AX.X, ALU.add).then_inc(sum_ready, 1)
                    dve.wait_ge(sum_ready, i + 2)
                    nc.vector.reciprocal(rinv[:, q, :], sm[:, q, :]).then_inc(rcp_ready, 1)
                if has(i - 1):
                    dve.wait_ge(r2_ready, i)
                    if fixed is None or i >= 3:
                        dve.wait_ge(yt_psum, i - 2)
                    row = xs_all[:, at(i - 1), :].rearrange("p a d -> p (a d)")
                    nc.vector.tensor_scalar(ybuf[:, q, :], row, mv2[:, q, 0:1], r2[:, q:q + 1], ALU.subtract, ALU.mult
                                            ).then_inc(y_ready, 1)
                    dve.wait_ge(y_ready, i)
                    nc.vector.tensor_copy(y_all[:, at(i - 1), :].rearrange("p a d -> p (a d)"), ybuf[:, q, :]
                                          ).then_inc(y_kept, 1)
                if has(i - 2):
                    dve.wait_ge(l_psum, i - 1)
                    nc.vector.tensor_tensor(lg[:, par, :], bank[0][:, 0:E], rb_bc[:, :], ALU.add).then_inc(l_ready, 1)
                    alone()
                    dve.wait_ge(l_ready, i - 1)
                    nc.vector.max(v8[:, par, :], lg[:, par, :]).then_inc(val_ready, 1)
                    alone()
                    dve.wait_ge(val_ready, i - 1)
                    nc.vector.max_index(i8[:, par, :], v8[:, par, :], lg[:, par, :]).then_inc(idx_ready, 1)
                    dve.wait_ge(idx_ready, i - 1)
                    nc.vector.tensor_copy(val[:, at(i - 2), :].rearrange("p a k -> p (a k)"), v8[:, par, 0:TOPK]
                                          ).then_inc(top_kept, 1)
                    nc.vector.tensor_copy(idx[:, at(i - 2), :].rearrange("p a k -> p (a k)"), i8[:, par, 0:TOPK]
                                          ).then_inc(top_kept, 1)
                if has(i + 4):
                    if i + 4 == GROUPS[0][1] if fixed is not None else False:
                        dve.wait_ge(r1_ready, len(GROUPS))
                    if fixed is None or i >= -2:
                        dve.wait_ge(zt_psum, i + 3)
                    t = i + 4
                    nc.vector.tensor_scalar(zbuf[:, par, :], xs_all[:, at(t), :].rearrange("p a d -> p (a d)"),
                                            mv1[:, at(t), 0:1].rearrange("p a d -> p (a d)"), r1[:, at(t)],
                                            ALU.subtract, ALU.mult).then_inc(z_ready, 1)
                if has(i + 2):
                    dve.wait_ge(s_psum, i + 3)
                    scores = psum[:, (2 + 2 * par) * BANK:(4 + 2 * par) * BANK].rearrange("p (h j) -> p h j", h=H)
                    nc.vector.tensor_reduce(mx[:, par, :], scores, AX.X, ALU.max).then_inc(max_ready, 1)
                    dve.wait_ge(max_ready, i + 3)
                    if fixed is None or i >= 0:
                        dve.wait_ge(pt_psum, i + 1)
                    nc.vector.tensor_tensor(Eb[par], scores, mx[:, par, :].unsqueeze(2).broadcast_to([P, H, CTX]),
                                            ALU.subtract).then_inc(sub_ready, 1)

            attention(dve, step)

            count = [0]

            def link(ins):
                count[0] += 1
                ins.then_inc(route, 1)
                dve.wait_ge(route, count[0])

            dve.wait_ge(top_kept, 2 * NT)
            dve.wait_ge(htg_ready, 4)
            nc.vector.tensor_tensor(dif[:, :], val[:, :, 1], val[:, :, 0], ALU.subtract).then_inc(dif_ready, 1)
            for k in range(TOPK):
                link(nc.vector.tensor_tensor(oh[:, k, :, :], iota_e[:, :].unsqueeze(1).broadcast_to([P, NT, E]),
                                             idx[:, :, k].unsqueeze(2).broadcast_to([P, NT, E]), ALU.is_equal))
            nc.vector.tensor_tensor(chosen[:, :, :], oh[:, 0, :, :], oh[:, 1, :, :], ALU.add).then_inc(chosen_ready, 1)
            for r in (*run_t, *run_e):
                link(nc.vector.memset(r[:, :, :] if len(r.shape) == 3 else r[:, :], 0.0))
            dve.wait_ge(count_psum, 1)
            by_tile = bank[1][:, 0:P].rearrange("p (t e) -> p t e", t=NT)
            link(nc.vector.tensor_copy(tot[:, :, :], by_tile))
            link(nc.vector.tensor_copy(run_t[0][:, PADT:, :], tot[:, :, :]))
            a, d = 0, 1
            while d < NT:
                link(nc.vector.tensor_tensor(run_t[1 - a][:, PADT:, :], run_t[a][:, PADT:, :],
                                             run_t[a][:, PADT - d:PADT + NT - d, :], ALU.add))
                a, d = 1 - a, 2 * d
            upto = run_t[a][:, PADT:, :]
            link(nc.vector.tensor_tensor(full_tile[:, :, :], upto[:, NT - 1, :].unsqueeze(2).broadcast_to([P, E, NT]),
                                         iota_tile[:, :].unsqueeze(1).broadcast_to([P, E, NT]), ALU.is_gt))
            link(nc.vector.tensor_reduce(tiles_e[:, :], full_tile[:, :, :], AX.X, ALU.add))
            link(nc.vector.tensor_copy(run_e[0][:, PADE:], tiles_e[:, :]))
            f, d = 0, 1
            while d < E:
                link(nc.vector.tensor_tensor(run_e[1 - f][:, PADE:], run_e[f][:, PADE:], run_e[f][:, PADE - d:PADE + E - d],
                                             ALU.add))
                f, d = 1 - f, 2 * d
            ends = run_e[f][:, PADE:]
            link(nc.vector.tensor_tensor(start_e[:, :], ends, tiles_e[:, :], ALU.subtract))
            link(nc.vector.tensor_tensor(place[:, :, :], upto, tot[:, :, :], ALU.subtract))
            link(nc.vector.tensor_tensor(place[:, :, :], place[:, :, :],
                                         bank[0][:, 0:P].rearrange("p (t e) -> p t e", t=NT), ALU.add))
            link(nc.vector.scalar_tensor_tensor(place[:, :, :], start_e[:, :].unsqueeze(1).broadcast_to([P, NT, E]),
                                                float(P), place[:, :, :], ALU.mult, ALU.add))
            link(nc.vector.tensor_tensor(picked[:, 0, :, :], oh[:, 0, :, :], place[:, :, :], ALU.mult))
            link(nc.vector.tensor_tensor(picked[:, 1, :, :], oh[:, 1, :, :], place[:, :, :], ALU.mult))
            link(nc.vector.tensor_reduce(pos_f[:, :, :], picked[:, :, :, :], AX.X, ALU.add))
            nc.vector.tensor_copy(pos[:, :, :], pos_f[:, :, :]).then_inc(pos_ready, 1)
            link(nc.vector.tensor_tensor(passed[:, :, :], iota_slot[:, :].unsqueeze(2).broadcast_to([P, SLOT_TILES, E - 1]),
                                         ends[:, 0:E - 1].unsqueeze(1).broadcast_to([P, SLOT_TILES, E - 1]), ALU.is_ge))
            link(nc.vector.tensor_reduce(emap_f[:, :], passed[:, :, :], AX.X, ALU.add))
            link(nc.vector.tensor_copy(emap[:, :], emap_f[:, :]))
            dve.wait_ge(ex_ready, 1)
            link(nc.vector.tensor_scalar(den[:, :], ex[:, :], 1.0, None, ALU.add))
            link(nc.vector.reciprocal(prob[:, 0, :], den[:, :]))
            link(nc.vector.tensor_tensor(prob[:, 1, :], ex[:, :], prob[:, 0, :], ALU.mult))
            link(nc.vector.tensor_scalar(wgt[:, :, :], prob[:, :, :], tg[:, 1:2], None, ALU.mult))
            for k in range(TOPK):
                link(nc.vector.tensor_tensor(ohp[:, k, :, :], oh[:, k, :, :],
                                             prob[:, k, :].unsqueeze(2).broadcast_to([P, NT, E]), ALU.mult))
            link(nc.vector.memset(comb[:, :, :], 1.0))
            link(nc.vector.tensor_tensor(place[:, :, :], ohp[:, 0, :, :], ohp[:, 1, :, :], ALU.add))
            link(nc.vector.tensor_scalar(comb[:, :, 0:E], place[:, :, :], float(S), None, ALU.mult))
            link(nc.vector.memset(ct_cur, 0.0))

            def bias_weights(c):
                nc.vector.tensor_copy(comb_cur[:, :, :], comb[:, bass.ds(c * TPC, TPC), :]).then_inc(comb_ready, 1)
                dve.wait_ge(ct_psum, c + 1)
                nc.vector.tensor_copy(ct_cur[0:BIAS_ROWS, :], bank[0][0:BIAS_ROWS, :]).then_inc(cur_ready, 1)

            def add_shared(c, t):
                dve.wait_ge(acc_psum, c * TPC + (t + 1))
                row = xs_all[:, at(c * TPC + t), :].rearrange("p a d -> p (a d)")
                nc.vector.scalar_tensor_tensor(row, bank[6 + t % 2][:, 0:D], half_tg[:, 0:1], row, ALU.mult, ALU.add
                                               ).then_inc(acc_free, 1)

            with dve.Fori(0, NCHUNK // 2) as c:
                bias_weights(c)
                for t in range(TPC):
                    add_shared(c, t)

            dve.wait_ge(ld_b1, 16)

            def turn(s, par):
                dve.wait_ge(xt_psum, s + 1)
                nc.vector.tensor_copy(xsT[:, par, :, :], bank[0][:, 0:D].rearrange("p (k n) -> p k n", k=KD)
                                      ).then_inc(xt_ready, 1)

            def step(s, par, first, last):
                expert = dve.value_load(emap[0:1, at(s)], min_val=0, max_val=E - 1)
                dve.wait_ge(h_psum, s + 1)
                nc.vector.tensor_tensor(hs[:, par, :], bank[2 + par][:, :], b1_bc[:, bass.ds(expert * HID, HID)], ALU.add
                                        ).then_inc(h_ready, 1)
                if not last:
                    turn(s + 1, 1 - par)

            turn(0, 0)
            routed(dve, step)

            PER = NT // (NT // 2)
            with dve.Fori(0, NCHUNK // 2) as h:
                c = h + NCHUNK // 2
                bias_weights(c)
                for t in range(TPC):
                    add_shared(c, t)
                    for r in range(PER):
                        u = t * PER + r
                        k0 = h * (TPC * PER) + u
                        dve.wait_ge(gathered[u % GBUF], h * (TPC * PER // GBUF * 16 * TOPK) + (u // GBUF + 1) * 16 * TOPK)
                        dve.wait_ge(acc_free, c * TPC + (t + 3))
                        row = xs_all[:, at(k0), :].rearrange("p a d -> p (a d)")
                        for k in range(TOPK):
                            if k:
                                dve.wait_ge(first_added, k0 + 1)
                            nc.vector.scalar_tensor_tensor(row, gb[:, u % GBUF, k, :], wgt[:, k, at(k0)], row, ALU.mult,
                                                           ALU.add).then_inc(out_ready if k else first_added, 1)


_INS = ['x', 'ctx_768', 'g_xattn', 'g_ffn', 'L0_xattn_g_x', 'L0_xattn_b_x', 'L0_xattn_g_c', 'L0_xattn_b_c', 'L0_xattn_Wq',
        'L0_xattn_Wk', 'L0_xattn_Wv', 'L0_xattn_Wo', 'L0_ffn_router_w', 'L0_ffn_router_b', 'L0_ffn_w1', 'L0_ffn_b1',
        'L0_ffn_w2', 'L0_ffn_b2', 'L0_ffn_sw1', 'L0_ffn_sb1', 'L0_ffn_sw2', 'L0_ffn_sb2']


def kernel(**inputs):
    import numpy as _np
    import concourse.bacc as _bacc
    from concourse import mybir as _mybir
    from concourse.bass_utils import run_bass_kernel_spmd as _run

    nc = _bacc.Bacc("TRN2", target_bir_lowering=False, num_devices=1)
    arrays, args = {}, []
    for name in _INS:
        a = _np.ascontiguousarray(inputs[name])
        arrays[f"in_{name}"] = a
        args.append(nc.dram_tensor(f"in_{name}", a.shape, _mybir.dt.from_np(a.dtype), kind="ExternalInput").ap())
    out = nc.dram_tensor("out_0", (BATCH, SEQ, D), F32, kind="ExternalOutput").ap()
    build(nc, *args, out)
    r = _run(nc, [arrays], core_ids=[0])
    return r.results[0]["out_0"]
```

```python
import numpy as np
import concourse.bass as bass
from concourse import mybir
from contextlib import ExitStack

F32 = mybir.dt.float32
F32R = mybir.dt.float32r
I32 = mybir.dt.int32
U32 = mybir.dt.uint32
ALU = mybir.AluOpType
ACT = mybir.ActivationFunctionType
AX = mybir.AxisListType

P = 128
BATCH, SEQ, D = 2, 1024, 256
TOK = BATCH * SEQ
NT = TOK // P
TPB = SEQ // P
KD = D // P
H, DH, CTX, CDIM = 16, 64, 64, 192
NPAIR = H // 2
HJ = H * CTX
KC, CK = 2, CDIM // 2
E, S, HID = 8, 2, 512
HC = HID // P
SHC = S * HC
TOPK = 2
SLOT_TILES = TOK * TOPK // P + E - 1
SLOTS = SLOT_TILES * P
SUB = 256
TPS = SUB // P
NSUB = TOK // SUB
EARLY = 6
PAIRS = SHC // 2
BANK = 512
INNER = H * DH
EPS = 1e-5
SCALE = 1.0 / np.sqrt(DH)
BIAS_ROWS = E + S
GROUPS = ((0, 4), (4, 8), (8, NT))
LEAD = 4
ROW = D + 1
GROUP_OUT = 4
COPIES = 3
GAP = 32


def build(nc, x, ctx, g_xattn, g_ffn, g_x, b_x, g_c, b_c, Wq, Wk, Wv, Wo,
          router_w, router_b, w1, b1, w2, b2, sw1, sb1, sw2, sb2, out):
    st = ExitStack()
    with st:
        def sb(name, shape, dt=F32):
            return st.enter_context(nc.sbuf_tensor(name, shape, dt))

        def sem(name):
            return st.enter_context(nc.semaphore(name))

        psum = st.enter_context(nc.psum_tensor("psum", [P, 8 * BANK], F32))
        bank = [psum[:, i * BANK:(i + 1) * BANK] for i in range(8)]

        x_slot = nc.dram_tensor("x_slot", [SLOTS, ROW], F32, kind="Internal").ap()
        y_tok = nc.dram_tensor("y_tok", [TOPK * TOK + SLOTS, D], F32, kind="Internal").ap()

        HT_WORDS, W_WORDS, SW_WORDS = SHC * SUB, E * HC * D, S * KD * HID
        AT_X = 0
        AT_COLS = AT_X + NT * D
        AT_Y = AT_COLS + 2 * KD * SUB
        AT_YT = AT_Y + NT * ROW
        AT_W = AT_YT + KD * TOK
        AT_SW = AT_W + 2 * W_WORDS
        AT_STEP = AT_SW + 4 * SW_WORDS
        AT_W2 = AT_STEP + 2 * SUB * 2 + 2 * HT_WORDS
        END = AT_W2 + W_WORDS
        AT_W2_HI = AT_YT + EARLY * KD * SUB - W_WORDS
        assert AT_W2_HI >= AT_COLS
        ALIGN = 32
        origin = -(-nc.sbuf_base // ALIGN) * ALIGN
        sb("mapped", [P, END])

        def at_words(name, shape, word, dt=F32):
            return nc.alloc_sbuf_tensor_at(name, shape, dt, offset=origin + 4 * word)

        def split(name, shape, hi_word, lo_word):
            return (at_words(name + "_hi", shape, hi_word, F32R), at_words(name + "_lo", shape, lo_word, F32R))

        xs_all = at_words("xs_all", [P, NT, D], AT_X)
        y_all = at_words("y_all", [P, NT, ROW], AT_Y)
        yT = at_words("yT", [P, NT, KD, P], AT_YT)
        A_WORDS = BATCH * KD * HJ
        A = split("A", [P, BATCH, KD, HJ], AT_W, AT_W + A_WORDS)
        VW = split("VW", [P, BATCH, NPAIR, D], AT_W + 2 * A_WORDS, AT_W + 3 * A_WORDS)
        w1_raw = at_words("w1_raw", [P, E, KD, HID], AT_W)
        w1_s = split("w1", [P, E, KD, HID], AT_W + W_WORDS, AT_W)
        w2_raw = at_words("w2_raw", [P, E, HC, D], AT_W2)
        w2_s = split("w2", [P, E, HC, D], AT_W2_HI, AT_W2)
        sw_raw = at_words("sw_raw", [P, 2 * SW_WORDS], AT_SW + 2 * SW_WORDS)
        sw_s = split("sw", [P, 2 * SW_WORDS], AT_SW, AT_SW + 2 * SW_WORDS)
        sw1_s = [v[:, 0:SW_WORDS].rearrange("p (s k n) -> p s k n", s=S, k=KD) for v in sw_s]
        sw2_s = [v[:, SW_WORDS:].rearrange("p (m n) -> p m n", m=SHC) for v in sw_s]

        wk_sb = at_words("wk_sb", [P, KC, INNER], AT_Y)
        wv_sb = at_words("wv_sb", [P, KC, INNER], AT_Y + KC * INNER)
        wq_sb = at_words("wq_sb", [P, KD, INNER], AT_YT)
        wo_sb = at_words("wo_sb", [P, NPAIR, D], AT_YT + KD * INNER)

        def row_of(word, specs):
            got = []
            for name, shape, dt in specs:
                got.append(at_words(name, shape, word, dt))
                word += int(np.prod(shape[1:]))
                word = -(-word // 8) * 8
            return got, word

        (ctx_sb, cn, cnT, kbd, wqT), end = row_of(AT_W + 2 * A_WORDS, [
            ("ctx_sb", [P, CDIM], F32), ("cn", [P, CDIM], F32), ("cnT", [P, KC, P], F32),
            ("kbd", [P, NPAIR, BATCH, P], F32), ("wqT", [P, NPAIR, KD, P], F32)])
        assert end <= AT_W + 4 * A_WORDS
        (Eb0, Eb1, half_sum, zbuf, xn_raw, xn_hi, xn_lo, pt_hi, pt_lo, ybuf, yTb, vbd), scratch = row_of(AT_STEP, [
            ("Eb0", [P, H, CTX], F32), ("Eb1", [P, H, CTX], F32), ("half_sum", [P, H, CTX // 2], F32),
            ("zbuf", [P, 2, D], F32), ("xn_raw", [P, 2, KD, P], F32), ("xn_hi", [P, 2, KD, P], F32R),
            ("xn_lo", [P, 2, KD, P], F32R), ("pt_hi", [P, NPAIR, P], F32R), ("pt_lo", [P, NPAIR, P], F32R),
            ("ybuf", [P, 2, D], F32), ("yTb", [P, 2, KD, P], F32), ("vbd", [P, NPAIR, BATCH, P], F32)])
        Eb = (Eb0, Eb1)
        NVEC, NCVEC = SHC + 2 * KD + E * HC, 2 * KC
        PADT, PADE = NT // 2, E // 2
        (zero_row, vec_rows, cvec_rows, b2_rows, st1, ones, before, iota_e_i, iota_tile_i, iota_slot_i,
         iota_e, iota_tile, iota_slot, oh, chosen, run_t0, run_t1, run_e0, run_e1, full_tile, tiles_e, start_e, tot, place,
         picked, pos_f, passed, emap_f, dif, ex, den, mv1, ve1, ra, rq, rb, r1, mx, sm, rinv, lg, v8, i8), end = row_of(scratch, [
             ("zero_row", [P, ROW], F32), ("vec_rows", [NVEC, P], F32), ("cvec_rows", [NCVEC, CK], F32),
             ("b2_rows", [COPIES * GAP, D], F32),
             ("st1", [P, NT, 6], F32), ("ones", [P, P], F32),
             ("before", [P, P], F32),
             ("iota_e_i", [P, E], I32), ("iota_tile_i", [P, NT], I32), ("iota_slot_i", [P, SLOT_TILES], I32),
             ("iota_e", [P, E], F32), ("iota_tile", [P, NT], F32), ("iota_slot", [P, SLOT_TILES], F32),
             ("oh", [P, TOPK, NT, E], F32), ("chosen", [P, NT, E], F32),
             ("run_t0", [P, PADT + NT, E], F32), ("run_t1", [P, PADT + NT, E], F32),
             ("run_e0", [P, PADE + E], F32), ("run_e1", [P, PADE + E], F32),
             ("full_tile", [P, E, NT], F32), ("tiles_e", [P, E], F32), ("start_e", [P, E], F32),
             ("tot", [P, NT, E], F32), ("place", [P, NT, E], F32), ("picked", [P, TOPK, NT, E], F32),
             ("pos_f", [P, TOPK, NT], F32), ("passed", [P, SLOT_TILES, E - 1], F32), ("emap_f", [P, SLOT_TILES], F32),
             ("dif", [P, NT], F32), ("ex", [P, NT], F32), ("den", [P, NT], F32),
             ("mv1", [P, NT, 2], F32), ("ve1", [P, NT], F32), ("ra", [P, NT], F32), ("rq", [P, NT], F32),
             ("rb", [P, NT], F32), ("r1", [P, NT], F32), ("mx", [P, 2, H], F32), ("sm", [P, 2, H], F32),
             ("rinv", [P, 2, H], F32), ("lg", [P, 2, E], F32), ("v8", [P, 2, 8], F32), ("i8", [P, 2, 8], U32)])
        assert AT_W2 <= scratch and end <= END, (scratch, end, END)
        run_t, run_e = (run_t0, run_t1), (run_e0, run_e1)
        ohp = picked

        def shared_buffers(name, cols_at, stage_at):
            return (split(name + "_cols", [P, TPS, KD, P], cols_at, cols_at + KD * SUB),
                    at_words(name + "_stage", [P, 2, 2, SUB], stage_at),
                    split(name + "_hT", [P, SHC, SUB], stage_at + 4 * SUB, stage_at + 4 * SUB + HT_WORDS))

        early = shared_buffers("early", AT_COLS, AT_STEP)
        late = shared_buffers("late", AT_W + W_WORDS, AT_W + W_WORDS + 2 * KD * SUB)
        y_got = at_words("y_got", [P, TOPK, NT, D], AT_W)
        assert TOPK * NT * D <= W_WORDS and 2 * KD * SUB + 4 * SUB + 2 * HT_WORDS <= W_WORDS
        (xsl, xsT_hi, xsT_lo, hs, hr, hr_hi, hr_lo, ysl), end = row_of(AT_STEP, [
            ("xsl", [P, 2, ROW], F32), ("xsT_hi", [P, KD, P], F32R), ("xsT_lo", [P, KD, P], F32R),
            ("hs", [P, HID], F32), ("hr", [P, HC, P], F32), ("hr_hi", [P, 2, HC, P], F32R),
            ("hr_lo", [P, 2, HC, P], F32R), ("ysl", [P, 2, D], F32)])
        assert end <= AT_W2 and ROW <= 2 * SUB

        ident = sb("ident", [P, P])
        vec_col, cvec_col = sb("vec_col", [P, NVEC]), sb("cvec_col", [CK, NCVEC])
        sb1_col = vec_col[:, 0:SHC]
        gx_col, bx_col = (vec_col[:, SHC + i * KD:SHC + (i + 1) * KD] for i in range(2))
        gc_col, bc_col = (cvec_col[:, i * KC:(i + 1) * KC] for i in range(2))
        b1_col = vec_col[:, NVEC - E * HC:]
        b1_cur = sb("b1_cur", [P, 2, HC])
        rw_sb = sb("rw_sb", [P, KD, E])
        rb_bc = sb("rb_bc", [P, E])
        bias_rows = sb("bias_rows", [COPIES * GAP, D], F32R)
        gate = sb("gate", [P, 2])
        tg = sb("tg", [P, 2])
        half_tg = sb("half_tg", [P, 1])
        minus_half = sb("minus_half", [P, NT])
        eps_col, warm = sb("eps_col", [P, 1]), sb("warm", [P, 1])
        stc, mvc, vec, rc = sb("stc", [P, 6]), sb("mvc", [P, 2]), sb("vec", [P, 1]), sb("rc", [P, 1])
        st2, mv2, ve2, r2 = sb("st2", [P, 2, 6]), sb("mv2", [P, 2, 2]), sb("ve2", [P, 2]), sb("r2", [P, 2])
        val = sb("val", [P, NT, TOPK])
        idx = sb("idx", [P, NT, TOPK])
        pos = sb("pos", [P, TOPK, NT], I32)
        emap = sb("emap", [P, SLOT_TILES], I32)
        dest = sb("dest", [P, SLOT_TILES], I32)
        spare = sb("spare", [P, SLOT_TILES], I32)
        prob = sb("prob", [P, TOPK, NT])
        wgt = sb("wgt", [P, TOPK, NT])
        comb = sb("comb", [P, NT, BIAS_ROWS])
        comb_cur = sb("comb_cur", [P, 2, TPS, COPIES * GAP])
        bias_w = sb("bias_w", [COPIES * GAP, 2, SUB], F32R)

        ld_ctx, ld_cvec, ld_k, ld_v, ld_o, ld_small, ld_gate, ld_b2 = (
            sem(n) for n in ("ld_ctx", "ld_cvec", "ld_k", "ld_v", "ld_o", "ld_small", "ld_gate", "ld_b2"))
        NX, NQ = 4, 2
        ld_q = [sem(f"ld_q{i}") for i in range(NQ)]
        ld_x = [sem(f"ld_x{i}") for i in range(NX)]
        ld_sw, ld_w1, ld_w2 = (sem(n) for n in ("ld_sw", "ld_w1", "ld_w2"))
        consts, consts_a, counters, zeros_ready, zero_filled, rows_zeroed, b2_hi, b2_ready = (
            sem(n) for n in ("consts", "consts_a", "counters", "zeros_ready", "zero_filled", "rows_zeroed", "b2_hi",
                             "b2_ready"))
        cst_ready, cmv_ready, cve_ready, crc_ready, cn_ready, cnt_psum, cnt_ready = (
            sem(n) for n in ("cst_ready", "cmv_ready", "cve_ready", "crc_ready", "cn_ready", "cnt_psum", "cnt_ready"))
        kv_zeroed, cvec_psum, cvec_ready, vec_psum, vec_ready, kv_psum, kv_ready, wqt_psum, wqt_ready = (
            sem(n) for n in ("kv_zeroed", "cvec_psum", "cvec_ready", "vec_psum", "vec_ready", "kv_psum", "kv_ready",
                             "wqt_psum", "wqt_ready"))
        fold_psum, fold_hi, fold_lo, vw_psum, vw_hi, vw_lo = (
            sem(n) for n in ("fold_psum", "fold_hi", "fold_lo", "vw_psum", "vw_hi", "vw_lo"))
        st1_ready, mv1_ready, r1_step, r1_ready, tg_ready, htg_ready = (
            sem(n) for n in ("st1_ready", "mv1_ready", "r1_step", "r1_ready", "tg_ready", "htg_ready"))
        z_ready, zt_psum, xn_raw_ready, xn_hi_ready, xn_ready, s_psum, max_ready, sub_ready, exp_ready = (
            sem(n) for n in ("z_ready", "zt_psum", "xn_raw_ready", "xn_hi_ready", "xn_ready", "s_psum", "max_ready",
                             "sub_ready", "exp_ready"))
        half_ready, sum_ready, rcp_ready, p_ready, pt_psum, pt_hi_ready, pt_lo_ready, o_psum = (
            sem(n) for n in ("half_ready", "sum_ready", "rcp_ready", "p_ready", "pt_psum", "pt_hi_ready", "pt_lo_ready",
                             "o_psum"))
        x1_ready, st2_ready, mv2_ready, ve2_ready, r2_ready, y_ready, y_kept = (
            sem(n) for n in ("x1_ready", "st2_ready", "mv2_ready", "ve2_ready", "r2_ready", "y_ready", "y_kept"))
        yt_psum, yt_ready, l_psum, l_ready, val_ready, idx_ready, top_kept = (
            sem(n) for n in ("yt_psum", "yt_ready", "l_psum", "l_ready", "val_ready", "idx_ready", "top_kept"))
        sw_hi_ready, sw_ready, w1_hi_ready, w1_ready, w2_hi_ready, w2_dve, w2_pool = (
            sem(n) for n in ("sw_hi_ready", "sw_ready", "w1_hi_ready", "w1_ready", "w2_hi_ready", "w2_dve", "w2_pool"))
        route, chosen_ready, count_psum, dif_ready, ex_ready, pos_ready, routed_all = (
            sem(n) for n in ("route", "chosen_ready", "count_psum", "dif_ready", "ex_ready", "pos_ready", "routed_all"))
        cols_hi, cols_ready, comb_ready, ct_psum, bias_hi, cur_ready, sh_psum, sh_raw, sh_hi, sh_lo, acc_psum, acc_free = (
            sem(n) for n in ("cols_hi", "cols_ready", "comb_ready", "ct_psum", "bias_hi", "cur_ready", "sh_psum", "sh_raw",
                             "sh_hi", "sh_lo", "acc_psum", "acc_free"))
        names_ready, scattered = sem("names_ready"), sem("scattered")
        xsl_loaded = [sem(f"xsl_loaded{i}") for i in range(2)]
        xt_psum, xt_hi, xt_lo, b1_ready, h_psum, h_ready, ht_psum, ht_raw, ht_hi, ht_lo, ye_psum, ye_ready = (
            sem(n) for n in ("xt_psum", "xt_hi", "xt_lo", "b1_ready", "h_psum", "h_ready", "ht_psum", "ht_raw", "ht_hi",
                             "ht_lo", "ye_psum", "ye_ready"))
        y_stored = [sem(f"y_stored{i}") for i in range(2)]
        y_loaded = [sem(f"y_loaded{i}") for i in range(NT // GROUP_OUT)]
        bias_psum = sem("bias_psum")
        first_added, out_ready = ([sem(f"{n}{i}") for i in range(2)] for n in ("first_added", "out_ready"))
        weighted, both_added, out_stored = sem("weighted"), sem("both_added"), sem("out_stored")

        x_rows = x.rearrange("b (t p) d -> p (b t) d", p=P)
        out_rows = out.rearrange("b (t p) d -> p (b t) d", p=P)
        x_slot_tiles = x_slot.rearrange("(s p) d -> s p d", p=P)
        y_tok_tiles = y_tok[0:TOPK * TOK, :].rearrange("(k t p) d -> p k t d", k=TOPK, p=P)

        block = st.enter_context(nc.Block())

        def at(t):
            return bass.ds(t, 1)

        def peeled(t):
            return isinstance(t, int)

        STEPS = range(-LEAD, NT + 3)
        LOOP0, LOOP1 = LEAD, NT - LEAD
        TOGETHER = 4

        WQ_BANK, K_BANKS, VEC_BANK = 1, (5, 6), 7
        FOLD_BANK, FOLDS = 1, 8
        FOLD_HALVES = (range(0, FOLDS // 2), range(FOLDS // 2, FOLDS))
        V_BANKS = (6, 7)
        VW_BANKS = (4, 5, 0, 1, 4, 6, 7, 1)
        VW_FIRST = 2
        VW_ORDER = ((0, 0), (0, 2), (1, 0), (1, 2), (0, 4), (0, 6), (1, 4), (1, 6))

        def attention(eng, step, before={}):
            for i in range(STEPS.start, LOOP0):
                if i in before:
                    before[i]()
                step(i, i % 2, lambda t: 0 <= t < NT, i)
            with eng.Fori(0, (LOOP1 - LOOP0) // TOGETHER) as j:
                for u in range(TOGETHER):
                    step(LOOP0 + u + j * TOGETHER, u % 2, lambda t: True, None)
            for i in range(LOOP1, STEPS.stop):
                if i in before:
                    before[i]()
                step(i, i % 2, lambda t: 0 <= t < NT, i)

        SW_PIECES = LOOP1 - LOOP0
        SW_PIECE = 2 * SW_WORDS // SW_PIECES

        SPLIT = 2
        W1_PER = 3
        W1_REST = E - W1_PER * (EARLY - 2 - SPLIT)
        W2_EARLY = (5, 6)
        W2_LAST, W2_THEN = (7, 1, 2), (3, 4, 0)
        W2_SPLIT = (*W2_EARLY, *W2_LAST, *W2_THEN)
        W2_POOL, W2_DVE = (5, 6, 1, 3), (7, 2, 4, 0)
        LATER = (0, 1)
        DELAY = 3
        HALVES = (range(0, PAIRS // 2), range(PAIRS // 2, PAIRS))

        def turn_of(c):
            return c - len(LATER)

        ROUTED0 = 5
        ROUTED1 = SLOT_TILES - 2
        UNROLL = 8
        IN_FLIGHT = 4
        assert (ROUTED1 - ROUTED0) % UNROLL == 0 and UNROLL % IN_FLIGHT == 0

        def experts(eng):
            regs = [eng.alloc_register(f"expert{n}") for n in range(IN_FLIGHT)]

            def fetch(s, u):
                eng.load(regs[u % IN_FLIGHT], emap[0:1, at(s)])

            return (lambda u: eng.snap(regs[u % IN_FLIGHT], min_val=0, max_val=E - 1)), fetch

        def routed(eng, step, before={}):
            for s in range(ROUTED0):
                if s in before:
                    before[s]()
                step(s, s % 2, s)
            with eng.Fori(0, (ROUTED1 - ROUTED0) // UNROLL) as j:
                for u in range(UNROLL):
                    step(j * UNROLL + (u + ROUTED0), (u + ROUTED0) % 2, u + ROUTED0)
            for s in range(ROUTED1, SLOT_TILES):
                step(s, s % 2, s)

        PAIRS_OUT = NT // TPS
        POOL_PAIRS = (0, 2, 4)
        VECTOR_PAIRS = [pair for pair in range(PAIRS_OUT) if pair not in POOL_PAIRS]
        LAST = NSUB - 1

        def routed_pair(eng, pair):
            first = pair * TPS
            eng.wait_ge(y_loaded[first // GROUP_OUT], 16 * TOPK)
            eng.wait_ge(acc_free, min(max(first + TPS, EARLY * TPS), LAST * TPS) + 2)
            return slice(first, first + TPS)

        def store(eng, pair, i, n):
            eng.wait_ge(out_ready[i], (n + 1) * TPS)
            tiles = slice(pair * TPS, (pair + 1) * TPS)
            eng.dma_start(out_rows[:, tiles, :], xs_all[:, tiles, :]).then_inc(out_stored, 16)

        def tiles_before(s, par):
            return (s // 2) * 16 if peeled(s) else (s - par) * 8

        @block.sync
        def _(sp):
            sp.dma_start(ctx_sb[:, :], ctx.rearrange("b j c -> (b j) c")).then_inc(ld_ctx, 16)
            for i in range(NQ):
                piece = slice(i * INNER // NQ, (i + 1) * INNER // NQ)
                sp.dma_start(wq_sb[:, :, piece], Wq[:, piece].rearrange("(k p) n -> p k n", p=P)).then_inc(ld_q[i], 16)
            sp.dma_start(wk_sb[0:CK], Wk.rearrange("(k p) n -> p k n", p=CK)).then_inc(ld_k, 16)
            n = NT // NX
            sp.dma_start(xs_all[:, 0:n, :], x_rows[:, 0:n, :]).then_inc(ld_x[0], 16)
            sp.dma_start(wv_sb[0:CK], Wv.rearrange("(k p) n -> p k n", p=CK)).then_inc(ld_v, 16)
            for i in range(1, NX):
                sp.dma_start(xs_all[:, i * n:(i + 1) * n, :], x_rows[:, i * n:(i + 1) * n, :]).then_inc(ld_x[i], 16)
            sp.dma_start(wo_sb[:, :, :], Wo.rearrange("(c p) n -> p c n", p=P)).then_inc(ld_o, 16)
            sp.dma_start(sw_raw[:, 0:SW_WORDS].rearrange("p (s k n) -> p s k n", s=S, k=KD),
                         sw1.rearrange("s (k p) n -> p s k n", p=P)).then_inc(ld_sw, 16)
            sp.dma_start(sw_raw[:, SW_WORDS:].rearrange("p (m n) -> p m n", m=SHC),
                         sw2.rearrange("s (m p) n -> p (s m) n", p=P)).then_inc(ld_sw, 16)
            sp.dma_start(gate[:, 0:1], g_xattn.partition_broadcast(P)).then_inc(ld_gate, 16)
            sp.dma_start(gate[:, 1:2], g_ffn.partition_broadcast(P)).then_inc(ld_gate, 16)
            sp.dma_start(rw_sb[:, :, :], router_w.rearrange("(k p) e -> p k e", p=P)).then_inc(ld_b2, 16)
            sp.dma_start(rb_bc[:, :], router_b.partition_broadcast(P)).then_inc(ld_b2, 16)
            sp.wait_ge(rows_zeroed, 1)
            for n in range(COPIES):
                sp.dma_start(b2_rows[n * GAP:n * GAP + E, :], b2).then_inc(ld_b2, 16)
                sp.dma_start(b2_rows[n * GAP + E:n * GAP + BIAS_ROWS, :], sb2).then_inc(ld_b2, 16)
            sp.wait_ge(zeros_ready, 2)
            sp.dma_start(x_slot_tiles.rearrange("s p d -> p s d"),
                         zero_row[:, :].unsqueeze(1).broadcast_to([P, SLOT_TILES, ROW])).then_inc(zero_filled, 16)
            sp.wait_ge(o_psum, NT)
            sp.dma_start(w1_raw[:, :, :, :], w1.rearrange("e (k p) n -> p e k n", p=P)).then_inc(ld_w1, 16)
            sp.wait_ge(routed_all, 1)
            sp.wait_ge(pos_ready, 1)
            sp.wait_ge(zero_filled, 16)
            sp.dma_start(w2_raw[:, :, :, :], w2.rearrange("e (m p) n -> p e m n", p=P)).then_inc(ld_w2, 16)

            sp.wait_ge(scattered, 16 * TOPK * NT)
            for s in range(2):
                sp.wait_ge(sh_lo, EARLY * PAIRS - 1 + s)
                sp.dma_start(xsl[:, s, :], x_slot_tiles[s]).then_inc(xsl_loaded[s], 16)

            def load(s, par):
                sp.wait_ge(xt_lo, s - 1)
                sp.dma_start(xsl[:, par, :], x_slot_tiles[at(s)].rearrange("a p d -> p (a d)")
                             ).then_inc(xsl_loaded[par], 16)

            with sp.Fori(0, (SLOT_TILES - 3) // 2) as j:
                for u in range(2):
                    load(j * 2 + (u + 2), u)
            load(SLOT_TILES - 1, (SLOT_TILES - 1) % 2)

            sp.wait_ge(ye_psum, SLOT_TILES)
            sp.wait_ge(y_stored[0], 16 * ((SLOT_TILES + 1) // 2))
            sp.wait_ge(y_stored[1], 16 * (SLOT_TILES // 2))
            for g in range(NT // GROUP_OUT):
                tiles = slice(g * GROUP_OUT, (g + 1) * GROUP_OUT)
                for k in range(TOPK):
                    sp.dma_start(y_got[:, k, tiles, :], y_tok_tiles[:, k, tiles, :]).then_inc(y_loaded[g], 16)

            for n, pair in enumerate(VECTOR_PAIRS):
                store(sp, pair, 1, n)
            sp.wait_ge(out_stored, 16 * NT // TPS)

        @block.gpsimd
        def _(pool):
            nc.gpsimd.memset(minus_half[:, :], -0.5).then_inc(consts_a, 1)
            nc.gpsimd.memset(eps_col[:, :], EPS).then_inc(consts_a, 1)
            nc.gpsimd.memset(ones[:, :], 1.0).then_inc(consts_a, 1)
            pool.wait_ge(consts_a, 3)
            nc.gpsimd.affine_select(out=ident[:, :], in_=ones[:, :], compare_op=ALU.is_equal, fill=0.0, base=0,
                                    pattern=[[-1, P]], channel_multiplier=1).then_inc(consts, 1)
            nc.gpsimd.affine_select(out=before[:, :], in_=ones[:, :], compare_op=ALU.is_gt, fill=0.0, base=0,
                                    pattern=[[1, P]], channel_multiplier=-1).then_inc(consts, 1)
            nc.gpsimd.memset(kbd[:, :, :, :], 0.0).then_inc(kv_zeroed, 1)
            pool.wait_ge(cmv_ready, 1)
            nc.gpsimd.tensor_scalar(vec[:, :], mvc[:, 1:2], EPS, None, ALU.add).then_inc(cve_ready, 1)
            pool.wait_ge(cve_ready, 1)
            nc.gpsimd.tensor_tensor(rc[:, :], vec[:, :], minus_half[:, 0:1], ALU.pow).then_inc(crc_ready, 1)
            nc.gpsimd.memset(vbd[:, :, :, :], 0.0).then_inc(kv_zeroed, 1)

            nc.gpsimd.iota(iota_e_i[:, :], [[1, E]], base=0, channel_multiplier=0).then_inc(counters, 1)
            nc.gpsimd.iota(iota_tile_i[:, :], [[P, NT]], base=0, channel_multiplier=0).then_inc(counters, 1)
            nc.gpsimd.iota(iota_slot_i[:, :], [[1, SLOT_TILES]], base=0, channel_multiplier=0).then_inc(counters, 1)
            nc.gpsimd.iota(spare[:, :], [[P, SLOT_TILES]], base=TOPK * TOK, channel_multiplier=1).then_inc(counters, 1)
            nc.gpsimd.memset(comb_cur[:, :, :], 0.0).then_inc(counters, 1)
            nc.gpsimd.memset(zero_row[:, 0:D], 0.0).then_inc(zeros_ready, 1)
            nc.gpsimd.iota(zero_row[:, D:].bitcast(I32), [[1, 1]], base=TOPK * TOK + SLOTS, channel_multiplier=0
                           ).then_inc(zeros_ready, 1)

            def twice(group):
                first, end = GROUPS[group]
                g, n = slice(first, end), group * 6
                pool.wait_ge(mv1_ready, end)
                nc.gpsimd.tensor_scalar(ve1[:, g], mv1[:, g, 1], EPS, None, ALU.add).then_inc(r1_step, 1)
                pool.wait_ge(r1_step, n + 1)
                nc.gpsimd.tensor_tensor(ra[:, g], ve1[:, g], minus_half[:, g], ALU.pow).then_inc(r1_step, 1)
                pool.wait_ge(r1_step, n + 2)
                nc.gpsimd.tensor_tensor(rq[:, g], ra[:, g], ra[:, g], ALU.mult).then_inc(r1_step, 1)
                pool.wait_ge(r1_step, n + 3)
                nc.gpsimd.tensor_tensor(rq[:, g], rq[:, g], mv1[:, g, 1], ALU.mult).then_inc(r1_step, 1)
                pool.wait_ge(r1_step, n + 4)
                nc.gpsimd.tensor_scalar(rq[:, g], rq[:, g], EPS, None, ALU.add).then_inc(r1_step, 1)
                pool.wait_ge(r1_step, n + 5)
                nc.gpsimd.tensor_tensor(rb[:, g], rq[:, g], minus_half[:, g], ALU.pow).then_inc(r1_step, 1)
                pool.wait_ge(r1_step, n + 6)
                nc.gpsimd.tensor_tensor(r1[:, g], ra[:, g], rb[:, g], ALU.mult).then_inc(r1_ready, 1)

            def beside_last():
                pool.wait_ge(kv_psum, 4)
                name_rows(0)
                columns_rest(0)

            twice(0)

            def name_rows(choice):
                return nc.gpsimd.iota(y_all[:, :, D:].bitcast(I32), [[P, NT], [1, 1]], base=choice * TOK,
                                      channel_multiplier=1).then_inc(names_ready, 1)

            def step(i, par, has, fixed):
                q = 1 - par
                if has(i + 1):
                    pool.wait_ge(exp_ready, i + 2)
                    if fixed is None or i >= 0:
                        pool.wait_ge(sum_ready, i + 1)
                    nc.gpsimd.tensor_tensor(half_sum[:, :, :], Eb[q][:, :, 0:CTX // 2], Eb[q][:, :, CTX // 2:], ALU.add
                                            ).then_inc(half_ready, 1)
                if fixed == -1:
                    twice(2)
                if has(i - 1):
                    pool.wait_ge(mv2_ready, i)
                    nc.gpsimd.tensor_tensor(ve2[:, q:q + 1], mv2[:, q, 1:2], eps_col[:, :], ALU.add).then_inc(ve2_ready, 1)
                    pool.wait_ge(ve2_ready, i)
                    nc.gpsimd.tensor_tensor(r2[:, q:q + 1], ve2[:, q:q + 1], minus_half[:, 0:1], ALU.pow
                                            ).then_inc(r2_ready, 1)
                if has(i + 1):
                    pool.wait_ge(rcp_ready, i + 2)
                    for g in range(2):
                        heads = slice(g * H // 2, (g + 1) * H // 2)
                        nc.gpsimd.tensor_tensor(Eb[q][:, heads, :], Eb[q][:, heads, :],
                                                rinv[:, q, heads].unsqueeze(2).broadcast_to([P, H // 2, CTX]), ALU.mult
                                                ).then_inc(p_ready, 1)
                if has(i + 3):
                    pool.wait_ge(xn_hi_ready, i + 4)
                    nc.gpsimd.tensor_tensor(xn_lo[:, q, :, :], xn_raw[:, q, :, :], xn_hi[:, q, :, :].bitcast(F32),
                                            ALU.subtract).then_inc(xn_ready, 1)
                if fixed is None:
                    piece = bass.ds((i - LOOP0) * SW_PIECE, SW_PIECE)
                    pool.wait_ge(sw_hi_ready, i - (LOOP0 - 1))
                    nc.gpsimd.tensor_tensor(sw_s[1][:, piece], sw_raw[:, piece], sw_s[0][:, piece].bitcast(F32),
                                            ALU.subtract).then_inc(sw_ready, 1)

            (cols_h, cols_l), stage, (hT_h, hT_l) = early

            def columns_rest(c):
                pool.wait_ge(cols_hi, c + 1)
                nc.gpsimd.tensor_tensor(cols_l[:, :, :, :], yT[:, c * TPS:(c + 1) * TPS, :, :],
                                        cols_h[:, :, :, :].bitcast(F32), ALU.subtract).then_inc(cols_ready, 1)

            attention(pool, step, {-1: lambda: twice(1), NT - 2: beside_last})

            for c in LATER:
                for j in range(PAIRS):
                    pool.wait_ge(sh_hi, c * PAIRS + j + 1)
                    pair = slice(2 * j, 2 * j + 2)
                    nc.gpsimd.tensor_tensor(hT_l[:, pair, :], stage[:, j % 2, :, :], hT_h[:, pair, :].bitcast(F32),
                                            ALU.subtract).then_inc(sh_lo, 1)
                columns_rest(c + 1)

            pool.wait_ge(pos_ready, 1)
            pool.wait_ge(y_kept, NT)
            pool.wait_ge(zero_filled, 16)
            for k in range(TOPK):
                if k:
                    pool.wait_ge(scattered, 16 * NT)
                    name_rows(k)
                pool.wait_ge(names_ready, k + 1)
                for t in range(NT):
                    nc.gpsimd.indirect_dma_start(x_slot, bass.IndirectOffsetOnAxis(ap=pos[:, k, t:t + 1], axis=0),
                                                 y_all[:, t, :], None).then_inc(scattered, 16)
            for e in W2_POOL:
                pool.wait_ge(w2_hi_ready, W2_SPLIT.index(e) + 1)
                nc.gpsimd.tensor_tensor(w2_s[1][:, e, :, :], w2_raw[:, e, :, :], w2_s[0][:, e, :, :].bitcast(F32),
                                        ALU.subtract).then_inc(w2_pool, 1)
            for s in range(SLOT_TILES):
                pool.wait_ge(ye_ready, s + 1)
                nc.gpsimd.indirect_dma_start(y_tok, bass.IndirectOffsetOnAxis(ap=dest[:, s:s + 1], axis=0),
                                             ysl[:, s % 2, :], None).then_inc(y_stored[s % 2], 16)
            for n, pair in enumerate(POOL_PAIRS):
                tiles = routed_pair(pool, pair)
                both = y_got[:, :, tiles, :]
                nc.gpsimd.tensor_tensor(both, both, wgt[:, :, tiles].unsqueeze(3).broadcast_to([P, TOPK, TPS, D]),
                                        ALU.mult).then_inc(weighted, 1)
                pool.wait_ge(weighted, n + 1)
                nc.gpsimd.tensor_tensor(y_got[:, 0, tiles, :], y_got[:, 0, tiles, :], y_got[:, 1, tiles, :], ALU.add
                                        ).then_inc(first_added[0], 1)
                pool.wait_ge(first_added[0], n + 1)
                nc.gpsimd.tensor_tensor(xs_all[:, tiles, :], xs_all[:, tiles, :], y_got[:, 0, tiles, :], ALU.add
                                        ).then_inc(out_ready[0], TPS)

        @block.scalar
        def _(act):
            for n, v in enumerate((g_c, b_c)):
                act.dma_start(cvec_rows[n * KC:(n + 1) * KC, :], v.rearrange("(k p) -> k p", p=CK)).then_inc(ld_cvec, 16)
            act.wait_ge(consts_a, 1)
            nc.scalar.activation(warm[:, :], minus_half[:, 0:1], ACT.Exp)
            at_row = 0
            for v, n in ((sb1.rearrange("s (m p) -> (s m) p", p=P), SHC), (g_x.rearrange("(k p) -> k p", p=P), KD),
                         (b_x.rearrange("(k p) -> k p", p=P), KD), (b1.rearrange("e (m p) -> (e m) p", p=P), E * HC)):
                act.dma_start(vec_rows[at_row:at_row + n, :], v).then_inc(ld_small, 16)
                at_row += n
            act.wait_ge(cvec_psum, 1)
            act.wait_ge(cnt_psum, 1)
            nc.scalar.activation(cvec_col[:, :], bank[0][0:CK, 2 * P:2 * P + NCVEC], ACT.Copy).then_inc(cvec_ready, 1)
            act.wait_ge(cvec_ready, 1)
            for k in range(KC):
                nc.scalar.activation(cnT[0:CK, k, :], bank[0][0:CK, k * P:(k + 1) * P], ACT.Identity,
                                     bias=bc_col[:, k:k + 1], scale=gc_col[:, k:k + 1]).then_inc(cnt_ready, 1)

            def blocks(dst, n, src, scale):
                act.wait_ge(kv_psum, n + 1)
                g = n % 2
                src = src[:, :].rearrange("p (c b j) -> p c b j", c=NPAIR // 2, b=BATCH)
                for a in range(2):
                    rows = slice(a * DH, (a + 1) * DH)
                    nc.scalar.activation(dst[rows, g * 4:(g + 1) * 4, :, a * CTX:(a + 1) * CTX], src[rows],
                                         ACT.Copy, scale=float(scale)).then_inc(kv_ready, 1)

            act.wait_ge(kv_zeroed, 2)
            for n in range(2):
                blocks(kbd, n, bank[K_BANKS[n]], SCALE)
            act.wait_ge(vec_psum, 1)
            nc.scalar.activation(vec_col[:, :], bank[VEC_BANK][:, 0:NVEC], ACT.Copy).then_inc(vec_ready, 1)
            act.wait_ge(vec_ready, 1)

            def fold_out(half):
                for n in FOLD_HALVES[half]:
                    act.wait_ge(fold_psum, n + 1)
                    k, c = n // 4, (n % 4) * 2
                    nc.scalar.activation(A[0][:, :, k, c * P:(c + 2) * P].rearrange("p b (c n) -> p c b n", c=2),
                                         bank[FOLD_BANK + n % 4].rearrange("p (c b n) -> p c b n", c=2, b=BATCH), ACT.Copy
                                         ).then_inc(fold_hi, 1)

            def values_blocks():
                for n in range(2):
                    blocks(vbd, 2 + n, bank[V_BANKS[n]], 1.0)

            def values_out():
                for n, (b, c) in enumerate(VW_ORDER):
                    act.wait_ge(vw_psum, n + 1)
                    nc.scalar.activation(VW[0][:, b, c:c + 2, :],
                                         bank[VW_BANKS[n]].rearrange("p (c n) -> p c n", c=2),
                                         ACT.Copy).then_inc(vw_hi, 1)
                act.wait_ge(ld_gate, 32)
                nc.scalar.activation(tg[:, :], gate[:, :], ACT.Tanh).then_inc(tg_ready, 1)

            def step(i, par, has, fixed):
                q = 1 - par
                if has(i):
                    if fixed is None or i >= 1:
                        act.wait_ge(o_psum, i)
                    for g in range(2):
                        act.wait_ge(pt_psum, i * 2 + (g + 1))
                        last = nc.scalar.activation(pt_hi[:, g * 4:(g + 1) * 4, :],
                                                    bank[6 + g][:, :].rearrange("p (c n) -> p c n", c=4), ACT.Copy)
                    last.then_inc(pt_hi_ready, 1)
                if has(i + 1):
                    act.wait_ge(sub_ready, i + 2)
                    nc.scalar.activation(Eb[q][:, :, :], Eb[q][:, :, :], ACT.Exp).then_inc(exp_ready, 1)
                if fixed == -1:
                    values_out()
                if has(i + 3):
                    act.wait_ge(zt_psum, i + 4)
                    if fixed is None or i >= -1:
                        act.wait_ge(s_psum, i + 2)
                    for k in range(KD):
                        last = nc.scalar.activation(xn_raw[:, q, k, :], bank[0][:, k * P:(k + 1) * P], ACT.Identity,
                                                    bias=bx_col[:, k:k + 1], scale=gx_col[:, k:k + 1])
                    last.then_inc(xn_raw_ready, 1)
                    act.wait_ge(xn_raw_ready, i + 4)
                    nc.scalar.activation(xn_hi[:, q, :, :], xn_raw[:, q, :, :], ACT.Copy).then_inc(xn_hi_ready, 1)
                if has(i - 3):
                    act.wait_ge(idx_ready, i - 2)
                    nc.scalar.activation(val[:, at(i - 3), :].rearrange("p a k -> p (a k)"), v8[:, q, 0:TOPK], ACT.Copy
                                         ).then_inc(top_kept, 1)
                    nc.scalar.activation(idx[:, at(i - 3), :].rearrange("p a k -> p (a k)"), i8[:, q, 0:TOPK], ACT.Copy
                                         ).then_inc(top_kept, 1)
                if fixed == NT - 1:
                    shared(0, early, range(0, 1))
                if has(i - 1):
                    act.wait_ge(yt_psum, i)
                    if fixed is None or i >= 3:
                        act.wait_ge(l_psum, i - 2)
                    src = bank[7][:, 0:D].rearrange("p (k n) -> p k n", k=KD)
                    nc.scalar.activation(yTb[:, q, :, :], src, ACT.Copy)
                    nc.scalar.activation(yT[:, at(i - 1), :, :].rearrange("p a k n -> p (a k) n"), src, ACT.Copy
                                         ).then_inc(yt_ready, 1)
                    nc.scalar.activation(y_all[:, at(i - 1), 0:D].rearrange("p a d -> p (a d)"), ybuf[:, q, :], ACT.Copy
                                         ).then_inc(y_kept, 1)
                if fixed is None:
                    act.wait_ge(ld_sw, 32)
                    piece = bass.ds((i - LOOP0) * SW_PIECE, SW_PIECE)
                    nc.scalar.activation(sw_s[0][:, piece], sw_raw[:, piece], ACT.Copy).then_inc(sw_hi_ready, 1)

            def columns(c, buffers):
                nc.scalar.activation(buffers[0][0][:, :, :, :], yT[:, bass.ds(c * TPS, TPS), :, :], ACT.Copy
                                     ).then_inc(cols_hi, 1)

            def shared(c, buffers, pairs=range(PAIRS)):
                _, stage, (hT_h, _) = buffers
                for j in pairs:
                    act.wait_ge(sh_psum, c * PAIRS + (j + 1))
                    if not (peeled(c) and c * PAIRS + j < 2):
                        act.wait_ge(sh_lo, c * PAIRS + (j - 1))
                    for u in range(2):
                        last = nc.scalar.activation(stage[:, j % 2, u, :], bank[2 + j][:, u * SUB:(u + 1) * SUB], ACT.Gelu,
                                                    bias=sb1_col[:, 2 * j + u:2 * j + u + 1])
                    last.then_inc(sh_raw, 1)
                    act.wait_ge(sh_raw, c * PAIRS + (j + 1))
                    nc.scalar.activation(hT_h[:, 2 * j:2 * j + 2, :], stage[:, j % 2, :, :], ACT.Copy).then_inc(sh_hi, 1)

            def warm_gelu():
                nc.scalar.activation(warm[:, :], minus_half[:, 0:1], ACT.Gelu)

            def first_columns():
                act.wait_ge(yt_ready, TPS)
                columns(0, early)

            attention(act, step, {-3: lambda: fold_out(0), -2: lambda: fold_out(1), -1: values_blocks,
                                  NT - 2: first_columns, NT - 1: warm_gelu,
                                  NT: lambda: shared(0, early, range(1, 2)),
                                  NT + 1: lambda: shared(0, early, range(2, PAIRS))})

            act.wait_ge(yt_ready, NT)
            columns(1, early)
            shared(1, early)
            columns(2, early)
            act.wait_ge(dif_ready, 1)
            nc.scalar.activation(ex[:, :], dif[:, :], ACT.Exp).then_inc(ex_ready, 1)
            warm_gelu()

            def w1_round(experts):
                for e in experts:
                    nc.scalar.activation(w1_s[0][:, at(e), :, :], w1_raw[:, at(e), :, :], ACT.Copy
                                         ).then_inc(w1_hi_ready, 1)

            def w2_round(e):
                nc.scalar.activation(w2_s[0][:, e, :, :], w2_raw[:, e, :, :], ACT.Copy).then_inc(w2_hi_ready, 1)

            act.wait_ge(ld_w1, 16)
            with act.Fori(SPLIT, EARLY - 2) as c:
                shared(c, early)
                columns(c + 1, early)
                w1_round((c - SPLIT) * W1_PER + n for n in range(W1_PER))
            shared(EARLY - 2, early)
            columns(EARLY - 1, early)
            w1_round(range(E - W1_REST, E))
            act.wait_ge(ld_w2, 16)
            act.wait_ge(cols_ready, EARLY - 1)
            for e in W2_EARLY:
                w2_round(e)
            shared(EARLY - 1, early)
            act.wait_ge(cols_ready, EARLY)
            act.wait_ge(scattered, 16 * TOPK * NT)
            for e in W2_LAST:
                w2_round(e)

            def turned(s, par):
                act.wait_ge(xt_psum, s + 1)
                nc.scalar.activation(xsT_hi[:, :, :], bank[par][:, 0:D].rearrange("p (k n) -> p k n", k=KD), ACT.Copy
                                     ).then_inc(xt_hi, 1)

            def output(s, par):
                act.wait_ge(ye_psum, s + 1)
                if not peeled(s) or s >= 2:
                    act.wait_ge(y_stored[par], tiles_before(s, par))
                nc.scalar.activation(ysl[:, par, :], bank[6 + par][:, 0:D], ACT.Copy).then_inc(ye_ready, 1)

            def step(s, par, *_):
                if not peeled(s) or s + 1 < SLOT_TILES:
                    turned(s + 1, 1 - par)
                else:
                    act.wait_ge(h_psum, SLOT_TILES)
                    columns(EARLY, late)
                if not peeled(s) or s >= 2:
                    output(s - 2, par)
                act.wait_ge(ht_psum, s + 1)
                act.wait_ge(b1_ready, s + 1)
                if not peeled(s) or s >= 1:
                    act.wait_ge(ht_lo, s)
                for m in range(HC):
                    last = nc.scalar.activation(hr[:, m, :], bank[4 + par][:, m * P:(m + 1) * P], ACT.Gelu,
                                                bias=b1_cur[:, par, m:m + 1])
                last.then_inc(ht_raw, 1)
                act.wait_ge(ht_raw, s + 1)
                nc.scalar.activation(hr_hi[:, par, :, :], hr[:, :, :], ACT.Copy).then_inc(ht_hi, 1)

            act.wait_ge(sh_lo, EARLY * PAIRS)
            turned(0, 0)
            for e in W2_THEN:
                w2_round(e)
            routed(act, step)
            for s in (SLOT_TILES - 2, SLOT_TILES - 1):
                output(s, s % 2)

            shared(EARLY, late)
            for c in range(EARLY + 1, NSUB):
                columns(c, late)
                shared(c, late)
            for n, pair in enumerate(POOL_PAIRS):
                store(act, pair, 0, n)

        @block.tensor
        def _(pe):
            pe.wait_ge(consts, 2)
            def context():
                pe.wait_ge(ld_cvec, 32)
                nc.tensor.transpose(bank[0][0:CK, 2 * P:2 * P + NCVEC], cvec_rows[:, :], ident[0:NCVEC, 0:NCVEC]
                                    ).then_inc(cvec_psum, 1)
                pe.wait_ge(cn_ready, 1)
                for k in range(KC):
                    last = nc.tensor.transpose(bank[0][0:CK, k * P:(k + 1) * P], cn[:, k * CK:(k + 1) * CK], ident[:, :])
                last.then_inc(cnt_psum, 1)

            def heads(w, g, out):
                for u in range(4):
                    c = g * 4 + u
                    for k in range(KC):
                        last = nc.tensor.matmul(out[:, u * P:(u + 1) * P], w[0:CK, k, c * P:(c + 1) * P],
                                                cnT[0:CK, k, :], start=(k == 0), stop=(k == KC - 1))
                last.then_inc(kv_psum, 1)

            for n in range(4):
                if n % (4 // NQ) == 0:
                    pe.wait_ge(ld_q[n // (4 // NQ)], 16)
                if n == 2:
                    context()
                for u in range(4):
                    c, k = n * 2 + u // 2, u % 2
                    last = nc.tensor.transpose(bank[WQ_BANK + n][:, u * P:(u + 1) * P], wq_sb[:, k, c * P:(c + 1) * P],
                                               ident[:, :])
                last.then_inc(wqt_psum, 1)
            pe.wait_ge(cnt_ready, KC)
            pe.wait_ge(ld_k, 16)
            for g in range(2):
                heads(wk_sb, g, bank[K_BANKS[g]])
            pe.wait_ge(ld_small, 64)
            nc.tensor.transpose(bank[VEC_BANK][:, 0:NVEC], vec_rows[:, :], ident[0:NVEC, 0:NVEC]).then_inc(vec_psum, 1)

            def fold(half):
                for n in FOLD_HALVES[half]:
                    if n == 0:
                        pe.wait_ge(wqt_ready, 4)
                        pe.wait_ge(kv_ready, 2)
                    if n == 2:
                        pe.wait_ge(kv_ready, 4)
                    if n >= 4:
                        pe.wait_ge(fold_lo, n - 3)
                    for u in range(2):
                        k, c = n // 4, (n % 4) * 2 + u
                        last = nc.tensor.matmul(bank[FOLD_BANK + n % 4][:, u * 2 * P:(u + 1) * 2 * P], wqT[:, c, k, :],
                                                kbd[:, c, :, :], start=True, stop=True)
                    last.then_inc(fold_psum, 1)
                if half:
                    pe.wait_ge(fold_lo, FOLDS)

            def values():
                pe.wait_ge(ld_v, 16)
                pe.wait_ge(vec_ready, 1)
                for g in range(2):
                    heads(wv_sb, g, bank[V_BANKS[g]])
                pe.wait_ge(ld_o, 16)
                for n, (b, c0) in enumerate(VW_ORDER):
                    if n == 0:
                        pe.wait_ge(kv_ready, 6)
                    if n == 3:
                        pe.wait_ge(kv_ready, 8)
                    if VW_BANKS.index(VW_BANKS[n]) < n:
                        pe.wait_ge(vw_lo, VW_BANKS.index(VW_BANKS[n]) + 1)
                    for u in range(2):
                        last = nc.tensor.matmul(bank[VW_BANKS[n]][:, u * D:(u + 1) * D],
                                                vbd[:, c0 + u, b, :], wo_sb[:, c0 + u, :], start=True, stop=True)
                    last.then_inc(vw_psum, 1)
                pe.wait_ge(vw_lo, 5)
                pe.wait_ge(ld_b2, (2 + 2 * COPIES) * 16)

            def step(i, par, has, fixed):
                q = 1 - par
                if has(i):
                    for c in range(NPAIR):
                        if c == 0 and fixed == 0:
                            pe.wait_ge(vw_lo, 7)
                        if c % 4 == 0:
                            pe.wait_ge(p_ready, i * 2 + (c // 4 + 1))
                        if c == NPAIR // 2 and (fixed is None or i >= 2):
                            pe.wait_ge(yt_ready, i - 1)
                        last = nc.tensor.transpose(bank[6 + c // 4][:, (c % 4) * P:(c % 4 + 1) * P],
                                                   Eb[par][:, 2 * c:2 * c + 2, :].rearrange("p h j -> p (h j)"), ident[:, :])
                        if c % 4 == 3:
                            last.then_inc(pt_psum, 1)
                if has(i + 3):
                    pe.wait_ge(z_ready, i + 4)
                    if fixed is None or i >= 3:
                        pe.wait_ge(l_ready, i - 2)
                    if fixed is None or i >= -2:
                        pe.wait_ge(xn_raw_ready, i + 3)
                    for k in range(KD):
                        last = nc.tensor.transpose(bank[0][:, k * P:(k + 1) * P], zbuf[:, q, k * P:(k + 1) * P], ident[:, :])
                    last.then_inc(zt_psum, 1)
                if has(i + 2):
                    pe.wait_ge(xn_ready, i + 3)
                    if fixed is None or i >= 0:
                        pe.wait_ge(sub_ready, i + 1)
                    b = (i + 2) // TPB
                    for g in range(2):
                        n = 0
                        for x_part, a_part in ((xn_hi, A[0]), (xn_hi, A[1]), (xn_lo, A[0])):
                            for k in range(KD):
                                last = nc.tensor.matmul(bank[2 + 2 * par + g][:, :], x_part[:, par, k, :],
                                                        a_part[:, at(b), k, g * BANK:(g + 1) * BANK
                                                               ].rearrange("p b n -> p (b n)"),
                                                        start=(n == 0), stop=(n == 3 * KD - 1))
                                n += 1
                    last.then_inc(s_psum, 1)
                if has(i - 2):
                    pe.wait_ge(yt_ready, i - 1)
                    if has(i + 3):
                        pe.wait_ge(xn_raw_ready, i + 4)
                    if fixed is not None and i >= 3:
                        pe.wait_ge(l_ready, i - 2)
                    for k in range(KD):
                        last = nc.tensor.matmul(bank[0][:, 0:E], yTb[:, par, k, :], rw_sb[:, k, :],
                                                start=(k == 0), stop=(k == KD - 1))
                    last.then_inc(l_psum, 1)
                def output(parts, start, stop):
                    b = i // TPB
                    n = 0
                    for p_part, v_part in parts:
                        for c in range(NPAIR):
                            last = nc.tensor.matmul(bank[1][:, 0:D], p_part[:, c, :],
                                                    v_part[:, at(b), c, :].rearrange("p b n -> p (b n)"),
                                                    start=start and n == 0, stop=stop and n == NPAIR - 1)
                            n += 1
                    return last

                if has(i):
                    pe.wait_ge(pt_hi_ready, i + 1)
                    if fixed == 0:
                        pe.wait_ge(vw_lo, 8)
                    if fixed is None or i >= 1:
                        pe.wait_ge(x1_ready, i)
                    output(((pt_hi, VW[0]), (pt_hi, VW[1])), True, False)
                    pe.wait_ge(pt_lo_ready, i + 1)
                    if not has(i + 2):
                        output(((pt_lo, VW[0]),), False, True).then_inc(o_psum, 1)
                if has(i - 1):
                    pe.wait_ge(y_ready, i)
                    for k in range(KD):
                        last = nc.tensor.transpose(bank[7][:, k * P:(k + 1) * P], ybuf[:, q, k * P:(k + 1) * P], ident[:, :])
                    last.then_inc(yt_psum, 1)
                if has(i) and has(i + 2):
                    output(((pt_lo, VW[0]),), False, True).then_inc(o_psum, 1)

            def hidden(c, buffers, pairs=range(PAIRS)):
                (cols_h, cols_l), _, _ = buffers
                pe.wait_ge(cols_ready, c + 1)
                for j in pairs:
                    if not peeled(c) or c >= 1:
                        pe.wait_ge(sh_raw, (c - 1) * PAIRS + (j + 1))
                    for u in range(2):
                        s, hc = (2 * j + u) // HC, (2 * j + u) % HC
                        n = 0
                        for w_part, x_part in ((sw1_s[0], cols_h), (sw1_s[1], cols_h), (sw1_s[0], cols_l)):
                            for k in range(KD):
                                last = nc.tensor.matmul(bank[2 + j][:, u * SUB:(u + 1) * SUB],
                                                        w_part[:, s, k, hc * P:(hc + 1) * P], x_part[:, :, k, :],
                                                        start=(n == 0), stop=(n == 3 * KD - 1))
                                n += 1
                    last.then_inc(sh_psum, 1)

            def bias_columns(c, steps=1):
                pe.wait_ge(comb_ready, turn_of(c) + 1)
                for n in range(steps):
                    for t in range(TPS):
                        last = nc.tensor.transpose(bank[0][0:COPIES * GAP, n * SUB + t * P:n * SUB + (t + 1) * P],
                                                   comb_cur[:, n, t, :], ident[:, :])
                last.then_inc(ct_psum, 1)

            def later_biases(c):
                pe.wait_ge(cur_ready, turn_of(c) + 1)
                for t in range(TPS):
                    last = nc.tensor.matmul(bank[1][:, t * D:(t + 1) * D], bias_w[:, 1, t * P:(t + 1) * P],
                                            bias_rows[:, :], start=True, stop=True)
                last.then_inc(bias_psum, 1)

            def project(c, buffers, with_bias=True, with_later=False, middle=None):
                _, _, (hT_h, hT_l) = buffers

                def products(j, h_part, w_parts, start=False, stop=False):
                    for t in range(TPS):
                        for m in (2 * j, 2 * j + 1):
                            for w_part in w_parts:
                                last = nc.tensor.matmul(bank[6 + t][:, 0:D], h_part[:, m, t * P:(t + 1) * P],
                                                        w_part[:, m, :],
                                                        start=start and m == 2 * j and w_part is w_parts[0],
                                                        stop=stop and m == 2 * j + 1)
                        if stop:
                            last.then_inc(acc_psum, 1)

                pe.wait_ge(acc_free, c * TPS + TPS)
                for j in range(PAIRS):
                    if j == PAIRS - 1 and middle:
                        middle()
                    pe.wait_ge(sh_hi, c * PAIRS + (j + 1))
                    products(j, hT_h, sw2_s, start=(j == 0))
                    if j == 1 and with_bias:
                        pe.wait_ge(cur_ready, turn_of(c) + 1)
                        for t in range(TPS):
                            nc.tensor.matmul(bank[6 + t][:, 0:D], bias_w[:, 0, t * P:(t + 1) * P], bias_rows[:, :],
                                             start=False, stop=False)
                        if with_later:
                            later_biases(c)
                    if j >= 1:
                        pe.wait_ge(sh_lo, c * PAIRS + j)
                        products(j - 1, hT_l, sw2_s[0:1])
                pe.wait_ge(sh_lo, c * PAIRS + PAIRS)
                products(PAIRS - 1, hT_l, sw2_s[0:1], stop=True)

            def hidden_first(half):
                pe.wait_ge(sw_ready, SW_PIECES)
                hidden(0, early, HALVES[half])

            attention(pe, step, {-3: lambda: fold(0), -2: lambda: fold(1), -1: values,
                                 NT - 1: lambda: hidden_first(0), NT: lambda: hidden_first(1)})

            project(0, early, with_bias=False)
            pe.wait_ge(chosen_ready, 1)
            chosen_flat = chosen[:, :, :].rearrange("p t e -> p (t e)")
            nc.tensor.matmul(bank[0][:, 0:P], before[:, :], chosen_flat, start=True, stop=True)
            nc.tensor.matmul(bank[1][:, 0:P], ones[:, :], chosen_flat, start=True, stop=True).then_inc(count_psum, 1)
            hidden(1, early)
            project(1, early, with_bias=False)

            def shared_step(c, buffers, with_later=False, middle=None):
                hidden(c, buffers, HALVES[0])
                bias_columns(c, 2 if with_later else 1)
                hidden(c, buffers, HALVES[1])
                project(c, buffers, with_later=with_later, middle=middle)

            pe.wait_ge(b2_ready, 1)
            shared_step(SPLIT, early)
            with pe.Fori(DELAY, DELAY + len(LATER)) as c:
                shared_step(c, early, with_later=True)

            def turn(s, par):
                pe.wait_ge(xsl_loaded[par], tiles_before(s, par) + 16)
                if not peeled(s) or s >= 2:
                    pe.wait_ge(xt_lo, s - 1)
                for k in range(KD):
                    last = nc.tensor.transpose(bank[par][:, k * P:(k + 1) * P], xsl[:, par, k * P:(k + 1) * P], ident[:, :])
                last.then_inc(xt_psum, 1)

            def give(s, par, u):
                pe.wait_ge(ht_lo, s + 1)
                if not peeled(s) or s >= 2:
                    pe.wait_ge(ye_ready, s - 1)
                n, e = 0, expert(u)
                for h_part, w_part in ((hr_hi, w2_s[0]), (hr_hi, w2_s[1]), (hr_lo, w2_s[0])):
                    for m in range(HC):
                        last = nc.tensor.matmul(bank[6 + par][:, 0:D], h_part[:, par, m, :],
                                                w_part[:, at(e), m, :].rearrange("p e n -> p (e n)"),
                                                start=(n == 0), stop=(n == 3 * HC - 1))
                        n += 1
                last.then_inc(ye_psum, 1)

            def step(s, par, u):
                pe.wait_ge(xt_lo, s + 1)
                if not peeled(s) or s >= 2:
                    pe.wait_ge(h_ready, s - 1)
                n, e = 0, expert(u)
                for x_part, w_part in ((xsT_hi, w1_s[0]), (xsT_hi, w1_s[1]), (xsT_lo, w1_s[0])):
                    for k in range(KD):
                        last = nc.tensor.matmul(bank[2 + par][:, :], x_part[:, k, :],
                                                w_part[:, at(e), k, :].rearrange("p e n -> p (e n)"),
                                                start=(n == 0), stop=(n == 3 * KD - 1))
                        n += 1
                last.then_inc(h_psum, 1)
                if not peeled(s) or s + 1 < SLOT_TILES:
                    fetch(s + 1, u + 1)
                    turn(s + 1, 1 - par)
                if not peeled(s) or s >= 2:
                    if peeled(s) and s == 2:
                        pe.wait_ge(w2_dve, len(W2_DVE))
                        pe.wait_ge(w2_pool, len(W2_POOL))
                        pe.wait_ge(acc_free, EARLY * TPS + 2)
                    give(s - 2, par, u - 2)
                pe.wait_ge(h_ready, s + 1)
                if not peeled(s) or s >= 2:
                    pe.wait_ge(ht_raw, s - 1)
                for m in range(HC):
                    last = nc.tensor.transpose(bank[4 + par][:, m * P:(m + 1) * P], hs[:, m * P:(m + 1) * P], ident[:, :])
                last.then_inc(ht_psum, 1)

            expert, fetch = experts(pe)
            fetch(0, 0)
            shared_step(EARLY - 1, early, middle=lambda: turn(0, 0))
            pe.wait_ge(w1_ready, E)
            pe.wait_ge(sh_raw, EARLY * PAIRS)
            routed(pe, step)

            give(SLOT_TILES - 2, SLOT_TILES % 2, SLOT_TILES - 2)
            hidden(EARLY, late, range(0, 1))
            give(SLOT_TILES - 1, (SLOT_TILES - 1) % 2, SLOT_TILES - 1)
            hidden(EARLY, late, range(1, PAIRS))
            bias_columns(EARLY)
            pe.wait_ge(ye_ready, SLOT_TILES)
            project(EARLY, late)
            for c in range(EARLY + 1, NSUB):
                shared_step(c, late)

        @block.vector
        def _(dve):
            dve.sem_inc(acc_free, 2)
            nc.vector.memset(b2_rows[:, :], 0.0).then_inc(rows_zeroed, 1)
            dve.wait_ge(ld_ctx, 16)
            nc.vector.bn_stats(stc[:, :], ctx_sb[:, :]).then_inc(cst_ready, 1)
            dve.wait_ge(cst_ready, 1)
            nc.vector.bn_aggr(mvc[:, :], stc[:, :]).then_inc(cmv_ready, 1)
            dve.wait_ge(crc_ready, 1)
            nc.vector.tensor_scalar(cn[:, :], ctx_sb[:, :], mvc[:, 0:1], rc[:, 0:1], ALU.subtract, ALU.mult
                                    ).then_inc(cn_ready, 1)

            def statistics(first, end):
                for t in range(first, end):
                    if t % (NT // NX) == 0:
                        dve.wait_ge(ld_x[t // (NT // NX)], 16)
                    nc.vector.bn_stats(st1[:, t, :], xs_all[:, t, :]).then_inc(st1_ready, 1)

            def moments(first, end):
                for t in range(first, end):
                    dve.wait_ge(st1_ready, t + 1)
                    nc.vector.bn_aggr(mv1[:, t, :], st1[:, t, :]).then_inc(mv1_ready, 1)

            for n in range(4):
                dve.wait_ge(wqt_psum, n + 1)
                src = bank[WQ_BANK + n].rearrange("p (c k n) -> p c k n", c=2, k=KD)
                nc.vector.tensor_copy(wqT[:, n * 2:(n + 1) * 2, :, :], src).then_inc(wqt_ready, 1)
            statistics(*GROUPS[0])
            moments(*GROUPS[0])
            dve.wait_ge(r1_ready, 1)

            def fold_rest(half):
                for n in FOLD_HALVES[half]:
                    dve.wait_ge(fold_psum, n + 1)
                    dve.wait_ge(fold_hi, n + 1)
                    k, c = n // 4, (n % 4) * 2
                    part = [a[:, :, k, c * P:(c + 2) * P].rearrange("p b (c n) -> p c b n", c=2) for a in A]
                    nc.vector.tensor_tensor(part[1], bank[FOLD_BANK + n % 4].rearrange("p (c b n) -> p c b n", c=2, b=BATCH),
                                            part[0].bitcast(F32), ALU.subtract).then_inc(fold_lo, 1)

            def fold_and_statistics():
                fold_rest(1)
                statistics(*GROUPS[1])
                moments(*GROUPS[1])

            def more_statistics():
                statistics(*GROUPS[2])
                moments(*GROUPS[2])

            def values_rest(pieces):
                for n in pieces:
                    b, c = VW_ORDER[n]
                    dve.wait_ge(vw_psum, n + 1)
                    dve.wait_ge(vw_hi, n + 1)
                    nc.vector.tensor_tensor(VW[1][:, b, c:c + 2, :], bank[VW_BANKS[n]].rearrange("p (c n) -> p c n", c=2),
                                            VW[0][:, b, c:c + 2, :].bitcast(F32), ALU.subtract).then_inc(vw_lo, 1)

            def small_things():
                dve.wait_ge(ld_b2, (2 + 2 * COPIES) * 16)
                nc.vector.tensor_copy(bias_rows[:, :], b2_rows[:, :]).then_inc(b2_hi, 1)
                dve.wait_ge(b2_hi, 1)
                r = slice(2 * GAP, 3 * GAP)
                nc.vector.tensor_tensor(bias_rows[r, :], b2_rows[r, :], bias_rows[r, :].bitcast(F32), ALU.subtract
                                        ).then_inc(b2_ready, 1)
                nc.vector.tensor_scalar(half_tg[:, :], tg[:, 1:2], 1.0 / S, None, ALU.mult).then_inc(htg_ready, 1)
                dve.wait_ge(counters, 5)
                nc.vector.tensor_copy(iota_e[:, :], iota_e_i[:, :]).then_inc(htg_ready, 1)
                nc.vector.tensor_copy(iota_tile[:, :], iota_tile_i[:, :]).then_inc(htg_ready, 1)
                nc.vector.tensor_copy(iota_slot[:, :], iota_slot_i[:, :]).then_inc(htg_ready, 1)

            def alone():
                dve.wait_ge(consts, 2)

            def step(i, par, has, fixed):
                q = 1 - par
                if has(i - 1):
                    dve.wait_ge(o_psum, i)
                    row = xs_all[:, at(i - 1), :].rearrange("p a d -> p (a d)")
                    nc.vector.scalar_tensor_tensor(row, bank[1][:, 0:D], tg[:, 0:1], row, ALU.mult, ALU.add
                                                   ).then_inc(x1_ready, 1)
                    alone()
                    dve.wait_ge(x1_ready, i)
                    nc.vector.bn_stats(st2[:, q, :], row).then_inc(st2_ready, 1)
                if has(i + 4):
                    if fixed == 0:
                        dve.wait_ge(r1_ready, 2)
                    if fixed == LOOP0 - 1:
                        dve.wait_ge(r1_ready, len(GROUPS))
                    if fixed is None or i >= -2:
                        dve.wait_ge(zt_psum, i + 3)
                    t = i + 4
                    nc.vector.tensor_scalar(zbuf[:, par, :], xs_all[:, at(t), :].rearrange("p a d -> p (a d)"),
                                            mv1[:, at(t), 0:1].rearrange("p a d -> p (a d)"), r1[:, at(t)],
                                            ALU.subtract, ALU.mult).then_inc(z_ready, 1)
                if has(i - 1):
                    alone()
                    dve.wait_ge(st2_ready, i)
                    nc.vector.bn_aggr(mv2[:, q, :], st2[:, q, :]).then_inc(mv2_ready, 1)
                if has(i):
                    dve.wait_ge(pt_psum, i * 2 + 2)
                    dve.wait_ge(pt_hi_ready, i + 1)
                    probs = psum[:, 6 * BANK:8 * BANK].rearrange("p (c n) -> p c n", c=NPAIR)
                    nc.vector.tensor_tensor(pt_lo[:, :, :], probs,
                                            pt_hi[:, :, :].bitcast(F32), ALU.subtract).then_inc(pt_lo_ready, 1)
                if fixed == -1:
                    values_rest(range(0, VW_FIRST))
                if has(i + 1):
                    alone()
                    dve.wait_ge(half_ready, i + 2)
                    nc.vector.tensor_reduce(sm[:, q, :], half_sum[:, :, :], AX.X, ALU.add).then_inc(sum_ready, 1)
                    dve.wait_ge(sum_ready, i + 2)
                    nc.vector.reciprocal(rinv[:, q, :], sm[:, q, :]).then_inc(rcp_ready, 1)
                if fixed == -1:
                    values_rest(range(VW_FIRST, len(VW_ORDER)))
                    dve.wait_ge(tg_ready, 1)
                if has(i - 1):
                    dve.wait_ge(r2_ready, i)
                    if fixed is None or i >= 3:
                        dve.wait_ge(yt_psum, i - 2)
                        dve.wait_ge(y_kept, i - 2)
                    row = xs_all[:, at(i - 1), :].rearrange("p a d -> p (a d)")
                    nc.vector.tensor_scalar(ybuf[:, q, :], row, mv2[:, q, 0:1], r2[:, q:q + 1], ALU.subtract, ALU.mult
                                            ).then_inc(y_ready, 1)
                if has(i + 2):
                    alone()
                    dve.wait_ge(s_psum, i + 3)
                    scores = psum[:, (2 + 2 * par) * BANK:(4 + 2 * par) * BANK].rearrange("p (h j) -> p h j", h=H)
                    nc.vector.tensor_reduce(mx[:, par, :], scores, AX.X, ALU.max).then_inc(max_ready, 1)
                if has(i - 2):
                    if fixed is None or i >= 4:
                        dve.wait_ge(top_kept, 2 * i - 6)
                    dve.wait_ge(l_psum, i - 1)
                    nc.vector.tensor_tensor(lg[:, par, :], bank[0][:, 0:E], rb_bc[:, :], ALU.add).then_inc(l_ready, 1)
                    alone()
                    dve.wait_ge(l_ready, i - 1)
                    nc.vector.max(v8[:, par, :], lg[:, par, :]).then_inc(val_ready, 1)
                if has(i + 2):
                    dve.wait_ge(max_ready, i + 3)
                    if fixed is None or i >= 0:
                        dve.wait_ge(pt_psum, i * 2 + 2)
                    nc.vector.tensor_tensor(Eb[par][:, :, :], scores, mx[:, par, :].unsqueeze(2).broadcast_to([P, H, CTX]),
                                            ALU.subtract).then_inc(sub_ready, 1)
                if has(i - 2):
                    alone()
                    dve.wait_ge(val_ready, i - 1)
                    nc.vector.max_index(i8[:, par, :], v8[:, par, :], lg[:, par, :]).then_inc(idx_ready, 1)

            attention(dve, step, {-3: lambda: fold_rest(0), -2: fold_and_statistics, -1: more_statistics,
                                  LOOP1: small_things})

            def columns_rest(c, buffers):
                cols_h, cols_l = buffers[0]
                dve.wait_ge(cols_hi, c + 1)
                nc.vector.tensor_tensor(cols_l[:, :, :, :], yT[:, bass.ds(c * TPS, TPS), :, :],
                                        cols_h[:, :, :, :].bitcast(F32), ALU.subtract).then_inc(cols_ready, 1)

            def hidden_rest(c, j, buffers):
                _, stage, (hT_h, hT_l) = buffers
                dve.wait_ge(sh_hi, c * PAIRS + (j + 1))
                pair = slice(2 * j, 2 * j + 2)
                nc.vector.tensor_tensor(hT_l[:, pair, :], stage[:, j % 2, :, :], hT_h[:, pair, :].bitcast(F32),
                                        ALU.subtract).then_inc(sh_lo, 1)

            def bias_weights(c, with_later=False):
                for n, b in enumerate((c, c - DELAY) if with_later else (c,)):
                    last = nc.vector.tensor_copy(
                        comb_cur[:, n, :, :].rearrange("p t (n e) -> p t n e", n=COPIES)[:, :, :, 0:BIAS_ROWS],
                        comb[:, bass.ds(b * TPS, TPS), :].unsqueeze(2).broadcast_to([P, TPS, COPIES, BIAS_ROWS]))
                last.then_inc(comb_ready, 1)

            def bias_split(c, steps=1):
                dve.wait_ge(ct_psum, turn_of(c) + 1)
                src = bank[0][:, 0:steps * SUB].rearrange("p (n t) -> p n t", n=steps)
                nc.vector.tensor_copy(bias_w[:, 0:steps, :], src[0:COPIES * GAP]).then_inc(bias_hi, 1)
                dve.wait_ge(bias_hi, turn_of(c) + 1)
                part = bias_w[GAP:2 * GAP, 0:steps, :]
                nc.vector.tensor_tensor(part, src[GAP:2 * GAP], part.bitcast(F32), ALU.subtract).then_inc(cur_ready, 1)

            def add_shared(c, t, done):
                dve.wait_ge(acc_psum, c * TPS + (t + 1))
                row = xs_all[:, at(c * TPS + t), :].rearrange("p a d -> p (a d)")
                nc.vector.scalar_tensor_tensor(row, bank[6 + t][:, 0:D], half_tg[:, 0:1], row, ALU.mult, ALU.add
                                               ).then_inc(done, 1)

            def add_later(c):
                dve.wait_ge(bias_psum, c - DELAY + 1)
                for t in range(TPS):
                    row = xs_all[:, at((c - DELAY) * TPS + t), :].rearrange("p a d -> p (a d)")
                    nc.vector.scalar_tensor_tensor(row, bank[1][:, t * D:(t + 1) * D], half_tg[:, 0:1], row, ALU.mult,
                                                   ALU.add)

            count = [0]

            def link(ins):
                count[0] += 1
                ins.then_inc(route, 1)
                dve.wait_ge(route, count[0])

            dve.wait_ge(top_kept, 2 * NT)
            dve.wait_ge(htg_ready, 4)
            nc.vector.tensor_tensor(dif[:, :], val[:, :, 1], val[:, :, 0], ALU.subtract).then_inc(dif_ready, 1)
            for k in range(TOPK):
                link(nc.vector.tensor_tensor(oh[:, k, :, :], iota_e[:, :].unsqueeze(1).broadcast_to([P, NT, E]),
                                             idx[:, :, k].unsqueeze(2).broadcast_to([P, NT, E]), ALU.is_equal))
            nc.vector.tensor_tensor(chosen[:, :, :], oh[:, 0, :, :], oh[:, 1, :, :], ALU.add).then_inc(chosen_ready, 1)
            for r in (*run_t, *run_e):
                link(nc.vector.memset(r[:, :, :] if len(r.shape) == 3 else r[:, :], 0.0))
            for t in range(TPS):
                add_shared(0, t, acc_free)
            dve.wait_ge(count_psum, 1)
            by_tile = bank[1][:, 0:P].rearrange("p (t e) -> p t e", t=NT)
            link(nc.vector.tensor_copy(tot[:, :, :], by_tile))
            link(nc.vector.tensor_copy(run_t[0][:, PADT:, :], tot[:, :, :]))
            a, d = 0, 1
            while d < NT:
                link(nc.vector.tensor_tensor(run_t[1 - a][:, PADT:, :], run_t[a][:, PADT:, :],
                                             run_t[a][:, PADT - d:PADT + NT - d, :], ALU.add))
                a, d = 1 - a, 2 * d
            upto = run_t[a][:, PADT:, :]
            link(nc.vector.tensor_tensor(full_tile[:, :, :], upto[:, NT - 1, :].unsqueeze(2).broadcast_to([P, E, NT]),
                                         iota_tile[:, :].unsqueeze(1).broadcast_to([P, E, NT]), ALU.is_gt))
            link(nc.vector.tensor_reduce(tiles_e[:, :], full_tile[:, :, :], AX.X, ALU.add))
            link(nc.vector.tensor_copy(run_e[0][:, PADE:], tiles_e[:, :]))
            f, d = 0, 1
            while d < E:
                link(nc.vector.tensor_tensor(run_e[1 - f][:, PADE:], run_e[f][:, PADE:], run_e[f][:, PADE - d:PADE + E - d],
                                             ALU.add))
                f, d = 1 - f, 2 * d
            ends = run_e[f][:, PADE:]
            link(nc.vector.tensor_tensor(start_e[:, :], ends, tiles_e[:, :], ALU.subtract))
            link(nc.vector.tensor_tensor(place[:, :, :], upto, tot[:, :, :], ALU.subtract))
            link(nc.vector.tensor_tensor(place[:, :, :], place[:, :, :],
                                         bank[0][:, 0:P].rearrange("p (t e) -> p t e", t=NT), ALU.add))
            link(nc.vector.scalar_tensor_tensor(place[:, :, :], start_e[:, :].unsqueeze(1).broadcast_to([P, NT, E]),
                                                float(P), place[:, :, :], ALU.mult, ALU.add))
            link(nc.vector.tensor_tensor(picked[:, 0, :, :], oh[:, 0, :, :], place[:, :, :], ALU.mult))
            link(nc.vector.tensor_tensor(picked[:, 1, :, :], oh[:, 1, :, :], place[:, :, :], ALU.mult))
            link(nc.vector.tensor_reduce(pos_f[:, :, :], picked[:, :, :, :], AX.X, ALU.add))
            nc.vector.tensor_copy(pos[:, :, :], pos_f[:, :, :]).then_inc(pos_ready, 1)
            link(nc.vector.tensor_tensor(passed[:, :, :], iota_slot[:, :].unsqueeze(2).broadcast_to([P, SLOT_TILES, E - 1]),
                                         ends[:, 0:E - 1].unsqueeze(1).broadcast_to([P, SLOT_TILES, E - 1]), ALU.is_ge))
            link(nc.vector.tensor_reduce(emap_f[:, :], passed[:, :, :], AX.X, ALU.add))
            link(nc.vector.tensor_copy(emap[:, :], emap_f[:, :]))
            dve.wait_ge(ex_ready, 1)
            link(nc.vector.tensor_scalar(den[:, :], ex[:, :], 1.0, None, ALU.add))
            link(nc.vector.reciprocal(prob[:, 0, :], den[:, :]))
            link(nc.vector.tensor_tensor(prob[:, 1, :], ex[:, :], prob[:, 0, :], ALU.mult))
            link(nc.vector.tensor_scalar(wgt[:, :, :], prob[:, :, :], tg[:, 1:2], None, ALU.mult))
            for k in range(TOPK):
                link(nc.vector.tensor_tensor(ohp[:, k, :, :], oh[:, k, :, :],
                                             prob[:, k, :].unsqueeze(2).broadcast_to([P, NT, E]), ALU.mult))
            link(nc.vector.memset(comb[:, :, :], 1.0))
            link(nc.vector.tensor_tensor(place[:, :, :], ohp[:, 0, :, :], ohp[:, 1, :, :], ALU.add))
            nc.vector.tensor_scalar(comb[:, :, 0:E], place[:, :, :], float(S), None, ALU.mult).then_inc(routed_all, 1)
            dve.wait_ge(routed_all, 1)

            for t in range(TPS):
                add_shared(1, t, acc_free)

            def w2_rest(e):
                dve.wait_ge(w2_hi_ready, W2_SPLIT.index(e) + 1)
                nc.vector.tensor_tensor(w2_s[1][:, e, :, :], w2_raw[:, e, :, :], w2_s[0][:, e, :, :].bitcast(F32),
                                        ALU.subtract).then_inc(w2_dve, 1)

            def hidden_rests(c, buffers, before={}, with_later=False):
                for j in range(PAIRS):
                    if j in before:
                        before[j]()
                    hidden_rest(c, j, buffers)
                    if j == 1:
                        bias_split(c, 2 if with_later else 1)
                if with_later:
                    add_later(c)

            def w1_rests(experts, before):
                for n, e in enumerate(experts):
                    dve.wait_ge(w1_hi_ready, before + (n + 1))
                    nc.vector.tensor_tensor(w1_s[1][:, at(e), :, :], w1_raw[:, at(e), :, :],
                                            w1_s[0][:, at(e), :, :].bitcast(F32), ALU.subtract).then_inc(w1_ready, 1)

            def add_step(c):
                for t in range(TPS):
                    add_shared(c, t, acc_free)

            bias_weights(SPLIT)
            hidden_rests(SPLIT, early)
            columns_rest(SPLIT + 1, early)
            with dve.Fori(DELAY, DELAY + len(LATER)) as c:
                bias_weights(c, with_later=True)
                first = (c - DELAY) * W1_PER
                w1_rests([first + n for n in range(W1_PER)], first)
                add_step(c - 1)
                hidden_rests(c, early, with_later=True)
                columns_rest(c + 1, early)
            bias_weights(EARLY - 1)
            w1_rests(range(E - W1_REST, E), E - W1_REST)
            add_step(EARLY - 2)
            hidden_rests(EARLY - 1, early)
            bias_weights(EARLY)
            w2_rest(W2_DVE[0])

            def turned(s, par):
                dve.wait_ge(xt_hi, s + 1)
                nc.vector.tensor_tensor(dest[:, at(s)], xsl[:, par, D:].bitcast(I32), spare[:, at(s)], ALU.min)
                nc.vector.tensor_tensor(xsT_lo[:, :, :], bank[par][:, 0:D].rearrange("p (k n) -> p k n", k=KD),
                                        xsT_hi[:, :, :].bitcast(F32), ALU.subtract).then_inc(xt_lo, 1)

            def hidden_left(s, par):
                dve.wait_ge(ht_hi, s + 1)
                nc.vector.tensor_tensor(hr_lo[:, par, :, :], hr[:, :, :], hr_hi[:, par, :, :].bitcast(F32), ALU.subtract
                                        ).then_inc(ht_lo, 1)

            def step(s, par, u):
                if not peeled(s) or s >= 2:
                    dve.wait_ge(ht_raw, s - 1)
                nc.vector.tensor_copy(b1_cur[:, par, :], b1_col[:, bass.ds(expert(u) * HC, HC)]).then_inc(b1_ready, 1)
                dve.wait_ge(h_psum, s + 1)
                nc.vector.tensor_copy(hs[:, :], bank[2 + par][:, :]).then_inc(h_ready, 1)
                if not peeled(s) or s + 1 < SLOT_TILES:
                    fetch(s + 1, u + 1)
                    turned(s + 1, 1 - par)
                if not peeled(s) or s >= 1:
                    hidden_left(s - 1, 1 - par)
                if peeled(s) and s + 1 == SLOT_TILES:
                    columns_rest(EARLY, late)

            expert, fetch = experts(dve)
            fetch(0, 0)
            turned(0, 0)
            w2_rest(W2_DVE[1])
            add_step(EARLY - 1)
            routed(dve, step, {1: lambda: w2_rest(W2_DVE[2]), 2: lambda: w2_rest(W2_DVE[3])})
            hidden_left(SLOT_TILES - 1, (SLOT_TILES - 1) % 2)

            def add_routed(pair, done):
                tiles = routed_pair(dve, pair)
                for k in range(TOPK):
                    if k:
                        dve.wait_ge(first_added[1], (VECTOR_PAIRS.index(pair) + 1) * TPS)
                    for t in range(tiles.start, tiles.stop):
                        row = xs_all[:, t, :]
                        nc.vector.scalar_tensor_tensor(row, y_got[:, k, t, :], wgt[:, k, t:t + 1], row, ALU.mult, ALU.add
                                                       ).then_inc(done if k else first_added[1], 1)

            for c in range(EARLY, LAST):
                hidden_rests(c, late)
                bias_weights(c + 1)
                columns_rest(c + 1, late)
                if c == LAST - 1:
                    add_routed(VECTOR_PAIRS[0], out_ready[1])
                add_step(c)
            add_routed(VECTOR_PAIRS[1], out_ready[1])
            hidden_rests(LAST, late, {2: lambda: add_routed(VECTOR_PAIRS[2], out_ready[1])})
            for pair in VECTOR_PAIRS[3:-1]:
                add_routed(pair, out_ready[1])
            add_routed(VECTOR_PAIRS[-1], both_added)
            dve.wait_ge(both_added, TPS)
            for t in range(TPS):
                add_shared(LAST, t, out_ready[1])


_INS = ['x', 'ctx_768', 'g_xattn', 'g_ffn', 'L0_xattn_g_x', 'L0_xattn_b_x', 'L0_xattn_g_c', 'L0_xattn_b_c', 'L0_xattn_Wq',
        'L0_xattn_Wk', 'L0_xattn_Wv', 'L0_xattn_Wo', 'L0_ffn_router_w', 'L0_ffn_router_b', 'L0_ffn_w1', 'L0_ffn_b1',
        'L0_ffn_w2', 'L0_ffn_b2', 'L0_ffn_sw1', 'L0_ffn_sb1', 'L0_ffn_sw2', 'L0_ffn_sb2']


def kernel(**inputs):
    import numpy as _np
    import concourse.bacc as _bacc
    from concourse import mybir as _mybir
    from concourse.bass_utils import run_bass_kernel_spmd as _run

    nc = _bacc.Bacc("TRN2", target_bir_lowering=False, num_devices=1)
    arrays, args = {}, []
    for name in _INS:
        a = _np.ascontiguousarray(inputs[name])
        arrays[f"in_{name}"] = a
        args.append(nc.dram_tensor(f"in_{name}", a.shape, _mybir.dt.from_np(a.dtype), kind="ExternalInput").ap())
    out = nc.dram_tensor("out_0", (BATCH, SEQ, D), F32, kind="ExternalOutput").ap()
    build(nc, *args, out)
    r = _run(nc, [arrays], core_ids=[0])
    return r.results[0]["out_0"]
```
